# Optimizing a Trainium2 kernel written in Bass

```python
import numpy as np
import jax
import jax.numpy as jnp

def _softmax(x, axis=-1):
    return jax.nn.softmax(x, axis=axis)

def _gelu(x):
    return jax.nn.gelu(x, approximate=True)

def _silu(x):
    return jax.nn.silu(x)

def _sigmoid(x):
    return jax.nn.sigmoid(x)

def _layernorm(x, axis=-1, eps=1e-05):
    m = jnp.mean(x, axis=axis, keepdims=True)
    v = jnp.var(x, axis=axis, keepdims=True)
    return (x - m) / jnp.sqrt(v + eps)

def _scatter_add(tgt, idx, src, axis=0):
    return tgt.at[idx].add(src)

def _segment_sum(src, seg, n):
    return jax.ops.segment_sum(src, seg, n)
kernel_name = 'mk_flamingo_gated_d4_seqx_r8_753dfc'

def setup_inputs(seed: int=0):
    np.random.seed(seed)
    _w = jnp.asarray

    def _rec_inputs():
        import jax
        import jax.numpy as jnp
        _rk = jax.random.key(seed)
        x = 7.22e-05 + 1 * jax.random.normal(jax.random.fold_in(_rk, 1), (64, 64, 128), jnp.float32)
        _lenS = 64 - jax.random.randint(jax.random.fold_in(_rk, 7), (64,), 0, max(1, 64 // 4) + 1, jnp.int32)
        _lenS2 = 64 - jax.random.randint(jax.random.fold_in(_rk, 8), (64,), 0, max(1, 64 // 4) + 1, jnp.int32)
        _ctx_1024P = jax.random.normal(jax.random.fold_in(_rk, 11), (64, 16, 128), jnp.float32)
        _ctx_1024c = jax.random.dirichlet(jax.random.fold_in(_rk, 511), 0.3 * jnp.ones((16,), jnp.float32), (64, 64))
        _ctx_1024t = jnp.einsum('bsk,bkd->bsd', _ctx_1024c, _ctx_1024P)
        _ctx_1024t = _ctx_1024t * jax.lax.rsqrt(jnp.mean(jnp.square(_ctx_1024t)) + 1e-12) * 0.953939
        ctx_1024 = 4.13588e-05 + 0.999923 * (_ctx_1024t + 0.3 * jax.random.normal(jax.random.fold_in(_rk, 611), (64, 64, 128), jnp.float32))
        itok_BxS_8_8191 = jax.random.randint(jax.random.fold_in(_rk, 13), (64, 64), 8, 1024, jnp.int32)
        itok_BxS2_1_8191 = jax.random.randint(jax.random.fold_in(_rk, 14), (64, 64), 1, 1024, jnp.int32)
        _validS = jnp.arange(64)[None, :] < _lenS[:, None]
        _validS2 = jnp.arange(64)[None, :] < _lenS2[:, None]
        _causal = jnp.tril(jnp.ones((64, 64), dtype=bool))
        mask_BxS2_if0 = jnp.where(jnp.ones((64, 64), dtype=bool), 0, 1).astype(jnp.int32)
        mask_BxSxS2_if1 = jnp.where(jnp.ones((64, 64, 64), dtype=bool), 1, 0).astype(jnp.int32)
        _g = jax.random.normal(jax.random.fold_in(_rk, 9001), (2, 4), jnp.float32)
        _g = jnp.sign(_g) * jnp.maximum(jnp.abs(_g), 1.0) + (_g == 0) * 1.0
        g_xattn = _g[0]
        g_ffn = _g[1]
        return (x, ctx_1024, itok_BxS_8_8191, itok_BxS2_1_8191, mask_BxS2_if0, mask_BxSxS2_if1, g_xattn, g_ffn)
    x, ctx_1024, itok_BxS_8_8191, itok_BxS2_1_8191, mask_BxS2_if0, mask_BxSxS2_if1, g_xattn, g_ffn = _rec_inputs()

    def _L0_xattn_setup():
        import jax, jax.numpy as jnp
        import numpy as np
        D_K = 128
        HEADS = 16
        HK = 64
        HV = 64
        key = jax.random.key(seed)
        ks = jax.random.split(key, 12)
        B, S = (4, 256)
        sc_in = 1.0 / np.sqrt(D_K)
        sc_u = 1.0 / np.sqrt(HV * HEADS)
        return {'q': jax.random.normal(ks[0], (B, S, D_K), jnp.float32), 'k': jax.random.normal(ks[1], (B, S, D_K), jnp.float32), 'v': jax.random.normal(ks[2], (B, S, D_K), jnp.float32), 'Wq': jax.random.normal(ks[3], (D_K, HK * HEADS), jnp.float32) * sc_in, 'bq': jax.random.normal(ks[4], (HK * HEADS,), jnp.float32) * sc_in, 'Wk': jax.random.normal(ks[5], (D_K, HK * HEADS), jnp.float32) * sc_in, 'bk': jax.random.normal(ks[6], (HK * HEADS,), jnp.float32) * sc_in, 'Wv': jax.random.normal(ks[7], (D_K, HV * HEADS), jnp.float32) * sc_in, 'bv': jax.random.normal(ks[8], (HV * HEADS,), jnp.float32) * sc_in, 'Wu': jax.random.normal(ks[9], (HV * HEADS, D_K), jnp.float32) * sc_u, 'bu': jax.random.normal(ks[10], (D_K,), jnp.float32) * sc_u}
    _L0_xattn_all = _L0_xattn_setup()
    _L0_xattn_in = {k: v for k, v in _L0_xattn_all.items() if k in ('Wq', 'bq', 'Wk', 'bk', 'Wv', 'bv', 'Wu', 'bu')}
    del _L0_xattn_all

    def _L0_ffn_setup():
        import jax, jax.numpy as jnp
        import numpy as np
        B, T, C, E, K, CAP, H = (8, 256, 128, 8, 2, 512, 512)
        key = jax.random.key(seed)
        ks = jax.random.split(key, 6)
        s = 0.02
        return {'x': jax.random.normal(ks[0], (B, T, C), jnp.float32), 'rw1': s * jax.random.normal(ks[1], (C, H), jnp.float32), 'rb1': jnp.zeros((H,), jnp.float32), 'rw2': s * jax.random.normal(ks[2], (H, E), jnp.float32), 'rb2': jnp.zeros((E,), jnp.float32), 'ew1': s * jax.random.normal(ks[3], (E, C, H), jnp.float32), 'eb1': jnp.zeros((E, H), jnp.float32), 'ew2': s * jax.random.normal(ks[4], (E, H, C), jnp.float32), 'eb2': jnp.zeros((E, C), jnp.float32)}
    _L0_ffn_all = _L0_ffn_setup()
    _L0_ffn_in = {k: v for k, v in _L0_ffn_all.items() if k in ('rw1', 'rb1', 'rw2', 'rb2', 'ew1', 'eb1', 'ew2', 'eb2')}
    del _L0_ffn_all

    def _L1_xattn_setup():
        import jax, jax.numpy as jnp
        import numpy as np
        D_MODEL = 128
        N_HEAD = 16

        def _split_heads(x, n_head):
            B, S, D = x.shape
            return x.reshape(B, S, n_head, D // n_head).transpose(0, 2, 1, 3)
        key = jax.random.key(seed)
        ks = jax.random.split(key, 11)
        B, S, D = (2, 256, D_MODEL)
        scale = 1.0 / np.sqrt(D)
        inp = {'q': jax.random.normal(ks[0], (B, S, D), jnp.float32), 'k': jax.random.normal(ks[1], (B, S, D), jnp.float32), 'v': jax.random.normal(ks[2], (B, S, D), jnp.float32), 'w_q': jax.random.normal(ks[3], (D, D), jnp.float32) * scale, 'b_q': jnp.zeros((D,), jnp.float32), 'w_k': jax.random.normal(ks[4], (D, D), jnp.float32) * scale, 'b_k': jnp.zeros((D,), jnp.float32), 'w_v': jax.random.normal(ks[5], (D, D), jnp.float32) * scale, 'b_v': jnp.zeros((D,), jnp.float32), 'w_o': jax.random.normal(ks[6], (D, D), jnp.float32) * scale, 'b_o': jnp.zeros((D,), jnp.float32)}
        return inp
    _L1_xattn_all = _L1_xattn_setup()
    _L1_xattn_in = {k: v for k, v in _L1_xattn_all.items() if k in ('w_q', 'b_q', 'w_k', 'b_k', 'w_v', 'b_v', 'w_o', 'b_o')}
    del _L1_xattn_all

    def _L1_ffn_setup():
        import jax, jax.numpy as jnp
        import numpy as np
        B, S, D, E, F, K = (4, 128, 128, 8, 352, 1)
        key = jax.random.key(seed)
        ks = jax.random.split(key, 8)
        sc = 0.02
        return {'x_bsD': jax.random.normal(ks[0], (B, S, D), jnp.float32), 'router_DE': jax.random.normal(ks[1], (D, E), jnp.float32) * sc, 'w1_eDF': jax.random.normal(ks[2], (E, D, F), jnp.float32) * sc, 'w3_eDF': jax.random.normal(ks[3], (E, D, F), jnp.float32) * sc, 'w2_eFD': jax.random.normal(ks[4], (E, F, D), jnp.float32) * sc, 'ws1_DF': jax.random.normal(ks[5], (D, F), jnp.float32) * sc, 'ws3_DF': jax.random.normal(ks[6], (D, F), jnp.float32) * sc, 'ws2_FD': jax.random.normal(ks[7], (F, D), jnp.float32) * sc}
    _L1_ffn_all = _L1_ffn_setup()
    _L1_ffn_in = {k: v for k, v in _L1_ffn_all.items() if k in ('router_DE', 'w1_eDF', 'w3_eDF', 'w2_eFD', 'ws1_DF', 'ws3_DF', 'ws2_FD')}
    del _L1_ffn_all

    def _L2_xattn_setup():
        import jax, jax.numpy as jnp
        import numpy as np
        import math
        B, M, D, H, NK = (4, 256, 128, 16, 5)
        HD = D // H

        def _gather_pad0(x, idx):
            Bx, Hx, W, hd = x.shape
            valid = (idx >= 0) & (idx < W)
            idxc = jnp.clip(idx, 0, W - 1).reshape(Bx, Hx, -1)
            g = jnp.take_along_axis(x, idxc[..., None], axis=2)
            g = g.reshape(idx.shape + (hd,))
            return g * valid[..., None].astype(x.dtype)
        key = jax.random.key(seed)
        ks = jax.random.split(key, 9)
        w = lambda k, shape: jax.random.normal(k, shape, jnp.float32) * 0.02
        return {'k': jax.random.normal(ks[0], (B, M, D), jnp.float32), 'v': jax.random.normal(ks[1], (B, M, D), jnp.float32), 'q': jax.random.normal(ks[2], (B, M, D), jnp.float32), 'mask': jnp.zeros((B, M), jnp.int32), 'Wk': w(ks[3], (D, D)), 'bk': jnp.zeros((D,), jnp.float32), 'Wv': w(ks[4], (D, D)), 'bv': jnp.zeros((D,), jnp.float32), 'Wq': w(ks[5], (D, D)), 'bq': jnp.zeros((D,), jnp.float32), 'Woff': w(ks[6], (H * NK, D)), 'boff': jnp.zeros((H * NK,), jnp.float32), 'Wo': w(ks[7], (D, D)), 'bo': jnp.zeros((D,), jnp.float32)}
    _L2_xattn_all = _L2_xattn_setup()
    _L2_xattn_in = {k: v for k, v in _L2_xattn_all.items() if k in ('Wk', 'bk', 'Wv', 'bv', 'Wq', 'bq', 'Woff', 'boff', 'Wo', 'bo')}
    del _L2_xattn_all

    def _L2_ffn_setup():
        import math
        import jax, jax.numpy as jnp
        import numpy as np
        B, S, H = (4, 256, 128)
        E, K, I = (8, 2, 128)
        NSH = 2
        CF, RSF = (1.25, 1.0)
        key = jax.random.key(seed)
        ks = jax.random.split(key, 8)
        w = lambda k, sh: jax.random.normal(k, sh, dtype=jnp.float32) * 0.02
        return {'hidden_states': jax.random.normal(ks[0], (B, S, H), dtype=jnp.float32), 'gate_w': w(ks[1], (E, H)), 'we_gate': w(ks[2], (E, I, H)), 'we_up': w(ks[3], (E, I, H)), 'we_down': w(ks[4], (E, H, I)), 'ws_gate': w(ks[5], (NSH * I, H)), 'ws_up': w(ks[6], (NSH * I, H)), 'ws_down': w(ks[7], (H, NSH * I))}
    _L2_ffn_all = _L2_ffn_setup()
    _L2_ffn_in = {k: v for k, v in _L2_ffn_all.items() if k in ('gate_w', 'we_gate', 'we_up', 'we_down', 'ws_gate', 'ws_up', 'ws_down')}
    del _L2_ffn_all

    def _L3_xattn_setup():
        import jax, jax.numpy as jnp
        import numpy as np
        DIM = 128
        NUM_HEADS = 16
        HEAD_DIM = DIM // NUM_HEADS

        def _slopes(num_heads):
            ratio = 2.0 ** (-8.0 / num_heads)
            return jnp.asarray([ratio ** i for i in range(1, num_heads + 1)], dtype=jnp.float32)
        key = jax.random.key(seed)
        ks = jax.random.split(key, 10)
        b, q_len, k_len = (2, 256, 512)
        query = jax.random.normal(ks[0], (b, q_len, DIM), dtype=jnp.float32)
        keys = jax.random.normal(ks[1], (b, k_len, DIM), dtype=jnp.float32)
        values = jax.random.normal(ks[2], (b, k_len, DIM), dtype=jnp.float32)
        query_pos = jnp.sort(jax.random.randint(ks[3], (b, q_len), 0, 1024), axis=-1)
        key_pos = jnp.sort(jax.random.randint(ks[4], (b, k_len), 0, 1024), axis=-1)
        mask = jnp.ones((b, q_len, k_len), dtype=jnp.int32)
        lim = float(np.sqrt(6.0 / (DIM + DIM)))
        W_q = jax.random.uniform(ks[5], (DIM, DIM), minval=-lim, maxval=lim, dtype=jnp.float32)
        W_k = jax.random.uniform(ks[6], (DIM, DIM), minval=-lim, maxval=lim, dtype=jnp.float32)
        W_v = jax.random.uniform(ks[7], (DIM, DIM), minval=-lim, maxval=lim, dtype=jnp.float32)
        W_o = jax.random.uniform(ks[8], (DIM, DIM), minval=-lim, maxval=lim, dtype=jnp.float32)
        return {'query': query, 'keys': keys, 'values': values, 'W_q': W_q, 'W_k': W_k, 'W_v': W_v, 'W_o': W_o, 'query_pos': query_pos, 'key_pos': key_pos, 'mask': mask}
    _L3_xattn_all = _L3_xattn_setup()
    _L3_xattn_in = {k: v for k, v in _L3_xattn_all.items() if k in ('W_q', 'W_k', 'W_v', 'W_o')}
    del _L3_xattn_all

    def _L3_ffn_setup():
        import jax, jax.numpy as jnp
        import numpy as np
        B, S, D, H, E = (4, 256, 128, 512, 8)
        key = jax.random.key(seed)
        ks = jax.random.split(key, 8)
        s_d = 1.0 / np.sqrt(D)
        s_h = 1.0 / np.sqrt(H)
        return {'x': jax.random.normal(ks[0], (B, S, D), dtype=jnp.float32), 'gate_w': jax.random.uniform(ks[1], (E, D), jnp.float32, -s_d, s_d), 'gate_b': jax.random.uniform(ks[2], (E,), jnp.float32, -s_d, s_d), 'w1': jax.random.uniform(ks[3], (E, H, D), jnp.float32, -s_d, s_d), 'b1': jax.random.uniform(ks[4], (E, H), jnp.float32, -s_d, s_d), 'w2': jax.random.uniform(ks[5], (E, D, H), jnp.float32, -s_h, s_h), 'b2': jax.random.uniform(ks[6], (E, D), jnp.float32, -s_h, s_h)}
    _L3_ffn_all = _L3_ffn_setup()
    _L3_ffn_in = {k: v for k, v in _L3_ffn_all.items() if k in ('gate_w', 'gate_b', 'w1', 'b1', 'w2', 'b2')}
    del _L3_ffn_all
    return {'x': x, 'ctx_1024': ctx_1024, 'itok_BxS_8_8191': itok_BxS_8_8191, 'itok_BxS2_1_8191': itok_BxS2_1_8191, 'mask_BxS2_if0': mask_BxS2_if0, 'mask_BxSxS2_if1': mask_BxSxS2_if1, 'g_xattn': g_xattn, 'g_ffn': g_ffn, 'L0_xattn_Wq': _L0_xattn_in['Wq'], 'L0_xattn_bq': _L0_xattn_in['bq'], 'L0_xattn_Wk': _L0_xattn_in['Wk'], 'L0_xattn_bk': _L0_xattn_in['bk'], 'L0_xattn_Wv': _L0_xattn_in['Wv'], 'L0_xattn_bv': _L0_xattn_in['bv'], 'L0_xattn_Wu': _L0_xattn_in['Wu'], 'L0_xattn_bu': _L0_xattn_in['bu'], 'L0_ffn_rw1': _L0_ffn_in['rw1'], 'L0_ffn_rb1': _L0_ffn_in['rb1'], 'L0_ffn_rw2': _L0_ffn_in['rw2'], 'L0_ffn_rb2': _L0_ffn_in['rb2'], 'L0_ffn_ew1': _L0_ffn_in['ew1'], 'L0_ffn_eb1': _L0_ffn_in['eb1'], 'L0_ffn_ew2': _L0_ffn_in['ew2'], 'L0_ffn_eb2': _L0_ffn_in['eb2'], 'L1_xattn_w_q': _L1_xattn_in['w_q'], 'L1_xattn_b_q': _L1_xattn_in['b_q'], 'L1_xattn_w_k': _L1_xattn_in['w_k'], 'L1_xattn_b_k': _L1_xattn_in['b_k'], 'L1_xattn_w_v': _L1_xattn_in['w_v'], 'L1_xattn_b_v': _L1_xattn_in['b_v'], 'L1_xattn_w_o': _L1_xattn_in['w_o'], 'L1_xattn_b_o': _L1_xattn_in['b_o'], 'L1_ffn_router_DE': _L1_ffn_in['router_DE'], 'L1_ffn_w1_eDF': _L1_ffn_in['w1_eDF'], 'L1_ffn_w3_eDF': _L1_ffn_in['w3_eDF'], 'L1_ffn_w2_eFD': _L1_ffn_in['w2_eFD'], 'L1_ffn_ws1_DF': _L1_ffn_in['ws1_DF'], 'L1_ffn_ws3_DF': _L1_ffn_in['ws3_DF'], 'L1_ffn_ws2_FD': _L1_ffn_in['ws2_FD'], 'L2_xattn_Wk': _L2_xattn_in['Wk'], 'L2_xattn_bk': _L2_xattn_in['bk'], 'L2_xattn_Wv': _L2_xattn_in['Wv'], 'L2_xattn_bv': _L2_xattn_in['bv'], 'L2_xattn_Wq': _L2_xattn_in['Wq'], 'L2_xattn_bq': _L2_xattn_in['bq'], 'L2_xattn_Woff': _L2_xattn_in['Woff'], 'L2_xattn_boff': _L2_xattn_in['boff'], 'L2_xattn_Wo': _L2_xattn_in['Wo'], 'L2_xattn_bo': _L2_xattn_in['bo'], 'L2_ffn_gate_w': _L2_ffn_in['gate_w'], 'L2_ffn_we_gate': _L2_ffn_in['we_gate'], 'L2_ffn_we_up': _L2_ffn_in['we_up'], 'L2_ffn_we_down': _L2_ffn_in['we_down'], 'L2_ffn_ws_gate': _L2_ffn_in['ws_gate'], 'L2_ffn_ws_up': _L2_ffn_in['ws_up'], 'L2_ffn_ws_down': _L2_ffn_in['ws_down'], 'L3_xattn_W_q': _L3_xattn_in['W_q'], 'L3_xattn_W_k': _L3_xattn_in['W_k'], 'L3_xattn_W_v': _L3_xattn_in['W_v'], 'L3_xattn_W_o': _L3_xattn_in['W_o'], 'L3_ffn_gate_w': _L3_ffn_in['gate_w'], 'L3_ffn_gate_b': _L3_ffn_in['gate_b'], 'L3_ffn_w1': _L3_ffn_in['w1'], 'L3_ffn_b1': _L3_ffn_in['b1'], 'L3_ffn_w2': _L3_ffn_in['w2'], 'L3_ffn_b2': _L3_ffn_in['b2']}

def reference(x, ctx_1024, itok_BxS_8_8191, itok_BxS2_1_8191, mask_BxS2_if0, mask_BxSxS2_if1, g_xattn, g_ffn, L0_xattn_Wq, L0_xattn_bq, L0_xattn_Wk, L0_xattn_bk, L0_xattn_Wv, L0_xattn_bv, L0_xattn_Wu, L0_xattn_bu, L0_ffn_rw1, L0_ffn_rb1, L0_ffn_rw2, L0_ffn_rb2, L0_ffn_ew1, L0_ffn_eb1, L0_ffn_ew2, L0_ffn_eb2, L1_xattn_w_q, L1_xattn_b_q, L1_xattn_w_k, L1_xattn_b_k, L1_xattn_w_v, L1_xattn_b_v, L1_xattn_w_o, L1_xattn_b_o, L1_ffn_router_DE, L1_ffn_w1_eDF, L1_ffn_w3_eDF, L1_ffn_w2_eFD, L1_ffn_ws1_DF, L1_ffn_ws3_DF, L1_ffn_ws2_FD, L2_xattn_Wk, L2_xattn_bk, L2_xattn_Wv, L2_xattn_bv, L2_xattn_Wq, L2_xattn_bq, L2_xattn_Woff, L2_xattn_boff, L2_xattn_Wo, L2_xattn_bo, L2_ffn_gate_w, L2_ffn_we_gate, L2_ffn_we_up, L2_ffn_we_down, L2_ffn_ws_gate, L2_ffn_ws_up, L2_ffn_ws_down, L3_xattn_W_q, L3_xattn_W_k, L3_xattn_W_v, L3_xattn_W_o, L3_ffn_gate_w, L3_ffn_gate_b, L3_ffn_w1, L3_ffn_b1, L3_ffn_w2, L3_ffn_b2):
    import jax
    import jax.numpy as jnp

    def _L0_xattn_ref(q, k, v, Wq, bq, Wk, bk, Wv, bv, Wu, bu):
        import jax, jax.numpy as jnp
        import numpy as np
        D_K = 128
        HEADS = 16
        HK = 64
        HV = 64
        B, S, _ = q.shape
        qh = (q @ Wq + bq).reshape(B, S, HEADS, HK).transpose(0, 2, 1, 3)
        kh = (k @ Wk + bk).reshape(B, S, HEADS, HK).transpose(0, 2, 1, 3)
        vh = (v @ Wv + bv).reshape(B, S, HEADS, HV).transpose(0, 2, 1, 3)
        scores = jnp.einsum('bhqd,bhkd->bhqk', qh, kh) / jnp.sqrt(jnp.asarray(HK, qh.dtype))
        attn = jax.nn.softmax(scores, axis=-1)
        out = jnp.einsum('bhqk,bhkd->bhqd', attn, vh)
        merged = out.transpose(0, 2, 1, 3).reshape(B, S, HEADS * HV)
        return merged @ Wu + bu

    def _L0_ffn_ref(x, rw1, rb1, rw2, rb2, ew1, eb1, ew2, eb2):
        import jax, jax.numpy as jnp
        import numpy as np
        B, T, C, E, K, CAP, H = (8, 256, 128, 8, 2, 512, 512)
        Bx, Tx, Cx = x.shape
        N = Bx * Tx
        logits = jax.nn.relu(x @ rw1 + rb1) @ rw2 + rb2
        vals, ids = jax.lax.top_k(logits, K)
        probs = jax.nn.softmax(vals, axis=-1)
        ids_f = ids.reshape(N * K)
        probs_f = probs.reshape(N * K)
        xr = jnp.repeat(x.reshape(N, Cx), K, axis=0)
        m = jax.nn.one_hot(ids_f, E, dtype=jnp.int32)
        pos = jnp.cumsum(m, axis=0) - 1
        pos_tok = jnp.take_along_axis(pos, ids_f[:, None], axis=1)[:, 0]
        keep = (pos_tok < CAP).astype(x.dtype)
        pos_c = jnp.clip(pos_tok, 0, CAP - 1)
        disp = jnp.zeros((E, CAP, Cx), x.dtype).at[ids_f, pos_c].add(xr * keep[:, None])
        h = jax.nn.relu(jnp.einsum('enc,ech->enh', disp, ew1) + eb1[:, None, :])
        eo = jnp.einsum('enh,ehc->enc', h, ew2) + eb2[:, None, :]
        y = eo[ids_f, pos_c] * (probs_f * keep)[:, None]
        return y.reshape(Bx, Tx, K, Cx).sum(axis=2)

    def _L1_xattn_ref(q, k, v, w_q, b_q, w_k, b_k, w_v, b_v, w_o, b_o):
        import jax, jax.numpy as jnp
        import numpy as np
        D_MODEL = 128
        N_HEAD = 16

        def _split_heads(x, n_head):
            B, S, D = x.shape
            return x.reshape(B, S, n_head, D // n_head).transpose(0, 2, 1, 3)
        qp = q @ w_q.T + b_q
        kp = k @ w_k.T + b_k
        vp = v @ w_v.T + b_v
        qh = _split_heads(qp, N_HEAD)
        kh = _split_heads(kp, N_HEAD)
        vh = _split_heads(vp, N_HEAD)
        d_head = qh.shape[-1]
        score = jnp.einsum('bhsd,bhtd->bhst', qh, kh) / jnp.sqrt(jnp.float32(d_head))
        attn = jax.nn.softmax(score, axis=-1)
        out = jnp.einsum('bhst,bhtd->bhsd', attn, vh)
        B, H, S, Dh = out.shape
        out = out.transpose(0, 2, 1, 3).reshape(B, S, H * Dh)
        return out @ w_o.T + b_o

    def _L1_ffn_ref(x_bsD, router_DE, w1_eDF, w3_eDF, w2_eFD, ws1_DF, ws3_DF, ws2_FD):
        import jax, jax.numpy as jnp
        import numpy as np
        B, S, D, E, F, K = (4, 128, 128, 8, 352, 1)
        b, s, d = x_bsD.shape
        a = b * s
        x_aD = x_bsD.reshape(a, d)
        scores_aE = x_aD @ router_DE
        vals_aK, idx_aK = jax.lax.top_k(scores_aE, K)
        masked_aE = jnp.full_like(scores_aE, -jnp.inf).at[jnp.arange(a)[:, None], idx_aK].set(vals_aK)
        gates_Ea = jax.nn.sigmoid(masked_aE).T
        routed_in_EaD = jax.lax.stop_gradient(gates_Ea[:, :, None] * x_aD[None, :, :])
        mid_EaF = jax.nn.silu(jnp.einsum('ead,edf->eaf', routed_in_EaD, w1_eDF)) * jnp.einsum('ead,edf->eaf', routed_in_EaD, w3_eDF)
        routed_out_EaD = jnp.einsum('eaf,efd->ead', mid_EaF, w2_eFD)
        shared_aD = jax.nn.silu(x_aD @ ws1_DF) * (x_aD @ ws3_DF) @ ws2_FD
        out_aD = shared_aD + routed_out_EaD.sum(axis=0)
        return out_aD.reshape(b, s, d)

    def _L2_xattn_ref(k, v, q, mask, Wk, bk, Wv, bv, Wq, bq, Woff, boff, Wo, bo):
        import jax, jax.numpy as jnp
        import numpy as np
        import math
        B, M, D, H, NK = (4, 256, 128, 16, 5)
        HD = D // H

        def _gather_pad0(x, idx):
            Bx, Hx, W, hd = x.shape
            valid = (idx >= 0) & (idx < W)
            idxc = jnp.clip(idx, 0, W - 1).reshape(Bx, Hx, -1)
            g = jnp.take_along_axis(x, idxc[..., None], axis=2)
            g = g.reshape(idx.shape + (hd,))
            return g * valid[..., None].astype(x.dtype)
        Bq, Q, _ = q.shape
        key_len = k.shape[1]
        K = jnp.einsum('bmd,ed->bme', k, Wk) + bk
        V = jnp.einsum('bmd,ed->bme', v, Wv) + bv
        Qp = jnp.einsum('bqd,ed->bqe', q, Wq) + bq
        off = jnp.einsum('bqd,ed->bqe', Qp, Woff) + boff
        off = off.reshape(Bq, Q, H, NK).transpose(0, 2, 1, 3)
        Kh = K.reshape(Bq, key_len, H, HD).transpose(0, 2, 1, 3)
        Vh = V.reshape(Bq, key_len, H, HD).transpose(0, 2, 1, 3)
        Qh = Qp.reshape(Bq, Q, H, HD).transpose(0, 2, 1, 3)
        loc = jnp.arange(Q, dtype=jnp.float32)[:, None]
        left = -NK // 2
        ref = jnp.arange(left, NK + left, dtype=jnp.float32)
        sign_lens = (1 - mask).sum(-1).astype(jnp.float32) - 1.0
        loc_x = jnp.mod(ref + off + loc, sign_lens[:, None, None, None])
        xg = loc_x / (key_len - 1) * 2.0 - 1.0
        ix = ((xg + 1.0) * key_len - 1.0) / 2.0
        x0 = jnp.floor(ix)
        dx = ix - x0
        i0 = x0.astype(jnp.int32)
        i1 = i0 + 1
        w0 = (1.0 - dx)[..., None]
        w1 = dx[..., None]
        sk = 0.5 * (w0 * _gather_pad0(Kh, i0) + w1 * _gather_pad0(Kh, i1))
        sv = 0.5 * (w0 * _gather_pad0(Vh, i0) + w1 * _gather_pad0(Vh, i1))
        scores = jnp.einsum('bhqd,bhqkd->bhqk', Qh / math.sqrt(HD), sk)
        attn = jax.nn.softmax(scores, axis=-1)
        ctx = jnp.einsum('bhqk,bhqkd->bhqd', attn, sv)
        ctx = ctx.transpose(0, 2, 1, 3).reshape(Bq, Q, H * HD)
        return jnp.einsum('bqd,ed->bqe', ctx, Wo) + bo

    def _L2_ffn_ref(hidden_states, gate_w, we_gate, we_up, we_down, ws_gate, ws_up, ws_down):
        import math
        import jax, jax.numpy as jnp
        import numpy as np
        B, S, H = (4, 256, 128)
        E, K, I = (8, 2, 128)
        NSH = 2
        CF, RSF = (1.25, 1.0)
        orig_shape = hidden_states.shape
        x = hidden_states.reshape(-1, H)
        N = x.shape[0]
        logits = x.astype(jnp.float32) @ gate_w.astype(jnp.float32).T
        scores = jax.nn.softmax(logits, axis=-1)
        topk_w, topk_idx = jax.lax.top_k(scores, K)
        topk_w = topk_w / (topk_w.sum(-1, keepdims=True) + 1e-20) * RSF
        capacity = math.ceil(CF * N * K / E)
        flat = topk_idx.reshape(-1)
        one_hot = jax.nn.one_hot(flat, E, dtype=jnp.int32)
        pos = jnp.cumsum(one_hot, axis=0) - 1
        pos_tok = jnp.take_along_axis(pos, flat[:, None], axis=1)[:, 0]
        keep = (pos_tok < capacity).reshape(N, K)
        topk_w = topk_w * keep.astype(topk_w.dtype)
        comb = jnp.zeros((N, E), jnp.float32).at[jnp.arange(N)[:, None], topk_idx].add(topk_w)
        g = jnp.einsum('nh,eih->nei', x, we_gate)
        u = jnp.einsum('nh,eih->nei', x, we_up)
        eo = jnp.einsum('nei,ehi->neh', jax.nn.silu(g) * u, we_down)
        y = jnp.einsum('neh,ne->nh', eo, comb)
        sh = jax.nn.silu(x @ ws_gate.T) * (x @ ws_up.T) @ ws_down.T
        return (y + sh).reshape(orig_shape)

    def _L3_xattn_ref(query, keys, values, W_q, W_k, W_v, W_o, query_pos, key_pos, mask):
        import jax, jax.numpy as jnp
        import numpy as np
        DIM = 128
        NUM_HEADS = 16
        HEAD_DIM = DIM // NUM_HEADS

        def _slopes(num_heads):
            ratio = 2.0 ** (-8.0 / num_heads)
            return jnp.asarray([ratio ** i for i in range(1, num_heads + 1)], dtype=jnp.float32)
        b, q_len, _ = query.shape
        k_len = keys.shape[1]
        scale = 1.0 / np.sqrt(HEAD_DIM)
        Q = (query @ W_q.T).reshape(b, q_len, NUM_HEADS, HEAD_DIM).transpose(0, 2, 1, 3)
        K = (keys @ W_k.T).reshape(b, k_len, NUM_HEADS, HEAD_DIM).transpose(0, 2, 1, 3)
        V = (values @ W_v.T).reshape(b, k_len, NUM_HEADS, HEAD_DIM).transpose(0, 2, 1, 3)
        scores = jnp.einsum('bhqd,bhkd->bhqk', Q, K) * scale
        dist = (query_pos[:, :, None] - key_pos[:, None, :]).astype(scores.dtype)
        bias = -_slopes(NUM_HEADS)[None, :, None, None] * dist[:, None, :, :]
        scores = scores + bias
        scores = jnp.where(mask[:, None, :, :] == 0, -jnp.inf, scores)
        m = jnp.max(scores, axis=-1, keepdims=True)
        e = jnp.exp(scores - m)
        attn = e / (1.0 + jnp.sum(e, axis=-1, keepdims=True))
        out = jnp.einsum('bhqk,bhkd->bhqd', attn, V)
        out = out.transpose(0, 2, 1, 3).reshape(b, q_len, DIM)
        return out @ W_o.T

    def _L3_ffn_ref(x, gate_w, gate_b, w1, b1, w2, b2):
        import jax, jax.numpy as jnp
        import numpy as np
        B, S, D, H, E = (4, 256, 128, 512, 8)
        b, s, d = x.shape
        xf = x.reshape(-1, d)
        logits = xf @ gate_w.T + gate_b
        top1 = jnp.argmax(logits, axis=-1)
        out = jnp.zeros_like(xf)
        n_experts = w1.shape[0]
        for e in range(n_experts):
            h = jax.nn.relu(xf @ w1[e].T + b1[e])
            y = h @ w2[e].T + b2[e]
            out = out + jnp.where((top1 == e)[:, None], y, jnp.zeros((), y.dtype))
        return out.reshape(b, s, d)
    x = x + jnp.tanh(g_xattn[0]) * _L0_xattn_ref(_layernorm(x, axis=-1), ctx_1024, ctx_1024, L0_xattn_Wq, L0_xattn_bq, L0_xattn_Wk, L0_xattn_bk, L0_xattn_Wv, L0_xattn_bv, L0_xattn_Wu, L0_xattn_bu)
    x = x + jnp.tanh(g_ffn[0]) * _L0_ffn_ref(_layernorm(x, axis=-1), L0_ffn_rw1, L0_ffn_rb1, L0_ffn_rw2, L0_ffn_rb2, L0_ffn_ew1, L0_ffn_eb1, L0_ffn_ew2, L0_ffn_eb2)
    x = x + jnp.tanh(g_xattn[1]) * _L1_xattn_ref(_layernorm(x, axis=-1), ctx_1024, ctx_1024, L1_xattn_w_q, L1_xattn_b_q, L1_xattn_w_k, L1_xattn_b_k, L1_xattn_w_v, L1_xattn_b_v, L1_xattn_w_o, L1_xattn_b_o)
    x = x + jnp.tanh(g_ffn[1]) * _L1_ffn_ref(_layernorm(x, axis=-1), L1_ffn_router_DE, L1_ffn_w1_eDF, L1_ffn_w3_eDF, L1_ffn_w2_eFD, L1_ffn_ws1_DF, L1_ffn_ws3_DF, L1_ffn_ws2_FD)
    x = x + jnp.tanh(g_xattn[2]) * _L2_xattn_ref(ctx_1024, ctx_1024, _layernorm(x, axis=-1), mask_BxS2_if0, L2_xattn_Wk, L2_xattn_bk, L2_xattn_Wv, L2_xattn_bv, L2_xattn_Wq, L2_xattn_bq, L2_xattn_Woff, L2_xattn_boff, L2_xattn_Wo, L2_xattn_bo)
    x = x + jnp.tanh(g_ffn[2]) * _L2_ffn_ref(_layernorm(x, axis=-1), L2_ffn_gate_w, L2_ffn_we_gate, L2_ffn_we_up, L2_ffn_we_down, L2_ffn_ws_gate, L2_ffn_ws_up, L2_ffn_ws_down)
    x = x + jnp.tanh(g_xattn[3]) * _L3_xattn_ref(_layernorm(x, axis=-1), ctx_1024, ctx_1024, L3_xattn_W_q, L3_xattn_W_k, L3_xattn_W_v, L3_xattn_W_o, itok_BxS_8_8191, itok_BxS2_1_8191, mask_BxSxS2_if1)
    x = x + jnp.tanh(g_ffn[3]) * _L3_ffn_ref(_layernorm(x, axis=-1), L3_ffn_gate_w, L3_ffn_gate_b, L3_ffn_w1, L3_ffn_b1, L3_ffn_w2, L3_ffn_b2)
    return x

_drawn_inputs = setup_inputs


def setup_inputs(seed=0):
    import zlib

    import numpy as np

    out = dict(_drawn_inputs(seed))
    spreads = {'L0_ffn_rb1': (0.0, 0.1),
     'L0_ffn_rb2': (0.0, 0.1),
     'L0_ffn_eb1': (0.0, 0.527),
     'L0_ffn_eb2': (0.0, 0.1),
     'L1_xattn_b_q': (0.0, 0.1),
     'L1_xattn_b_k': (0.0, 2.0),
     'L1_xattn_b_v': (0.0, 0.1),
     'L1_xattn_b_o': (0.0, 0.1),
     'L2_xattn_bk': (0.0, 2.0),
     'L2_xattn_bv': (0.0, 0.438),
     'L2_xattn_bq': (0.0, 0.8),
     'L2_xattn_boff': (0.0, 0.8),
     'L2_xattn_bo': (0.0, 0.1)}
    factors = {'g_ffn': 8.0,
     'L0_xattn_bk': 64.0,
     'L0_ffn_ew1': 2.703,
     'L1_ffn_router_DE': 6.546,
     'L1_ffn_w1_eDF': 6.97,
     'L1_ffn_w3_eDF': 6.874,
     'L1_ffn_w2_eFD': 6.244,
     'L1_ffn_ws1_DF': 3.693,
     'L1_ffn_ws3_DF': 3.541,
     'L1_ffn_ws2_FD': 3.526,
     'L2_xattn_Wk': 8.0,
     'L2_xattn_Wv': 2.873,
     'L2_xattn_Wq': 8.0,
     'L2_xattn_Woff': 8.0,
     'L2_ffn_gate_w': 8.0,
     'L2_ffn_we_gate': 7.299,
     'L2_ffn_we_up': 6.439,
     'L2_ffn_we_down': 8.0,
     'L2_ffn_ws_gate': 4.716,
     'L2_ffn_ws_up': 4.689,
     'L2_ffn_ws_down': 4.816,
     'L3_ffn_b1': 11.586,
     'L3_ffn_b2': 8.776}
    for name, (base, spread) in spreads.items():
        noise = np.random.default_rng([zlib.crc32(name.encode()), seed]).standard_normal(out[name].shape)
        drawn = base * np.exp(spread * noise) if base else spread * noise
        out[name] = jnp.asarray(drawn.astype(out[name].dtype))
    for name, factor in factors.items():
        out[name] = (out[name] * factor).astype(out[name].dtype)
    return out
```

```python
from contextlib import ExitStack

import numpy as np
import concourse.bass as bass
from concourse import mybir

ALU = mybir.AluOpType
ACT = mybir.ActivationFunctionType
AX = mybir.AxisListType
F32 = mybir.dt.float32
I32 = mybir.dt.int32

P = 128
B, S, D = 64, 64, 128
NT = B * S // P
GT = 4
NG = NT // GT
GW = GT * P
H = 16
HP = H // 2
HD0 = 64
HD = 8
NK = 5
E = 8
CAP0, CAP2 = 512, 1280
F1 = 352
F1C = [(0, 128), (128, 128), (256, 96)]
EPS = 1e-5
MAGIC = 12582912.0
BIG = 1000.0


def layout(*fields):
    at, n = {}, 0
    for name, width in fields:
        at[name] = (n, n + width)
        n += width
    return at, n


CONST, NCONST = layout(("ident", P), ("before", P), ("ones", P), ("iota8", E), ("iota64", S),
                       ("slopes", H), ("headmask", 4), ("refloc", H * NK))
ROWS, NROWS = layout(("bv0", 1024), ("bu0", D), ("bv1", D), ("bo1", D), ("bv2", D), ("boff", H * NK),
                     ("bo2", D), ("g", 8))
COLS, NCOLS = layout(("bq0", 8), ("bk0", 8), ("bq1", 1), ("bk1", 1), ("bq2", 1), ("bk2", 1), ("rb1", 4),
                     ("rb2", 1), ("eb1", E * 4), ("gb3", 1), ("b13", E * 4), ("eb2", D), ("b23", D))
WA0, NWA0 = layout(("q", 1024), ("k", 1024), ("v", 1024), ("u", 1024))
WSA, NWSA = layout(("q1", D), ("k1", D), ("v1", D), ("o1", D), ("q2", D), ("k2", D), ("v2", D),
                   ("off2", H * NK), ("o2", D), ("q3", D), ("k3", D), ("v3", D), ("o3", D))
WF0, NWF0 = layout(("rw1", 512), ("rw2", 4 * E), ("w1", E * 512), ("w2", E * 512))
WF1, NWF1 = layout(("router", E), ("w1", 9 * F1), ("w3", 9 * F1), ("w2", 9 * 3 * D))
WF2, NWF2 = layout(("router", E), ("w1", 10 * D), ("w3", 10 * D), ("w2", 10 * D))
WF3, NWF3 = layout(("router", E), ("w1", E * 512), ("w2", E * 512))
SLAB0 = max(NWF0, NWF2 + H * NK * S)
SLAB1 = max(NWA0, NWF1, NWF3, 2 * H * NK * S)


class Ffn:

    def __init__(self, layer, experts, chunks, gated, sets, cap, softmax, topk, shared, bias):
        self.layer, self.experts, self.chunks, self.gated = layer, experts, chunks, gated
        self.sets, self.cap, self.softmax, self.topk = sets, cap, softmax, topk
        self.shared, self.bias = shared, bias
        self.jobs = experts * len(chunks)
        self.ys = experts + (1 if bias else 0)


FFNS = [
    Ffn(0, 8, [(128 * c, 128) for c in range(4)], False, 2, CAP0, "top", 2, 0, "eb2"),
    Ffn(1, 9, F1C, True, 3, None, None, 1, 1, None),
    Ffn(2, 10, [(0, 128)], True, 2, CAP2, "all", 2, 2, None),
    Ffn(3, 8, [(128 * c, 128) for c in range(4)], False, 2, None, None, 1, 0, "b23"),
]

SEMAPHORES = """x_loaded ctx_loaded wa0_loaded wsa_loaded rows_loaded cols_loaded consts_loaded
w0_loaded w1_loaded w2_loaded w3_loaded mask2_loaded qpos_loaded kpos_loaded maskq_loaded stored
gains_ready bias_ready lens_ready setup_steps route_exp_ready gates_ready
x_updated ln_stats_done ln_aggr_done ln_shifted ln_guessed newton_steps xn_centred xn_ready xn_turned xt_group_ready xt_tile_ready
ctx_staged q_projected k_projected v_projected q_ready k_ready v_ready kexp_ready scores_ready scores_copied
row_max_ready scores_centred exp_ready exp_sum_ready exp_recip_ready probs_ready probs_turned probs_t_ready
heads_summed heads_ready heads_scaled qs_ready ks_ready vs_projected cdup_staged vm_ready sum_plus_one heads_turned heads_t_ready out_projected x_biased
attention_zeroed dist_ready dist_steps bias_scaled biased_ready
qk_projected values_projected offsets_projected offsets_ready position_steps positions_ready distance_ready hat_abs_ready hat_ready
sampled_half sampled_max sampled_centred sampled_exp sampled_sum sampled_recip weights_ready hat_weighted_pool
hat_weighted_dve product_ready base_ready
hidden_full gate_silu_ready hidden_relu_ready hidden_gated_ready expert_summed expert_added
logits_t_full logits_t_ready logits_turned logits_ready comb_staged comb_turned comb_t_ready
route_steps mask_ready prefix_ready comb_ready xg_ready xg_turned xg_t_ready pe_passed dve_passed pool_passed""".split()


def flamingo(nc, x_in, ctx_t, wa0, wsa, wf0, wf1, wf2, wf3, rows_in, cols_in, consts_in, mask2, qpos, kpos, maskq,
             out, stop_after=8):
    with ExitStack() as stack:
        def sb(name, width, dt=F32):
            return stack.enter_context(nc.sbuf_tensor(name, [P, width], dt))

        sem = {n: stack.enter_context(nc.semaphore(n)) for n in SEMAPHORES}

        x_sb = sb("x_sb", NT * D)
        xt_sb = sb("xt_sb", NT * P)
        ctx_sb = sb("ctx_sb", NT * P)
        xn_sb = sb("xn_sb", NT * D)
        slab0 = sb("slab0", SLAB0)
        slab1 = sb("slab1", SLAB1)
        wsa_sb = sb("wsa_sb", NWSA)
        rows_sb = sb("rows_sb", NROWS)
        cols_sb = sb("cols_sb", NCOLS)
        const_sb = sb("const_sb", NCONST)
        gain_sb = sb("gain_sb", 8)
        gbias_sb = sb("gbias_sb", 3 * D)
        stats_sb = sb("stats_sb", GT * 6)
        moments_sb = sb("moments_sb", GT * 2)
        shift_sb = sb("shift_sb", GT, I32)
        rstd_sb = sb("rstd_sb", GT)
        newt_sb = sb("newt_sb", GT)
        xns_sb = sb("xns_sb", GW)
        comb_sb = sb("comb_sb", NT * E)
        m1_sb = sb("m1_sb", NT)
        rs_sb = sb("rs_sb", 4 * H)
        lens_sb = sb("lens_sb", NT)
        rlens_sb = sb("rlens_sb", NT)
        qpos_sb = sb("qpos_sb", NT, I32)
        xb_sb = sb("xb_sb", D)
        arena = sb("arena", 10700)
        ps = stack.enter_context(nc.psum_tensor("ps", [P, 4096], F32))

        def view(t, table, name):
            a, b = table[name]
            return t[:, a:b]

        def const(name):
            return view(const_sb, CONST, name)

        def row(name):
            return view(rows_sb, ROWS, name)

        def col(name):
            return view(cols_sb, COLS, name)

        ident = const("ident")

        def bank(n, a=0, b=512):
            return ps[:, 512 * n + a:512 * n + b]

        used = [0]

        def cut(width):
            used[0] += width
            assert used[0] <= 10700
            return arena[:, used[0] - width:used[0]]

        qt0 = [cut(1024) for _ in range(2)]
        kt0 = [cut(1024) for _ in range(2)]
        v0 = [cut(1024) for _ in range(2)]
        e0 = [cut(1024) for _ in range(2)]
        pt0, ot0 = cut(1024), cut(1024)
        c0 = [cut(P) for _ in range(2)]
        used[0] = 0
        qt = [cut(P) for _ in range(2)]
        kt = [cut(P) for _ in range(2)]
        kexp = [cut(512) for _ in range(2)]
        cdup = [cut(4 * S) for _ in range(2)]
        vm = [cut(HP * 32) for _ in range(2)]
        ex = [cut(1024) for _ in range(2)]
        pt, ob, obt = cut(1024), cut(P), cut(P)
        prod = [cut(1024) for _ in range(2)]
        o80 = [cut(H * NK) for _ in range(9)]
        used[0] = 0
        hid = [cut(512) for _ in range(9)]
        gate = [cut(512) for _ in range(2)]
        acc, xg, xgt, lgt, cbt = cut(512), cut(512), cut(512), cut(512), cut(512)
        combs = cut(GT * E)
        rt = [cut(NT * E) for _ in range(8)]
        logit_sb = cut(NT * E)
        small = [cut(NT) for _ in range(3)]

        hat = [slab1[:, 0:5120], slab1[:, 5120:10240]]
        hprod = slab0[:, NWF2:NWF2 + 5120]

        def positive(value):
            return not isinstance(value, int) or value > 0


        def x_tiles(t, w):
            return x_sb[:, bass.ds(t * D, w * D)]

        def ln_dve(dve, n, t, w, first=False):
            if isinstance(n, int) and n < NG or first:
                dve.wait_ge(sem["x_loaded"], 16)
            else:
                dve.wait_ge(sem["x_updated"], n - NG + 1)
            if positive(n):
                dve.wait_ge(sem["xn_ready"], n)
            dve.sem_inc(sem["dve_passed"], 1)
            for u in range(w):
                i = dve.bn_stats(stats_sb[:, 6 * u:6 * u + 6], x_sb[:, bass.ds((t + u) * D, D)])
            i.then_inc(sem["ln_stats_done"], 1)
            dve.wait_ge(sem["ln_stats_done"], n + 1)
            dve.sem_inc(sem["dve_passed"], 1)
            for u in range(w):
                i = dve.bn_aggr(moments_sb[:, 2 * u:2 * u + 2], stats_sb[:, 6 * u:6 * u + 6])
            i.then_inc(sem["ln_aggr_done"], 1)
            dve.wait_ge(sem["ln_aggr_done"], n + 1)
            var = moments_sb[:, 0:2 * w].rearrange("p (w c) -> p w c", c=2)[:, :, 1]
            dve.tensor_scalar(newt_sb[:, 0:w], var, EPS, None, ALU.add).then_inc(sem["ln_shifted"], 1)
            dve.wait_ge(sem["ln_shifted"], 2 * n + 1)
            dve.tensor_scalar(shift_sb[:, 0:w], newt_sb[:, 0:w].bitcast(I32), 1, None,
                              ALU.logical_shift_right).then_inc(sem["ln_shifted"], 1)
            dve.wait_ge(sem["ln_shifted"], 2 * n + 2)
            dve.tensor_scalar(rstd_sb[:, 0:w].bitcast(I32), shift_sb[:, 0:w], -1.0, float(0x5F3759DF),
                              ALU.mult, ALU.add).then_inc(sem["ln_guessed"], 1)

        def ln_pool(pool, n, t, w, keep=False):
            pool.wait_ge(sem["ln_guessed"], n + 1)
            y, v, a = rstd_sb[:, 0:w], newt_sb[:, 0:w], shift_sb[:, 0:w].bitcast(F32)
            for k in range(3):
                pool.tensor_tensor(a, y, y, ALU.mult).then_inc(sem["newton_steps"], 1)
                pool.wait_ge(sem["newton_steps"], 12 * n + 4 * k + 1)
                pool.tensor_tensor(a, a, v, ALU.mult).then_inc(sem["newton_steps"], 1)
                pool.wait_ge(sem["newton_steps"], 12 * n + 4 * k + 2)
                pool.sem_inc(sem["pool_passed"], 1)
                pool.tensor_scalar(a, a, -0.5, 1.5, ALU.mult, ALU.add).then_inc(sem["newton_steps"], 1)
                pool.wait_ge(sem["newton_steps"], 12 * n + 4 * k + 3)
                pool.tensor_tensor(y, y, a, ALU.mult).then_inc(sem["newton_steps"], 1)
                pool.wait_ge(sem["newton_steps"], 12 * n + 4 * k + 4)
            if positive(n):
                pool.wait_ge(sem["xn_turned"], n)
            pool.sem_inc(sem["pool_passed"], 1)

            def wide(a):
                return a.unsqueeze(2).broadcast_to([P, w, D])

            def rows_of(a):
                return a.rearrange("p (w d) -> p w d", d=D)

            mean = moments_sb[:, 0:2 * w].rearrange("p (w c) -> p w c", c=2)[:, :, 0]
            xns = rows_of(xns_sb[:, 0:w * D])
            pool.tensor_tensor(xns, rows_of(x_tiles(t, w)), wide(mean), ALU.subtract).then_inc(sem["xn_centred"], 1)
            pool.wait_ge(sem["xn_centred"], n + 1)
            if keep:
                pool.tensor_tensor(rows_of(xn_sb[:, bass.ds(t * D, w * D)]), xns, wide(y), ALU.mult)
            pool.tensor_tensor(xns, xns, wide(y), ALU.mult).then_inc(sem["xn_ready"], 1)

        def updates(n):
            return n - NG + 1

        def ln_pe(pe, n, out_ps, w):
            pe.wait_ge(sem["xn_ready"], n + 1)
            for u in range(w):
                i = pe.transpose(out_ps[:, u * P:(u + 1) * P], xns_sb[:, u * D:(u + 1) * D], ident)
            i.then_inc(sem["xn_turned"], 1)

        def ln_act(act, n, out_ps, t, w):
            act.wait_ge(sem["xn_turned"], n + 1)
            act.activation(xt_sb[:, bass.ds(t * P, w * P)], out_ps[:, 0:w * P], ACT.Copy).then_inc(
                sem["xt_group_ready" if w == GT else "xt_tile_ready"], w)

        def ln_number_attn(layer, t):
            return NG + (NT + NG) * layer + t

        def ln_number_ffn(layer, g):
            return NG + (NT + NG) * layer + NT + g

        def steps(eng, lag, step):
            first = lag + 1
            last = first + (NT - first) // 2 * 2
            for u in range(first):
                step(u, u % 2)
            with eng.Fori(0, (last - first) // 2) as i:
                u = i * 2 + first
                step(u, first % 2)
                step(u + 1, (first + 1) % 2)
            for u in range(last, NT + lag):
                step(u, u % 2)

        def on(u, back):
            return not isinstance(u, int) or 0 <= u - back < NT

        def a0_w(name):
            return view(slab1, WA0, name)

        Q0 = ps[:, 0:1024]
        K0 = ps[:, 1024:2048]
        T0 = ps[:, 2048:3072]
        S0 = ps[:, 3072:4096]

        def a0_pe(pe):
            pe.wait_ge(sem["wa0_loaded"], 16)

            def step(u, p):
                cur, old = on(u, 0), on(u, 1)
                t = u - 1
                if cur:
                    pe.wait_ge(sem["xt_group_ready"], u + 1)
                    pe.wait_ge(sem["ctx_staged"], u + 1)
                    if positive(u):
                        pe.wait_ge(sem["v_ready"], u)
                    for c in range(8):
                        i = pe.matmul(Q0[:, c * P:(c + 1) * P], a0_w("q")[:, c * P:(c + 1) * P],
                                      xt_sb[:, bass.ds(u * P, P)], start=True, stop=True)
                    i.then_inc(sem["q_projected"], 1)
                    if positive(t):
                        pe.wait_ge(sem["heads_ready"], t)
                    for c in range(8):
                        i = pe.matmul(K0[:, c * P:(c + 1) * P], a0_w("k")[:, c * P:(c + 1) * P], c0[p],
                                      start=True, stop=True)
                    i.then_inc(sem["k_projected"], 1)
                if old:
                    pe.wait_ge(sem["probs_ready"], t + 1)
                    if positive(updates(ln_number_attn(0, t - 1))):
                        pe.wait_ge(sem["x_updated"], updates(ln_number_attn(0, t - 1)))
                    if positive(t - 1):
                        pe.wait_ge(sem["xt_tile_ready"], t - 1)
                    for c in range(8):
                        i = pe.transpose(T0[:, c * P:(c + 1) * P], e0[1 - p][:, c * P:(c + 1) * P], ident)
                    i.then_inc(sem["probs_turned"], 1)
                if cur:
                    pe.wait_ge(sem["q_ready"], u + 1)
                    for j in range(2):
                        i = pe.matmul(Q0[:, j * 512:(j + 1) * 512], c0[p], a0_w("v")[:, j * 512:(j + 1) * 512],
                                      start=True, stop=True)
                    i.then_inc(sem["v_projected"], 1)
                    pe.wait_ge(sem["k_ready"], u + 1)
                    if positive(u):
                        pe.wait_ge(sem["scores_centred"], u)
                    pe.sem_inc(sem["pe_passed"], 1)
                    for h2 in range(2):
                        h = slice(64 * h2, 64 * h2 + 64)
                        for c in range(8):
                            for b in range(2):
                                at = slice(c * P + b * 64, c * P + b * 64 + 64)
                                i = pe.matmul(S0[h, at], qt0[p][h, at], kt0[p][h, at], start=True, stop=True)
                    i.then_inc(sem["scores_ready"], 1)
                if old:
                    pe.wait_ge(sem["v_ready"], t + 1)
                    pe.wait_ge(sem["probs_t_ready"], t + 1)
                    pe.sem_inc(sem["pe_passed"], 1)
                    for b in range(2):
                        r = slice(64 * b, 64 * b + 64)
                        for c in range(8):
                            for h2 in range(2):
                                i = pe.matmul(K0[64 * h2:64 * h2 + 64, b * 512 + c * 64:b * 512 + c * 64 + 64],
                                              v0[1 - p][r, c * P + h2 * 64:c * P + h2 * 64 + 64],
                                              pt0[r, c * P + h2 * 64:c * P + h2 * 64 + 64], start=True, stop=True)
                    i.then_inc(sem["heads_summed"], 1)
                if on(u, 2):
                    if old:
                        pe.wait_ge(sem["probs_t_ready"], t + 1)
                    if positive(u - 2):
                        pe.wait_ge(sem["xt_tile_ready"], u - 2)
                    ln_pe(pe, ln_number_attn(0, u - 2), T0[:, 512:640], 1)
                if old:
                    pe.wait_ge(sem["heads_ready"], t + 1)
                    for c in range(8):
                        i = pe.matmul(T0[:, 0:P], ot0[:, c * P:(c + 1) * P],
                                      a0_w("u")[:, c * P:(c + 1) * P], start=c == 0, stop=c == 7)
                    i.then_inc(sem["out_projected"], 1)
            steps(pe, 2, step)

        def a0_dve(dve):
            def evict(src, dst, bias, ready, full, t):
                dve.wait_ge(sem[full], t + 1)
                dve.tensor_tensor(dst.rearrange("p (c t) -> p c t", c=8), src.rearrange("p (c t) -> p c t", c=8),
                                  bias, ALU.add).then_inc(sem[ready], 1)

            def step(u, p):
                t = u - 1
                if on(u, 1):
                    o = e0[1 - p].rearrange("p (h t) -> p h t", h=H)
                    dve.wait_ge(sem["exp_ready"], t + 1)
                    if positive(t):
                        dve.wait_ge(sem["probs_ready"], t)
                    dve.tensor_reduce(rs_sb[:, H:2 * H], o, AX.X, ALU.add).then_inc(sem["exp_sum_ready"], 1)
                    dve.wait_ge(sem["exp_sum_ready"], t + 1)
                    dve.reciprocal(rs_sb[:, 2 * H:3 * H], rs_sb[:, H:2 * H]).then_inc(sem["exp_recip_ready"], 1)
                if on(u, 0):
                    evict(Q0, qt0[p], col("bq0").unsqueeze(2).broadcast_to([P, 8, P]), "q_ready", "q_projected", u)
                    evict(K0, kt0[p], col("bk0").unsqueeze(2).broadcast_to([P, 8, P]), "k_ready", "k_projected", u)
                    evict(Q0, v0[p], row("bv0").rearrange("p (c t) -> p c t", c=8), "v_ready", "v_projected", u)
                    s = S0.rearrange("p (h t) -> p h t", h=H)
                    dve.wait_ge(sem["scores_ready"], u + 1)
                    dve.tensor_reduce(rs_sb[:, 0:H], s, AX.X, ALU.max).then_inc(sem["row_max_ready"], 1)
                    dve.wait_ge(sem["row_max_ready"], u + 1)
                    dve.tensor_tensor(e0[p].rearrange("p (h t) -> p h t", h=H), s,
                                      rs_sb[:, 0:H].unsqueeze(2).broadcast_to([P, H, S]),
                                      ALU.subtract).then_inc(sem["scores_centred"], 1)
                if on(u, 1):
                    n = ln_number_attn(0, t)
                    dve.wait_ge(sem["out_projected"], t + 1)
                    dve.wait_ge(sem["x_biased"], t + 1)
                    dve.scalar_tensor_tensor(x_tiles(t, 1), T0[:, 0:P], gain_sb[:, 0:1], xb_sb[:], ALU.mult,
                                             ALU.add).then_inc(sem["x_updated"], 1)
                    ln_dve(dve, n, t, 1)
            steps(dve, 2, step)

        def a0_act(act):
            def step(u, p):
                t = u - 1
                if on(u, 1):
                    act.wait_ge(sem["probs_turned"], t + 1)
                    act.activation(pt0, T0, ACT.Copy).then_inc(sem["probs_t_ready"], 1)
                if on(u, 0):
                    act.wait_ge(sem["scores_centred"], u + 1)
                    act.activation(e0[p], e0[p], ACT.Exp, scale=HD0 ** -0.5).then_inc(sem["exp_ready"], 1)
                if on(u, 1):
                    act.wait_ge(sem["heads_summed"], t + 1)
                    act.activation(ot0.rearrange("p (c b q) -> p b c q", c=8, b=2),
                                   K0.rearrange("p (b c q) -> p b c q", b=2, c=8),
                                   ACT.Copy).then_inc(sem["heads_ready"], 1)
                if on(u, 2):
                    ln_act(act, ln_number_attn(0, u - 2), T0[:, 512:640], u - 2, 1)
            steps(act, 2, step)

        def a0_pool(pool):
            def stage(t, p):
                if positive(t - 1):
                    pool.wait_ge(sem["v_projected"], t - 1)
                pool.tensor_copy(c0[p], ctx_sb[:, bass.ds(t * P, P)]).then_inc(sem["ctx_staged"], 1)

            def step(u, p):
                if isinstance(u, int) and u == 0:
                    stage(0, 0)
                if on(u, 1):
                    t, o = u - 1, e0[1 - p].rearrange("p (h t) -> p h t", h=H)
                    pool.wait_ge(sem["exp_recip_ready"], t + 1)
                    pool.tensor_tensor(o, o, rs_sb[:, 2 * H:3 * H].unsqueeze(2).broadcast_to([P, H, S]),
                                       ALU.mult).then_inc(sem["probs_ready"], 1)
                if on(u, -1):
                    stage(u + 1, 1 - p)
                if on(u, 1):
                    if positive(updates(ln_number_attn(0, t - 1))):
                        pool.wait_ge(sem["x_updated"], updates(ln_number_attn(0, t - 1)))
                    pool.sem_inc(sem["pool_passed"], 1)
                    pool.tensor_tensor(xb_sb[:], x_sb[:, bass.ds(t * D, D)], gbias_sb[:, 0:D],
                                       ALU.add).then_inc(sem["x_biased"], 1)
                    ln_pool(pool, ln_number_attn(0, t), t, 1)
            steps(pool, 2, step)

        USED_IN = dict(qs_ready=(1, 2, 3), ks_ready=(1, 2, 3), kexp_ready=(1, 2, 3), heads_scaled=(1, 2, 3),
                       heads_turned=(1, 2, 3), heads_t_ready=(1, 2, 3), biased_ready=(3,), bias_scaled=(3,),
                       vs_projected=(1, 3), cdup_staged=(1, 2, 3), vm_ready=(1, 2, 3), scores_centred=(0, 1, 3),
                       scores_ready=(0, 1, 2, 3), row_max_ready=(0, 1, 3), exp_ready=(0, 1, 3),
                       exp_sum_ready=(0, 1, 3), exp_recip_ready=(0, 1, 3), probs_turned=(0, 1, 2, 3),
                       probs_t_ready=(0, 1, 2, 3), heads_summed=(0, 1, 2, 3), out_projected=(0, 1, 2, 3),
                       x_biased=(0, 1, 2), sum_plus_one=(3,),
                       **{n: (2,) for n in ("qk_projected", "values_projected", "offsets_projected", "offsets_ready", "positions_ready",
                                            "distance_ready", "hat_abs_ready", "hat_ready", "scores_copied",
                                            "sampled_half", "sampled_max", "sampled_centred", "sampled_exp",
                                            "sampled_sum", "sampled_recip", "weights_ready", "hat_weighted_pool",
                                            "hat_weighted_dve", "product_ready")})

        def past(layer, name):
            return NT * sum(l < layer for l in USED_IN[name])

        XB = bank(0)
        SB = ps[:, 512:2560].rearrange("p (r x) -> p r x", r=4)[:, :, 0:256]
        PTB = ps[:, 2560:3584]
        OB = bank(7)

        def w_attn(layer, name):
            return view(wsa_sb, WSA, f"{name}{layer}")

        def halves():
            return [slice(0, 64), slice(64, 128)]

        def narrow_project(pe, L, u, p):
            pe.matmul(XB[:, 0:P], w_attn(L, "q"), xt_sb[:, bass.ds(u * P, P)], start=True, stop=True)
            pe.matmul(XB[:, P:2 * P], w_attn(L, "k"), ctx_sb[:, bass.ds(u * P, P)], start=True, stop=True)
            for b in range(2):
                i = pe.matmul(XB[:, 256 + b * P:256 + (b + 1) * P], cdup[p][:, b * P:(b + 1) * P],
                              w_attn(L, "v"), start=True, stop=True)
            i.then_inc(sem["vs_projected"], 1)

        def narrow_scores(pe, p):
            for r in range(4):
                rows = slice(32 * r, 32 * r + 32)
                for b in range(2):
                    i = pe.matmul(SB[64 * b:64 * b + 64, r, :], qt[p][rows, 64 * b:64 * b + 64],
                                  kexp[p][rows, 256 * b:256 * b + 256], start=True, stop=True)
            i.then_inc(sem["scores_ready"], 1)

        def narrow_heads(pe, L, t, old_p):
            pe.wait_ge(sem["vm_ready"], t + 1 + past(L, "vm_ready"))
            pe.wait_ge(sem["x_updated"], updates(ln_number_attn(L, t - 1)))
            for c in range(HP):
                i = pe.matmul(OB[:, c * 32:(c + 1) * 32], pt[:, c * P:(c + 1) * P],
                              vm[old_p][:, c * 32:(c + 1) * 32], start=True, stop=True)
            i.then_inc(sem["heads_summed"], 1)

        def narrow_output(pe, L, t):
            pe.wait_ge(sem["heads_scaled"], t + 1 + past(L, "heads_scaled"))
            pe.transpose(OB[:, 256:384], ob, ident).then_inc(sem["heads_turned"], 1)
            pe.wait_ge(sem["heads_t_ready"], t + 1 + past(L, "heads_t_ready"))
            pe.matmul(OB[:, 384:512], obt, w_attn(L, "o"), start=True, stop=True).then_inc(sem["out_projected"], 1)

        def narrow_evict_qk(act, L, u, p):
            act.wait_ge(sem["vs_projected"], u + 1 + past(L, "vs_projected"))
            for dst, at, name, done in ((qt[p], 0, "bq", "qs_ready"), (kt[p], P, "bk", "ks_ready")):
                if L == 3:
                    i = act.activation(dst, XB[:, at:at + P], ACT.Copy)
                else:
                    i = act.activation(dst, XB[:, at:at + P], ACT.Identity, bias=col(f"{name}{L}"))
                i.then_inc(sem[done], 1)

        def narrow_values(dve, L, u, p):
            dve.wait_ge(sem["ks_ready"], u + 1 + past(L, "ks_ready"))
            dve.sem_inc(sem["dve_passed"], 1)
            for h2, r in enumerate(halves()):
                dst = vm[p][r].rearrange("p (c b h d) -> p h b c d", c=HP, b=2, h=2)[:, h2]
                src = XB[r, 256:512].rearrange("p (b c h d) -> p h b c d", b=2, c=HP, h=2)[:, h2]
                if L == 3:
                    i = dve.tensor_copy(dst, src)
                else:
                    bv = row(f"bv{L}")[r].rearrange("p (c h d) -> p h c d", c=HP, h=2)[:, h2]
                    i = dve.tensor_tensor(dst, src, bv.unsqueeze(1).broadcast_to([64, 2, HP, HD]), ALU.add)
            i.then_inc(sem["vm_ready"], 1)

        def narrow_scale(dve, L, t, recip):
            dve.wait_ge(sem["heads_summed"], t + 1 + past(L, "heads_summed"))
            for b, r in enumerate(halves()):
                i = dve.tensor_tensor(ob[r].rearrange("p (c h d) -> p c h d", c=HP, h=2),
                                      OB[r, 0:256].rearrange("p (c b h d) -> p b c h d", c=HP, b=2, h=2)[:, b],
                                      recip[r].rearrange("p (c h) -> p c h", h=2).unsqueeze(3).broadcast_to(
                                          [64, HP, 2, HD]), ALU.mult)
            i.then_inc(sem["heads_scaled"], 1)

        def narrow_update(dve, L, t):
            dve.wait_ge(sem["out_projected"], t + 1 + past(L, "out_projected"))
            if L == 3:
                res = x_tiles(t, 1)
            else:
                dve.wait_ge(sem["x_biased"], t + 1 + past(L, "x_biased"))
                res = xb_sb[:]
            dve.scalar_tensor_tensor(x_tiles(t, 1), OB[:, 384:512], gain_sb[:, L:L + 1], res, ALU.mult,
                                     ALU.add).then_inc(sem["x_updated"], 1)
            ln_dve(dve, ln_number_attn(L, t), t, 1)

        def narrow_stage(pool, L, t, p):
            if positive(t - 1 + past(L, "vs_projected")):
                pool.wait_ge(sem["vs_projected"], t - 1 + past(L, "vs_projected"))
            pool.tensor_copy(cdup[p].rearrange("p (b c t) -> p b c t", b=2, c=2),
                             ctx_sb[:, bass.ds(t * P, P)].rearrange("p (b t) -> p b t", b=2).unsqueeze(2).broadcast_to(
                                 [P, 2, 2, S])).then_inc(sem["cdup_staged"], 1)

        def narrow_expand(pool, L, u, p):
            pool.wait_ge(sem["ks_ready"], u + 1 + past(L, "ks_ready"))
            pool.tensor_tensor(kexp[p].rearrange("p (b h t) -> p b h t", b=2, h=4),
                               kt[p].rearrange("p (b t) -> p b t", b=2).unsqueeze(2).broadcast_to([P, 2, 4, S]),
                               const("headmask").unsqueeze(1).unsqueeze(3).broadcast_to([P, 2, 4, S]),
                               ALU.mult).then_inc(sem["kexp_ready"], 1)

        def narrow_pool_tail(pool, L, t):
            if L != 3:
                pool.wait_ge(sem["x_updated"], updates(ln_number_attn(L, t - 1)))
                pool.sem_inc(sem["pool_passed"], 1)
                pool.tensor_tensor(xb_sb[:], x_sb[:, bass.ds(t * D, D)], gbias_sb[:, L * D:(L + 1) * D],
                                   ALU.add).then_inc(sem["x_biased"], 1)
            ln_pool(pool, ln_number_attn(L, t), t, 1, keep=L == 1)

        def zero_values(dve):
            dve.memset(vm[0], 0.0)
            dve.memset(vm[1], 0.0).then_inc(sem["attention_zeroed"], 1)

        def a13_pe(L):
            def program(pe):
                pe.wait_ge(sem["wsa_loaded"], 16)
                pe.wait_ge(sem["xt_group_ready"], (L + 1) * NT)

                def step(u, p):
                    t = u - 1
                    if on(u, 0):
                        pe.wait_ge(sem["cdup_staged"], u + 1 + past(L, "cdup_staged"))
                        if positive(u + past(L, "vm_ready")):
                            pe.wait_ge(sem["vm_ready"], u + past(L, "vm_ready"))
                        pe.wait_ge(sem["xt_tile_ready"], u - 2 + L * NT)
                        narrow_project(pe, L, u, p)
                    if on(u, 1):
                        pe.wait_ge(sem["exp_ready"], t + 1 + past(L, "exp_ready"))
                        pe.wait_ge(sem["probs_t_ready"], t + past(L, "probs_t_ready"))
                        for c in range(HP):
                            i = pe.transpose(PTB[:, c * P:(c + 1) * P], ex[1 - p][:, c * P:(c + 1) * P], ident)
                        i.then_inc(sem["probs_turned"], 1)
                    if on(u, 0):
                        pe.wait_ge(sem["qs_ready"], u + 1 + past(L, "qs_ready"))
                        pe.wait_ge(sem["kexp_ready"], u + 1 + past(L, "kexp_ready"))
                        if positive(u + past(L, "biased_ready" if L == 3 else "scores_centred")):
                            pe.wait_ge(sem["biased_ready" if L == 3 else "scores_centred"], u + past(L, "biased_ready" if L == 3 else "scores_centred"))
                        pe.sem_inc(sem["pe_passed"], 1)
                        narrow_scores(pe, p)
                    if on(u, 2):
                        if on(u, 0):
                            pe.wait_ge(sem["vm_ready"], u + 1 + past(L, "vm_ready"))
                        pe.wait_ge(sem["xt_tile_ready"], u - 2 + L * NT)
                        ln_pe(pe, ln_number_attn(L, u - 2), XB, 1)
                    if on(u, 1):
                        pe.wait_ge(sem["probs_t_ready"], t + 1 + past(L, "probs_t_ready"))
                        narrow_heads(pe, L, t, 1 - p)
                        narrow_output(pe, L, t)
                steps(pe, 2, step)
            return program

        def a13_act(L):
            def program(act):
                def step(u, p):
                    t = u - 1
                    if on(u, 0):
                        narrow_evict_qk(act, L, u, p)
                    if on(u, 1):
                        act.wait_ge(sem["probs_turned"], t + 1 + past(L, "probs_turned"))
                        act.activation(pt, PTB, ACT.Copy).then_inc(sem["probs_t_ready"], 1)
                    if on(u, 2):
                        ln_act(act, ln_number_attn(L, u - 2), XB, u - 2, 1)
                    if on(u, 1):
                        act.wait_ge(sem["heads_turned"], t + 1 + past(L, "heads_turned"))
                        act.activation(obt, OB[:, 256:384], ACT.Copy).then_inc(sem["heads_t_ready"], 1)
                    if on(u, 0):
                        act.wait_ge(sem["scores_centred"], u + 1 + past(L, "scores_centred"))
                        act.activation(ex[p], ex[p], ACT.Exp, scale=1.0 if L == 3 else HD ** -0.5).then_inc(
                            sem["exp_ready"], 1)
                steps(act, 2, step)
            return program

        def a13_dve(L):
            def program(dve):
                zero_values(dve)
                dve.wait_ge(sem["attention_zeroed"], {1: 1, 3: 3}[L])

                def step(u, p):
                    t = u - 1
                    if on(u, 1):
                        dve.wait_ge(sem["exp_ready"], t + 1 + past(L, "exp_ready"))
                        dve.tensor_reduce(rs_sb[:, H:2 * H], ex[1 - p].rearrange("p (h t) -> p h t", h=H), AX.X,
                                          ALU.add).then_inc(sem["exp_sum_ready"], 1)
                        dve.wait_ge(sem["exp_sum_ready"], t + 1 + past(L, "exp_sum_ready"))
                        if L == 3:
                            dve.tensor_scalar(rs_sb[:, H:2 * H], rs_sb[:, H:2 * H], 1.0, None, ALU.add).then_inc(
                                sem["sum_plus_one"], 1)
                            dve.wait_ge(sem["sum_plus_one"], t + 1 + past(L, "sum_plus_one"))
                        dve.reciprocal(rs_sb[:, 2 * H:3 * H], rs_sb[:, H:2 * H]).then_inc(sem["exp_recip_ready"], 1)
                        dve.wait_ge(sem["exp_recip_ready"], t + 1 + past(L, "exp_recip_ready"))
                    if on(u, 0):
                        narrow_values(dve, L, u, p)
                        dve.wait_ge(sem["scores_ready"], u + 1 + past(L, "scores_ready"))
                        s4 = SB
                        flat = ex[p].rearrange("p (r x) -> p r x", r=4)
                        if L == 3:
                            dve.wait_ge(sem["bias_scaled"], u + 1 + past(L, "bias_scaled"))
                            dve.scalar_tensor_tensor(flat, s4, float(np.float32(HD ** -0.5)),
                                                     prod[p].rearrange("p (r x) -> p r x", r=4), ALU.mult,
                                                     ALU.add).then_inc(sem["biased_ready"], 1)
                            dve.wait_ge(sem["biased_ready"], u + 1 + past(L, "biased_ready"))
                            s4 = flat
                        heads = s4.rearrange("p r (h t) -> p r h t", h=4)
                        dve.tensor_reduce(rs_sb[:, 0:H].rearrange("p (r h) -> p r h", r=4), heads, AX.X,
                                          ALU.max).then_inc(sem["row_max_ready"], 1)
                        dve.wait_ge(sem["row_max_ready"], u + 1 + past(L, "row_max_ready"))
                        dve.tensor_tensor(ex[p].rearrange("p (r h t) -> p r h t", r=4, h=4), heads,
                                          rs_sb[:, 0:H].rearrange("p (r h) -> p r h", r=4).unsqueeze(3).broadcast_to(
                                              [P, 4, 4, S]), ALU.subtract).then_inc(sem["scores_centred"], 1)
                    if on(u, 1):
                        narrow_scale(dve, L, t, rs_sb[:, 2 * H:3 * H])
                        narrow_update(dve, L, t)
                steps(dve, 2, step)
            return program

        def a13_pool(L):
            def bias_of(pool, t, p):
                if positive(t - 1 + past(L, "biased_ready")):
                    pool.wait_ge(sem["biased_ready"], t - 1 + past(L, "biased_ready"))
                pool.sem_inc(sem["pool_passed"], 1)
                pool.tensor_tensor(prod[p].rearrange("p (h t) -> p h t", h=H),
                                   const("slopes").unsqueeze(2).broadcast_to([P, H, S]),
                                   xn_sb[:, bass.ds(t * S, S)].unsqueeze(1).broadcast_to([P, H, S]),
                                   ALU.mult).then_inc(sem["bias_scaled"], 1)

            def program(pool):
                if L == 3:
                    pool.wait_ge(sem["dist_steps"], 4)

                def step(u, p):
                    if isinstance(u, int) and u == 0:
                        narrow_stage(pool, L, 0, 0)
                        if L == 3:
                            bias_of(pool, 0, 0)
                    if on(u, 0):
                        narrow_expand(pool, L, u, p)
                    if on(u, -1):
                        narrow_stage(pool, L, u + 1, 1 - p)
                        if L == 3:
                            bias_of(pool, u + 1, 1 - p)
                    if on(u, 1):
                        narrow_pool_tail(pool, L, u - 1)
                steps(pool, 2, step)
            return program

        PAIRS_POOL = 5
        NSAMP = H * NK
        wbuf = slab0[:, NWF2:NWF2 + NSAMP * S]
        product = xn_sb[:, 0:NSAMP * S // 2]
        pos, samp, wgt, offs, base = o80[0], o80[1], o80[2], o80[3], o80[4]
        tmp = [o80[5], o80[6]]
        kscore = prod

        def a2_pe(pe):
            pe.wait_ge(sem["wsa_loaded"], 16)
            pe.wait_ge(sem["xt_group_ready"], 3 * NT)

            def step(u, p):
                t = u - 2
                pe.wait_ge(sem["xt_tile_ready"], u - 3 + 2 * NT)
                if on(u, 1):
                    pe.wait_ge(sem["offsets_ready"], u + past(2, "offsets_ready"))
                if on(u, 0):
                    pe.wait_ge(sem["kexp_ready"], u + past(2, "kexp_ready"))
                    pe.matmul(XB[:, 0:P], w_attn(2, "q"), xt_sb[:, bass.ds(u * P, P)], start=True, stop=True)
                    pe.matmul(XB[:, P:2 * P], w_attn(2, "k"), ctx_sb[:, bass.ds(u * P, P)], start=True,
                              stop=True).then_inc(sem["qk_projected"], 1)
                if on(u, 2):
                    pe.wait_ge(sem["cdup_staged"], t + 1 + past(2, "cdup_staged"))
                    pe.sem_inc(sem["pe_passed"], 1)
                    if on(u, 0):
                        pe.wait_ge(sem["ks_ready"], u + 1 + past(2, "ks_ready"))
                        pe.sem_inc(sem["pe_passed"], 1)
                    for b in range(2):
                        i = pe.matmul(XB[:, 256 + b * P:256 + (b + 1) * P], cdup[p][:, b * P:(b + 1) * P],
                                      w_attn(2, "v"), start=True, stop=True)
                    i.then_inc(sem["values_projected"], 1)
                if on(u, 0):
                    pe.wait_ge(sem["qs_ready"], u + 1 + past(2, "qs_ready"))
                    pe.wait_ge(sem["ks_ready"], u + 1 + past(2, "ks_ready"))
                    if on(u, 2):
                        pe.wait_ge(sem["vm_ready"], t + 1 + past(2, "vm_ready"))
                    pe.sem_inc(sem["pe_passed"], 1)
                    pe.matmul(XB[:, 0:NSAMP], qt[p], w_attn(2, "off"), start=True, stop=True).then_inc(
                        sem["offsets_projected"], 1)
                    pe.wait_ge(sem["kexp_ready"], u + 1 + past(2, "kexp_ready"))
                    if positive(u + past(2, "scores_copied")):
                        pe.wait_ge(sem["scores_copied"], u + past(2, "scores_copied"))
                    pe.sem_inc(sem["pe_passed"], 1)
                    narrow_scores(pe, p)
                if on(u, 2):
                    pe.wait_ge(sem["hat_weighted_pool"], t + 1 + past(2, "hat_weighted_pool"))
                    pe.wait_ge(sem["hat_weighted_dve"], t + 1 + past(2, "hat_weighted_dve"))
                    pe.wait_ge(sem["probs_t_ready"], t + past(2, "probs_t_ready"))
                    for c in range(HP):
                        for k in range(NK):
                            at = (c * NK + k) * P
                            i = pe.matmul(PTB[:, c * P:(c + 1) * P], wbuf[:, at:at + P], ident, start=k == 0,
                                          stop=k == NK - 1)
                    i.then_inc(sem["probs_turned"], 1)
                    pe.wait_ge(sem["probs_t_ready"], t + 1 + past(2, "probs_t_ready"))
                    narrow_heads(pe, 2, t, p)
                    narrow_output(pe, 2, t)
                if on(u, 3):
                    if on(u, 0):
                        pe.wait_ge(sem["offsets_ready"], u + 1 + past(2, "offsets_ready"))
                    elif on(u, 2):
                        pe.wait_ge(sem["vm_ready"], t + 1 + past(2, "vm_ready"))
                    ln_pe(pe, ln_number_attn(2, u - 3), XB, 1)
            steps(pe, 3, step)

        def a2_act(act):
            def step(u, p):
                t = u - 2
                if on(u, 0):
                    act.wait_ge(sem["qk_projected"], u + 1 + past(2, "qk_projected"))
                    act.activation(qt[p], XB[:, 0:P], ACT.Identity, bias=col("bq2")).then_inc(sem["qs_ready"], 1)
                    act.activation(kt[p], XB[:, P:2 * P], ACT.Identity, bias=col("bk2")).then_inc(sem["ks_ready"], 1)
                    act.wait_ge(sem["scores_ready"], u + 1 + past(2, "scores_ready"))
                    if positive(2 * (u - 1) + past(2, "product_ready")):
                        act.wait_ge(sem["product_ready"], 2 * (u - 1) + past(2, "product_ready"))
                    act.activation(kscore[p].rearrange("p (r x) -> p r x", r=4), SB, ACT.Copy,
                                   scale=float(np.float32(0.5 * HD ** -0.5))).then_inc(sem["scores_copied"], 1)
                    act.wait_ge(sem["distance_ready"], u + 1 + past(2, "distance_ready"))
                    act.activation(hat[p], hat[p], ACT.Abs).then_inc(sem["hat_abs_ready"], 1)
                if on(u, 2):
                    act.wait_ge(sem["probs_turned"], t + 1 + past(2, "probs_turned"))
                    act.activation(pt, PTB, ACT.Copy).then_inc(sem["probs_t_ready"], 1)
                if on(u, 1):
                    act.wait_ge(sem["sampled_centred"], u + past(2, "sampled_centred"))
                    act.activation(samp, samp, ACT.Exp).then_inc(sem["sampled_exp"], 1)
                if on(u, 0):
                    act.wait_ge(sem["hat_abs_ready"], u + 1 + past(2, "hat_abs_ready"))
                    act.activation(hat[p], hat[p], ACT.Relu, scale=-1.0, bias=1.0).then_inc(sem["hat_ready"], 1)
                if on(u, 2):
                    act.wait_ge(sem["heads_turned"], t + 1 + past(2, "heads_turned"))
                    act.activation(obt, OB[:, 256:384], ACT.Copy).then_inc(sem["heads_t_ready"], 1)
                if on(u, 3):
                    ln_act(act, ln_number_attn(2, u - 3), XB, u - 3, 1)
            steps(act, 3, step)

        def a2_dve(dve):
            zero_values(dve)
            dve.tensor_tensor(base, row("boff"), const("refloc"), ALU.add).then_inc(sem["base_ready"], 1)
            dve.wait_ge(sem["attention_zeroed"], 2)
            dve.wait_ge(sem["base_ready"], 1)

            def samples(u, p, half):
                n = NSAMP // 2
                hs = slice(half * n * S, (half + 1) * n * S)
                dve.tensor_tensor(product.rearrange("p (h k j) -> p h k j", h=HP, k=NK),
                                  hat[1 - p][:, hs].rearrange("p (h k j) -> p h k j", h=HP, k=NK),
                                  kscore[1 - p][:, half * 512:half * 512 + 512].rearrange(
                                      "p (h j) -> p h j", h=HP).unsqueeze(2).broadcast_to([P, HP, NK, S]),
                                  ALU.mult).then_inc(sem["product_ready"], 1)
                dve.wait_ge(sem["product_ready"], (u - 1) * 2 + half + 1)
                dve.tensor_reduce(samp[:, half * n:(half + 1) * n], product.rearrange("p (s j) -> p s j", j=S), AX.X,
                                  ALU.add).then_inc(sem["sampled_half"], 1)

            def step(u, p):
                t = u - 2
                if on(u, 2):
                    dve.wait_ge(sem["values_projected"], t + 1 + past(2, "values_projected"))
                    for h2, r in enumerate(halves()):
                        dst = vm[p][r].rearrange("p (c b h d) -> p h b c d", c=HP, b=2, h=2)[:, h2]
                        src = XB[r, 256:512].rearrange("p (b c h d) -> p h b c d", b=2, c=HP, h=2)[:, h2]
                        bv = row("bv2")[r].rearrange("p (c h d) -> p h c d", c=HP, h=2)[:, h2]
                        i = dve.tensor_tensor(dst, src, bv.unsqueeze(1).broadcast_to([64, 2, HP, HD]), ALU.add)
                    i.then_inc(sem["vm_ready"], 1)
                if on(u, 0):
                    dve.wait_ge(sem["offsets_projected"], u + 1 + past(2, "offsets_projected"))
                    if positive(u + past(2, "positions_ready")):
                        dve.wait_ge(sem["positions_ready"], u + past(2, "positions_ready"))
                    dve.tensor_tensor(offs, XB[:, 0:NSAMP], base, ALU.add).then_inc(sem["offsets_ready"], 1)
                if on(u, 1):
                    dve.wait_ge(sem["hat_ready"], u + past(2, "hat_ready"))
                    dve.wait_ge(sem["scores_copied"], u + past(2, "scores_copied"))
                    samples(u, p, 0)
                if on(u, 0):
                    dve.wait_ge(sem["positions_ready"], u + 1 + past(2, "positions_ready"))
                    if positive(u - 1 + past(2, "hat_weighted_pool")):
                        dve.wait_ge(sem["hat_weighted_pool"], u - 1 + past(2, "hat_weighted_pool"))
                    dve.tensor_tensor(hat[p].rearrange("p (s j) -> p s j", j=S),
                                      const("iota64").unsqueeze(1).broadcast_to([P, NSAMP, S]),
                                      pos.unsqueeze(2).broadcast_to([P, NSAMP, S]), ALU.subtract).then_inc(
                        sem["distance_ready"], 1)
                if on(u, 1):
                    dve.wait_ge(sem["sampled_half"], u * 2 - 1)
                    samples(u, p, 1)
                    dve.wait_ge(sem["sampled_half"], u * 2)
                    s3 = samp.rearrange("p (h k) -> p h k", k=NK)

                    def wide(a):
                        return a.unsqueeze(2).broadcast_to([P, H, NK])

                    dve.tensor_reduce(rs_sb[:, 0:H], s3, AX.X, ALU.max).then_inc(sem["sampled_max"], 1)
                    dve.wait_ge(sem["sampled_max"], u + past(2, "sampled_max"))
                    dve.tensor_tensor(s3, s3, wide(rs_sb[:, 0:H]), ALU.subtract).then_inc(sem["sampled_centred"], 1)
                    dve.wait_ge(sem["sampled_exp"], u + past(2, "sampled_exp"))
                    dve.tensor_reduce(rs_sb[:, H:2 * H], s3, AX.X, ALU.add).then_inc(sem["sampled_sum"], 1)
                    dve.wait_ge(sem["sampled_sum"], u + past(2, "sampled_sum"))
                    dve.reciprocal(rs_sb[:, 2 * H:3 * H], rs_sb[:, H:2 * H]).then_inc(sem["sampled_recip"], 1)
                    dve.wait_ge(sem["sampled_recip"], u + past(2, "sampled_recip"))
                    if positive(u - 1 + past(2, "hat_weighted_pool")):
                        dve.wait_ge(sem["hat_weighted_pool"], u - 1 + past(2, "hat_weighted_pool"))
                    dve.scalar_tensor_tensor(wgt.rearrange("p (h k) -> p h k", k=NK), s3, 0.5,
                                             wide(rs_sb[:, 2 * H:3 * H]), ALU.mult, ALU.mult).then_inc(
                        sem["weights_ready"], 1)
                    dve.wait_ge(sem["weights_ready"], u + past(2, "weights_ready"))
                    dve.wait_ge(sem["probs_turned"], u - 1 + past(2, "probs_turned"))
                    weight(dve, 1 - p, PAIRS_POOL, HP).then_inc(sem["hat_weighted_dve"], 1)
                if on(u, 2):
                    dve.wait_ge(sem["heads_summed"], t + 1 + past(2, "heads_summed"))
                    for b, r in enumerate(halves()):
                        i = dve.tensor_copy(ob[r].rearrange("p (c h d) -> p c h d", c=HP, h=2),
                                            OB[r, 0:256].rearrange("p (c b h d) -> p b c h d", c=HP, b=2, h=2)[:, b])
                    i.then_inc(sem["heads_scaled"], 1)
                    narrow_update(dve, 2, t)
            steps(dve, 3, step)

        def weight(eng, p, c0, c1):
            for h2 in range(2):
                def part(a, order):
                    return a.rearrange(order, c=HP, h=2, k=NK)[:, c0:c1, h2]
                i = eng.tensor_tensor(part(wbuf, "p (c k h j) -> p c h k j"),
                                      part(hat[p], "p (c h k j) -> p c h k j"),
                                      part(wgt, "p (c h k) -> p c h k").unsqueeze(3).broadcast_to(
                                          [P, c1 - c0, NK, S]), ALU.mult)
            return i

        def a2_pool(pool):
            def positions(u):
                k = [0]

                def done(ins):
                    ins.then_inc(sem["position_steps"], 1)
                    k[0] += 1
                    pool.wait_ge(sem["position_steps"], u * 8 + k[0])

                m = lens_sb[:, bass.ds(u, 1)].broadcast_to([P, NSAMP])
                rm = rlens_sb[:, bass.ds(u, 1)].broadcast_to([P, NSAMP])
                a, b = tmp
                pool.wait_ge(sem["offsets_ready"], u + 1 + past(2, "offsets_ready"))
                if positive(u + past(2, "distance_ready")):
                    pool.wait_ge(sem["distance_ready"], u + past(2, "distance_ready"))
                pool.sem_inc(sem["pool_passed"], 1)
                done(pool.tensor_tensor(a, offs, rm, ALU.mult))
                pool.sem_inc(sem["pool_passed"], 1)
                done(pool.tensor_scalar(a, a, MAGIC, -MAGIC, ALU.add, ALU.add))
                pool.sem_inc(sem["pool_passed"], 1)
                done(pool.tensor_tensor(a, a, m, ALU.mult))
                done(pool.tensor_tensor(a, offs, a, ALU.subtract))
                pool.sem_inc(sem["pool_passed"], 1)
                done(pool.tensor_tensor(b, a, m, ALU.mult))
                pool.sem_inc(sem["pool_passed"], 1)
                done(pool.tensor_scalar(b, b, 0.0, None, ALU.is_lt))
                pool.sem_inc(sem["pool_passed"], 1)
                done(pool.tensor_tensor(b, b, m, ALU.mult))
                done(pool.tensor_tensor(a, a, b, ALU.add))
                pool.sem_inc(sem["pool_passed"], 1)
                pool.tensor_scalar(pos, a, float(np.float32(S / (S - 1))), -0.5, ALU.mult, ALU.add).then_inc(
                    sem["positions_ready"], 1)

            def step(u, p):
                if on(u, 0):
                    narrow_expand(pool, 2, u, p)
                    positions(u)
                if on(u, 2):
                    t = u - 2
                    pool.wait_ge(sem["x_updated"], updates(ln_number_attn(2, t - 1)))
                    pool.sem_inc(sem["pool_passed"], 1)
                    pool.tensor_tensor(xb_sb[:], x_sb[:, bass.ds(t * D, D)], gbias_sb[:, 2 * D:3 * D],
                                       ALU.add).then_inc(sem["x_biased"], 1)
                if on(u, 3):
                    ln_pool(pool, ln_number_attn(2, u - 3), u - 3, 1)
                if on(u, 1):
                    t = u - 1
                    if positive(t - 1 + past(2, "values_projected")):
                        pool.wait_ge(sem["values_projected"], t - 1 + past(2, "values_projected"))
                    pool.tensor_copy(cdup[1 - p].rearrange("p (b c t) -> p b c t", b=2, c=2),
                                     ctx_sb[:, bass.ds(t * P, P)].rearrange("p (b t) -> p b t", b=2).unsqueeze(
                                         2).broadcast_to([P, 2, 2, S])).then_inc(sem["cdup_staged"], 1)
                    pool.wait_ge(sem["weights_ready"], u + past(2, "weights_ready"))
                    weight(pool, 1 - p, 0, PAIRS_POOL).then_inc(sem["hat_weighted_pool"], 1)
            steps(pool, 3, step)

        def distances(dve):
            dve.wait_ge(sem["kpos_loaded"], 32)
            dve.wait_ge(sem["maskq_loaded"], 16)
            dve.wait_ge(sem["qpos_loaded"], 16)
            keys, masked = xn_sb[:, 0:NT * S], xn_sb[:, NT * S:]
            dve.tensor_scalar(masked, masked.bitcast(I32), 0.0, -3.0e38, ALU.is_equal, ALU.mult).then_inc(
                sem["dist_steps"], 1)
            dve.tensor_tensor(keys.rearrange("p (n t) -> p n t", t=S),
                               keys.bitcast(I32).rearrange("p (n t) -> p n t", t=S),
                               qpos_sb[:].unsqueeze(2).broadcast_to([P, NT, S]), ALU.subtract).then_inc(
                sem["dist_steps"], 1)
            dve.wait_ge(sem["dist_steps"], 1)
            dve.tensor_scalar(masked, masked, 10.0, None, ALU.mult).then_inc(sem["dist_steps"], 1)
            dve.wait_ge(sem["dist_steps"], 3)
            dve.tensor_tensor(keys, keys, masked, ALU.add).then_inc(sem["dist_steps"], 1)
            dve.wait_ge(sem["dist_steps"], 4)

        JOB0 = {0: 0}
        Y0 = {0: 0}
        for f in FFNS:
            JOB0[f.layer + 1] = JOB0[f.layer] + f.jobs * NG + (4 * NG if f.layer == 0 else 0)
            Y0[f.layer + 1] = Y0[f.layer] + f.ys * NG
        gated_before = {0: 0, 1: 0, 2: FFNS[1].jobs * NG, 3: (FFNS[1].jobs + FFNS[2].jobs) * NG}
        plain_before = {0: 0, 1: JOB0[1], 2: JOB0[1], 3: JOB0[1]}
        bias_before = {0: 0, 3: NG}
        LT, TT = bank(6), bank(7)

        def slab_of(f):
            return slab1 if f.layer in (1, 3) else slab0

        def w_of(f, name):
            return view(slab_of(f), [WF0, WF1, WF2, WF3][f.layer], name)

        def hidden_bank(f, k):
            return (bank(2 * (k % 2)), bank(2 * (k % 2) + 1)) if f.gated else (bank(k % 4), None)

        def ring(f):
            return 2 if f.gated else 4

        def hidden_set_free(f, g, e):
            if isinstance(g, int) and g == 0 and e < f.sets:
                return Y0[f.layer]
            n = Y0[f.layer] + (1 if f.bias else 0) + e - f.sets + 1
            return g * f.ys + (n if e >= f.sets or not f.bias else n - 1)

        def ready_name(f):
            return "hidden_gated_ready" if f.gated else "hidden_relu_ready"

        def own(f, k):
            return (gated_before if f.gated else plain_before)[f.layer] + k

        def route_pe(pe, f):
            L = f.layer
            pe.wait_ge(sem[f"w{L}_loaded"], 16)
            pe.wait_ge(sem["xt_tile_ready"], (L + 1) * NT)
            with pe.Fori(0, NG) as g:
                G = g + L * NG
                if L == 0:
                    for c in range(4):
                        i = pe.matmul(bank(c), w_of(f, "rw1")[:, c * P:(c + 1) * P],
                                      xt_sb[:, bass.ds(g * GW, GW)], start=True, stop=True)
                        i.then_inc(sem["hidden_full"], 1)
                    for c in range(4):
                        pe.wait_ge(sem["hidden_relu_ready"], g * 4 + (c + 1))
                        i = pe.matmul(LT[0:E, :], w_of(f, "rw2")[:, c * E:(c + 1) * E], hid[c],
                                      start=c == 0, stop=c == 3)
                else:
                    i = pe.matmul(LT[0:E, :], w_of(f, "router"), xt_sb[:, bass.ds(g * GW, GW)], start=True, stop=True)
                i.then_inc(sem["logits_t_full"], 1)
                pe.wait_ge(sem["logits_t_ready"], G + 1)
                pe.sem_inc(sem["pe_passed"], 1)
                for u in range(GT):
                    i = pe.transpose(TT[:, u * E:(u + 1) * E], lgt[0:E, u * P:(u + 1) * P], ident[0:E, 0:E])
                i.then_inc(sem["logits_turned"], 1)
                pe.wait_ge(sem["logits_ready"], G + 1)
            if f.cap:
                n = 1 if L == 0 else 2
                pe.wait_ge(sem["mask_ready"], n)
                pe.matmul(LT[:, 0:NT * E], const("before"), rt[3], start=True, stop=True)
                pe.matmul(TT[:, 0:NT * E], const("ones"), rt[3], start=True, stop=True).then_inc(
                    sem["prefix_ready"], 1)

        def route_act(act, f):
            L = f.layer
            with act.Fori(0, NG) as g:
                G = g + L * NG
                if L == 0:
                    for c in range(4):
                        act.wait_ge(sem["hidden_full"], g * 4 + (c + 1))
                        act.activation(hid[c], bank(c), ACT.Relu, bias=col("rb1")[:, c:c + 1]).then_inc(
                            sem["hidden_relu_ready"], 1)
                act.wait_ge(sem["logits_t_full"], G + 1)
                if L in (0, 3):
                    act.activation(lgt[0:E, :], LT[0:E, :], ACT.Identity,
                                   bias=col("rb2" if L == 0 else "gb3")[0:E, :]).then_inc(sem["logits_t_ready"], 1)
                else:
                    act.activation(lgt[0:E, :], LT[0:E, :], ACT.Copy).then_inc(sem["logits_t_ready"], 1)
            if f.softmax:
                act.wait_ge(sem["route_steps"], ROUTE0[L] + 2)
                act.activation(rt[1], rt[1], ACT.Exp).then_inc(sem["route_exp_ready"], 1)
            if L == 1:
                act.wait_ge(sem["route_steps"], ROUTE0[L] + 1)
                act.activation(m1_sb[:], small[0], ACT.Sigmoid).then_inc(sem["gates_ready"], 1)

        ROUTE0 = {}

        def route_dve(dve, f):
            L = f.layer
            with dve.Fori(0, NG) as g:
                dve.wait_ge(sem["logits_turned"], g + (L * NG + 1))
                dve.tensor_copy(logit_sb[:, bass.ds(g * (GT * E), GT * E)], TT[:, 0:GT * E]).then_inc(
                    sem["logits_ready"], 1)
            dve.wait_ge(sem["logits_ready"], (L + 1) * NG)
            n = [ROUTE0[L]]

            def link(ins):
                ins.then_inc(sem["route_steps"], 1)
                n[0] += 1
                dve.wait_ge(sem["route_steps"], n[0])

            def v(a):
                return a.rearrange("p (t e) -> p t e", e=E)

            def wide(a):
                return a.unsqueeze(2).broadcast_to([P, NT, E])

            iota = const("iota8").unsqueeze(1).broadcast_to([P, NT, E])
            link(dve.tensor_reduce(small[0], v(logit_sb), AX.X, ALU.max))
            keys = logit_sb
            if f.softmax:
                link(dve.tensor_tensor(v(rt[1]), v(logit_sb), wide(small[0]), ALU.subtract))
                dve.wait_ge(sem["route_exp_ready"], 1 if L == 0 else 2)
                if f.softmax == "all":
                    link(dve.tensor_reduce(small[1], v(rt[1]), AX.X, ALU.add))
                    link(dve.reciprocal(small[2], small[1]))
                    link(dve.tensor_tensor(v(rt[1]), v(rt[1]), wide(small[2]), ALU.mult))
                    keys = rt[1]
                    link(dve.tensor_reduce(small[0], v(keys), AX.X, ALU.max))

            def one_hot(dst, values):
                link(dve.tensor_tensor(v(rt[4]), v(values), wide(small[0]), ALU.is_lt))
                link(dve.scalar_tensor_tensor(v(rt[5]), v(rt[4]), BIG, iota, ALU.mult, ALU.add))
                link(dve.tensor_reduce(small[1], v(rt[5]), AX.X, ALU.min))
                link(dve.tensor_tensor(v(dst), iota, wide(small[1]), ALU.is_equal))

            one_hot(rt[2], keys)
            chosen = rt[2]
            if f.topk == 2:
                link(dve.scalar_tensor_tensor(v(rt[6]), v(rt[2]), -3.0e38, v(keys), ALU.mult, ALU.add))
                link(dve.tensor_reduce(small[0], v(rt[6]), AX.X, ALU.max))
                one_hot(rt[7], rt[6])
                dve.tensor_tensor(rt[3], rt[2], rt[7], ALU.add).then_inc(sem["mask_ready"], 1)
                dve.wait_ge(sem["mask_ready"], 1 if L == 0 else 2)
                chosen = rt[3]
            if not f.softmax:
                dve.tensor_copy(comb_sb[:], chosen).then_inc(sem["comb_ready"], 1)
                return
            link(dve.tensor_tensor(rt[4], rt[1], rt[3], ALU.mult))
            link(dve.tensor_reduce(small[1], v(rt[4]), AX.X, ALU.add))
            if f.softmax == "all":
                link(dve.tensor_scalar(small[1], small[1], 1e-20, None, ALU.add))
            link(dve.reciprocal(small[2], small[1]))
            link(dve.tensor_tensor(v(rt[4]), v(rt[4]), wide(small[2]), ALU.mult))
            dve.wait_ge(sem["prefix_ready"], 1 if L == 0 else 2)
            link(dve.memset(rt[5][:, 0:E], 0.0))
            link(dve.tensor_copy(rt[5][:, E:], TT[:, 0:(NT - 1) * E]))
            a, b, s = rt[5], rt[6], 1
            while s < NT:
                link(dve.tensor_tensor(b[:, s * E:], a[:, s * E:], a[:, :(NT - s) * E], ALU.add))
                link(dve.tensor_copy(b[:, :s * E], a[:, :s * E]))
                a, b, s = b, a, 2 * s
            link(dve.tensor_tensor(a, a, LT[:, 0:NT * E], ALU.add))
            link(dve.tensor_scalar(a, a, float(f.cap), None, ALU.is_lt))
            dve.tensor_tensor(comb_sb[:], rt[4], a, ALU.mult).then_inc(sem["comb_ready"], 1)

        def count_route(f):
            n = 1 + 4
            if f.softmax:
                n += 1 + (4 if f.softmax == "all" else 0)
            if f.topk == 2:
                n += 2 + 4
            if f.softmax:
                n += 4 + (1 if f.softmax == "all" else 0) + 2 + 10 + 2
            return n

        total = 0
        for f in FFNS:
            ROUTE0[f.layer] = total
            total += count_route(f)

        def groups(eng, body):
            body(0)
            with eng.Fori(1, NG) as g:
                body(g)

        def ffn_pe(pe, f):
            L, nc_, J = f.layer, len(f.chunks), f.jobs
            k0 = 4 * NG if L == 0 else 0
            src_full = JOB0[L] + k0

            def turn(g):
                pe.wait_ge(sem["xt_group_ready"], g * GT + (L + 1) * NT)
                ln_pe(pe, ln_number_ffn(L, g), LT, GT)

            def body(g):
                G = g + L * NG
                y = [0]

                def y_slot():
                    n = g * f.ys + (Y0[L] + y[0])
                    if positive(n if y[0] == 0 else n - 1):
                        pe.wait_ge(sem["expert_added"], n if y[0] == 0 else n - 1)
                    k = y[0]
                    y[0] += 1
                    return k

                def first(e):
                    for c, (c0_, w) in enumerate(f.chunks):
                        j = e * nc_ + c
                        a, b = hidden_bank(f, j)
                        back = ring(f) if j >= ring(f) or J % ring(f) == 0 else 1
                        if positive(g * J + (own(f, k0 + j) - back + 1)):
                            pe.wait_ge(sem[ready_name(f)], g * J + (own(f, k0 + j) - back + 1))
                        rhs = xgt if (L == 1 and e < E) else xt_sb[:, bass.ds(g * GW, GW)]
                        fw = F1 if L == 1 else (P if L == 2 else 512)
                        i = pe.matmul(a[0:w, :], w_of(f, "w1")[:, e * fw + c0_:e * fw + c0_ + w], rhs,
                                      start=True, stop=True)
                        if f.gated:
                            i = pe.matmul(b[0:w, :], w_of(f, "w3")[:, e * fw + c0_:e * fw + c0_ + w], rhs,
                                          start=True, stop=True)
                        i.then_inc(sem["hidden_full"], 1)

                def second(e):
                    k = y_slot()
                    yb = bank(4 + k % 2)
                    pe.wait_ge(sem[ready_name(f)], g * J + own(f, k0 + (e + 1) * nc_))
                    for u in range(GT):
                        for c, (_, w) in enumerate(f.chunks):
                            i = pe.matmul(yb[:, u * P:(u + 1) * P],
                                          hid[(e % f.sets) * nc_ + c][0:w, u * P:(u + 1) * P],
                                          w_of(f, "w2")[0:w, (e * nc_ + c) * D:(e * nc_ + c + 1) * D],
                                          start=c == 0, stop=c == nc_ - 1)
                    i.then_inc(sem["expert_summed"], 1)

                if f.bias:
                    n = g + bias_before[L]
                    pe.wait_ge(sem["comb_staged"], G + 1)
                    for u in range(GT):
                        i = pe.transpose(TT[0:E, u * P:(u + 1) * P], combs[:, u * E:(u + 1) * E], ident)
                    i.then_inc(sem["comb_turned"], 1)
                    pe.wait_ge(sem["comb_t_ready"], n + 1)
                    k = y_slot()
                    for u in range(GT):
                        i = pe.matmul(bank(4 + k % 2)[:, u * P:(u + 1) * P], cbt[0:E, u * P:(u + 1) * P],
                                      col(f.bias)[0:E, :], start=True, stop=True)
                    i.then_inc(sem["expert_summed"], 1)
                if L == 1:
                    pe.wait_ge(sem["xg_ready"], g + 1)
                    for u in range(GT):
                        i = pe.transpose(TT[:, u * P:(u + 1) * P], xg[:, u * P:(u + 1) * P], ident)
                    i.then_inc(sem["xg_turned"], 1)
                    pe.wait_ge(sem["xg_t_ready"], g + 1)
                order = list(range(f.experts))
                for m, e in enumerate(order):
                    first(e)
                    if m:
                        second(order[m - 1])
                    if m == 2 and L != 3 and not (isinstance(g, int) and g == 0):
                        turn(g - 1)
                second(order[-1])

            groups(pe, body)
            if L != 3:
                turn(NG - 1)

        def ffn_act(act, f):
            L, nc_, J = f.layer, len(f.chunks), f.jobs
            k0 = 4 * NG if L == 0 else 0
            full0 = JOB0[L] + k0

            def body(g):
                G = g + L * NG
                if f.bias:
                    n = g + bias_before[L]
                    act.wait_ge(sem["comb_turned"], n + 1)
                    act.activation(cbt[0:E, :], TT[0:E, :], ACT.Copy).then_inc(sem["comb_t_ready"], 1)
                if L == 1:
                    act.wait_ge(sem["xg_turned"], g + 1)
                    act.activation(xgt, TT, ACT.Copy).then_inc(sem["xg_t_ready"], 1)
                for e in range(f.experts):
                    for c, (_, w) in enumerate(f.chunks):
                        j = e * nc_ + c
                        a, b = hidden_bank(f, j)
                        act.wait_ge(sem["hidden_full"], g * J + (full0 + j + 1))
                        if f.gated:
                            if positive(g * J + (own(f, k0 + j) - (0 if j == 0 else 1))):
                                act.wait_ge(sem[ready_name(f)], g * J + (own(f, k0 + j) - (0 if j == 0 else 1)))
                            act.activation(gate[j % 2][0:w, :], a[0:w, :], ACT.Silu).then_inc(
                                sem["gate_silu_ready"], 1)
                        else:
                            if positive(hidden_set_free(f, g, e)):
                                act.wait_ge(sem["expert_summed"], hidden_set_free(f, g, e))
                            act.activation(hid[(e % f.sets) * nc_ + c][0:w, :], a[0:w, :], ACT.Relu,
                                           bias=col("eb1" if L == 0 else "b13")[:, e * 4 + c:e * 4 + c + 1]).then_inc(
                                sem["hidden_relu_ready"], 1)
                    if e == 2 and not (isinstance(g, int) and g == 0) and L != 3:
                        ln_act(act, ln_number_ffn(L, g - 1), LT, (g - 1) * GT, GT)

            groups(act, body)
            if L != 3:
                ln_act(act, ln_number_ffn(L, NG - 1), LT, (NG - 1) * GT, GT)

        def ffn_dve(dve, f):
            L, nc_, J = f.layer, len(f.chunks), f.jobs
            k0 = 4 * NG if L == 0 else 0

            def body(g):
                G = g + L * NG
                y = [0]
                dve.wait_ge(sem["comb_ready"], L + 1)
                if f.bias:
                    if positive(g + bias_before[L]):
                        dve.wait_ge(sem["comb_turned"], g + bias_before[L])
                dve.tensor_copy(combs[:], comb_sb[:, bass.ds(g * (GT * E), GT * E)]).then_inc(sem["comb_staged"], 1)
                dve.wait_ge(sem["comb_staged"], G + 1)

                def mult(e):
                    for c, (_, w) in enumerate(f.chunks):
                        j = e * nc_ + c
                        _, b = hidden_bank(f, j)
                        dve.wait_ge(sem["gate_silu_ready"], g * J + (own(f, k0 + j) + 1))
                        dve.wait_ge(sem["expert_summed"], hidden_set_free(f, g, e))
                        dve.tensor_tensor(hid[(e % f.sets) * nc_ + c][0:w, :], gate[j % 2][0:w, :], b[0:w, :],
                                          ALU.mult).then_inc(sem["hidden_gated_ready"], 1)

                def add(e):
                    n = g * f.ys + (Y0[L] + y[0])
                    yb = bank(4 + y[0] % 2)
                    dve.wait_ge(sem["expert_summed"], n + 1)
                    if positive(n):
                        dve.wait_ge(sem["expert_added"], n)
                    if e is None:
                        dve.tensor_copy(acc, yb).then_inc(sem["expert_added"], 1)
                    else:
                        for u in range(GT):
                            a, yy = acc[:, u * P:(u + 1) * P], yb[:, u * P:(u + 1) * P]
                            w = combs[:, u * E + e:u * E + e + 1] if e < E else 1.0
                            if y[0] == 0:
                                i = dve.tensor_scalar(a, yy, w, None, ALU.mult)
                            else:
                                i = dve.scalar_tensor_tensor(a, yy, w, a, ALU.mult, ALU.add)
                        i.then_inc(sem["expert_added"], 1)
                    y[0] += 1

                if f.bias:
                    add(None)
                for e in range(f.experts):
                    if f.gated:
                        mult(e)
                    if e:
                        add(e - 1)
                add(f.experts - 1)
                dve.wait_ge(sem["expert_added"], (g + 1) * f.ys + Y0[L])
                xs = x_tiles(g * GT, GT)
                dve.scalar_tensor_tensor(xs, acc, gain_sb[:, 4 + L:5 + L], xs, ALU.mult, ALU.add).then_inc(
                    sem["x_updated"], 1)
                if L != 3:
                    ln_dve(dve, ln_number_ffn(L, g), g * GT, GT)

            groups(dve, body)
            if L == 2:
                distances(dve)

        def ffn_pool(pool, f):
            L = f.layer

            def body(g):
                if L == 1:
                    pool.wait_ge(sem["gates_ready"], 1)
                    if positive(g):
                        pool.wait_ge(sem["xg_turned"], g)
                    pool.sem_inc(sem["pool_passed"], 1)
                    pool.tensor_tensor(xg.rearrange("p (w d) -> p w d", d=D),
                                       xn_sb[:, bass.ds(g * GW, GW)].rearrange("p (w d) -> p w d", d=D),
                                       m1_sb[:, bass.ds(g * GT, GT)].unsqueeze(2).broadcast_to([P, GT, D]),
                                       ALU.mult).then_inc(sem["xg_ready"], 1)
                if L != 3:
                    ln_pool(pool, ln_number_ffn(L, g), g * GT, GT)

            if L != 3:
                groups(pool, body)

        def setup_act(act):
            act.wait_ge(sem["rows_loaded"], 16)
            act.activation(gain_sb[:], row("g"), ACT.Tanh).then_inc(sem["gains_ready"], 1)

        def setup_dve(dve):
            dve.wait_ge(sem["gains_ready"], 1)
            for k, name in enumerate(("bu0", "bo1", "bo2")):
                i = dve.tensor_scalar(gbias_sb[:, k * D:(k + 1) * D], row(name), gain_sb[:, k:k + 1], None, ALU.mult)
            i.then_inc(sem["bias_ready"], 1)

        def setup_lens(dve):
            dve.wait_ge(sem["mask2_loaded"], 32)
            dve.tensor_reduce(lens_sb[:], xn_sb[:, 0:NT * S].bitcast(I32).rearrange("p (n t) -> p n t", t=S), AX.X,
                              ALU.add).then_inc(sem["setup_steps"], 1)
            dve.wait_ge(sem["setup_steps"], 1)
            dve.tensor_scalar(lens_sb[:], lens_sb[:], -1.0, float(S - 1), ALU.mult, ALU.add).then_inc(
                sem["setup_steps"], 1)
            dve.wait_ge(sem["setup_steps"], 2)
            dve.reciprocal(rlens_sb[:], lens_sb[:]).then_inc(sem["lens_ready"], 1)

        ATT_PE = {1: a13_pe(1), 2: a2_pe, 3: a13_pe(3)}
        ATT_ACT = {1: a13_act(1), 2: a2_act, 3: a13_act(3)}
        ATT_DVE = {1: a13_dve(1), 2: a2_dve, 3: a13_dve(3)}
        ATT_POOL = {1: a13_pool(1), 2: a2_pool, 3: a13_pool(3)}
        block = stack.enter_context(nc.Block())

        @block.sync
        def _(sp):
            for dst, src, name in ((x_sb, x_in, "x_loaded"), (const_sb, consts_in, "consts_loaded"),
                                   (slab1[:, 0:NWA0], wa0, "wa0_loaded"), (ctx_sb, ctx_t, "ctx_loaded"),
                                   (cols_sb, cols_in, "cols_loaded"), (slab0[:, 0:NWF0], wf0, "w0_loaded"),
                                   (wsa_sb, wsa, "wsa_loaded")):
                sp.dma_start(dst[:], src).then_inc(sem[name], 16)
            mask2b = mask2.rearrange("(n b) t -> b n t", b=2)
            for b, r in enumerate(halves()):
                sp.dma_start(xn_sb[r, 0:NT * S].bitcast(I32).rearrange("p (n t) -> p n t", t=S),
                             mask2b[b].unsqueeze(0).broadcast_to([64, NT, S])).then_inc(sem["mask2_loaded"], 16)
            sp.dma_start(qpos_sb[:], qpos).then_inc(sem["qpos_loaded"], 16)
            if stop_after >= 2:
                sp.wait_ge(sem["xt_tile_ready"], NT)
                sp.dma_start(slab1[:, 0:NWF1], wf1).then_inc(sem["w1_loaded"], 16)
            if stop_after > 3:
                sp.wait_ge(sem["xt_group_ready"], 2 * NT)
                sp.dma_start(slab0[:, 0:NWF2], wf2).then_inc(sem["w2_loaded"], 16)
            if stop_after > 5:
                sp.wait_ge(sem["xt_tile_ready"], 3 * NT)
                kposb = kpos.rearrange("(n b) t -> b n t", b=2)
                for b, r in enumerate(halves()):
                    sp.dma_start(xn_sb[r, 0:NT * S].bitcast(I32).rearrange("p (n t) -> p n t", t=S),
                                 kposb[b].unsqueeze(0).broadcast_to([64, NT, S])).then_inc(sem["kpos_loaded"], 16)
                sp.dma_start(xn_sb[:, NT * S:].bitcast(I32), maskq).then_inc(sem["maskq_loaded"], 16)
                sp.dma_start(slab1[:, 0:NWF3], wf3).then_inc(sem["w3_loaded"], 16)
            base = updates(ln_number_ffn(3, 0)) if stop_after == 8 else None
            if base:
                with sp.Fori(0, NG) as g:
                    sp.wait_ge(sem["x_updated"], g + base)
                    sp.dma_start(out[:, bass.ds(g * GW, GW)], x_sb[:, bass.ds(g * GW, GW)]).then_inc(
                        sem["stored"], 16)
                sp.wait_ge(sem["stored"], 16 * NG)
            else:
                n = updates(ln_number_attn(stop_after // 2, NT - 1) if stop_after % 2 else
                            ln_number_ffn(stop_after // 2 - 1, NG - 1)) if stop_after else 0
                sp.wait_ge(sem["x_updated"], n)
                sp.dma_start(out, x_sb[:]).then_inc(sem["stored"], 16)
                sp.wait_ge(sem["stored"], 16)

        @block.tensor
        def _(pe):
            pe.wait_ge(sem["consts_loaded"], 16)

            def first(g):
                if positive(g * GT):
                    pe.wait_ge(sem["xt_group_ready"], g * GT)
                ln_pe(pe, g, bank(7), GT)
            groups(pe, first)
            pe.wait_ge(sem["xt_group_ready"], NT)
            if stop_after > 0:
                a0_pe(pe)
            for f in FFNS:
                if f.layer:
                    if stop_after > 2 * f.layer:
                        ATT_PE[f.layer](pe)
                if stop_after > 2 * f.layer + 1:
                    route_pe(pe, f)
                    ffn_pe(pe, f)

        @block.scalar
        def _(act):
            act.dma_start(rows_sb[:], rows_in.broadcast_to([P, NROWS])).then_inc(sem["rows_loaded"], 16)
            setup_act(act)
            groups(act, lambda g: ln_act(act, g, bank(7), g * GT, GT))
            act.wait_ge(sem["cols_loaded"], 16)
            if stop_after > 0:
                a0_act(act)
            for f in FFNS:
                if f.layer:
                    if stop_after > 2 * f.layer:
                        ATT_ACT[f.layer](act)
                if stop_after > 2 * f.layer + 1:
                    route_act(act, f)
                    ffn_act(act, f)

        @block.vector
        def _(dve):
            setup_dve(dve)
            dve.wait_ge(sem["x_loaded"], 16)
            groups(dve, lambda g: ln_dve(dve, g, g * GT, GT, True))
            dve.wait_ge(sem["cols_loaded"], 16)
            dve.wait_ge(sem["consts_loaded"], 16)
            if stop_after > 0:
                a0_dve(dve)
                setup_lens(dve)
            for f in FFNS:
                if f.layer:
                    if stop_after > 2 * f.layer:
                        ATT_DVE[f.layer](dve)
                if stop_after > 2 * f.layer + 1:
                    route_dve(dve, f)
                    ffn_dve(dve, f)

        @block.gpsimd
        def _(pool):
            pool.wait_ge(sem["x_loaded"], 16)
            groups(pool, lambda g: ln_pool(pool, g, g * GT, GT))
            pool.wait_ge(sem["bias_ready"], 1)
            pool.wait_ge(sem["ctx_loaded"], 16)
            if stop_after > 0:
                a0_pool(pool)
            for f in FFNS:
                if f.layer:
                    if stop_after > 2 * f.layer:
                        ATT_POOL[f.layer](pool)
                if stop_after > 2 * f.layer + 1:
                    ffn_pool(pool, f)


def arrays_of(inputs):
    f = {k: np.asarray(v) for k, v in inputs.items()}

    def fill(table, width, **fields):
        a = np.zeros((P, width), np.float32)
        for name, v in fields.items():
            lo, hi = table[name]
            v = v.reshape(v.shape[0], -1)
            assert v.shape[1] == hi - lo, (name, v.shape, hi - lo)
            a[:v.shape[0], lo:hi] = v
        return a

    def tokens(a):
        return np.ascontiguousarray(a.reshape(NT, P, -1).transpose(1, 0, 2).reshape(P, -1))

    def chunks(a):
        return a.reshape(-1, P, a.shape[-1]).transpose(1, 0, 2)

    def experts(a):
        return a.transpose(1, 0, 2)

    def hidden(a):
        return a.reshape(a.shape[0], -1, P, a.shape[-1]).transpose(2, 0, 1, 3)

    def padded(a):
        z = np.zeros((a.shape[0], 3 * P, D), np.float32)
        z[:, :F1] = a
        return z

    i, j = np.arange(P)[:, None], np.arange(P)[None, :]
    consts = fill(CONST, NCONST, ident=(i == j), before=(i < j), ones=np.ones((P, P)),
                  iota8=np.tile(np.arange(E), (P, 1)), iota64=np.tile(np.arange(S), (P, 1)),
                  slopes=np.tile(np.float32(2.0 ** -0.5) ** np.arange(1, H + 1), (P, 1)),
                  headmask=(i % 32 // HD == np.arange(4)[None]),
                  refloc=np.tile((i % S + np.arange(-3, 2)[None]), (1, H)))
    rows = np.concatenate([f["L0_xattn_bv"], f["L0_xattn_bu"], f["L1_xattn_b_v"], f["L1_xattn_b_o"],
                           f["L2_xattn_bv"], f["L2_xattn_boff"], f["L2_xattn_bo"], f["g_xattn"], f["g_ffn"]])[None]
    cols = fill(COLS, NCOLS, bq0=f["L0_xattn_bq"].reshape(8, P).T, bk0=f["L0_xattn_bk"].reshape(8, P).T,
                bq1=f["L1_xattn_b_q"][:, None], bk1=f["L1_xattn_b_k"][:, None], bq2=f["L2_xattn_bq"][:, None],
                bk2=f["L2_xattn_bk"][:, None], rb1=f["L0_ffn_rb1"].reshape(4, P).T, rb2=f["L0_ffn_rb2"][:, None],
                eb1=f["L0_ffn_eb1"].reshape(E * 4, P).T, gb3=f["L3_ffn_gate_b"][:, None],
                b13=f["L3_ffn_b1"].reshape(E * 4, P).T, eb2=f["L0_ffn_eb2"], b23=f["L3_ffn_b2"])
    shared_g = f["L2_ffn_ws_gate"].reshape(2, P, D)
    shared_u = f["L2_ffn_ws_up"].reshape(2, P, D)
    shared_d = f["L2_ffn_ws_down"].reshape(D, 2, P).transpose(1, 0, 2)

    def swap(a):
        return a.transpose(0, 2, 1)

    return {
        "x": tokens(f["x"].reshape(B * S, D)),
        "ctx_t": np.ascontiguousarray(f["ctx_1024"].reshape(B * S, D).T),
        "wa0": fill(WA0, NWA0, q=f["L0_xattn_Wq"], k=f["L0_xattn_Wk"], v=f["L0_xattn_Wv"], u=chunks(f["L0_xattn_Wu"])),
        "wsa": fill(WSA, NWSA, q1=f["L1_xattn_w_q"].T, k1=f["L1_xattn_w_k"].T, v1=f["L1_xattn_w_v"].T,
                    o1=f["L1_xattn_w_o"].T, q2=f["L2_xattn_Wq"].T, k2=f["L2_xattn_Wk"].T, v2=f["L2_xattn_Wv"].T,
                    off2=f["L2_xattn_Woff"].T, o2=f["L2_xattn_Wo"].T, q3=f["L3_xattn_W_q"].T,
                    k3=f["L3_xattn_W_k"].T, v3=f["L3_xattn_W_v"].T, o3=f["L3_xattn_W_o"].T),
        "wf0": fill(WF0, NWF0, rw1=f["L0_ffn_rw1"], rw2=chunks(f["L0_ffn_rw2"]), w1=experts(f["L0_ffn_ew1"]),
                    w2=hidden(f["L0_ffn_ew2"])),
        "wf1": fill(WF1, NWF1, router=f["L1_ffn_router_DE"],
                    w1=experts(np.concatenate([f["L1_ffn_w1_eDF"], f["L1_ffn_ws1_DF"][None]])),
                    w3=experts(np.concatenate([f["L1_ffn_w3_eDF"], f["L1_ffn_ws3_DF"][None]])),
                    w2=hidden(padded(np.concatenate([f["L1_ffn_w2_eFD"], f["L1_ffn_ws2_FD"][None]])))),
        "wf2": fill(WF2, NWF2, router=f["L2_ffn_gate_w"].T,
                    w1=experts(swap(np.concatenate([f["L2_ffn_we_gate"], shared_g]))),
                    w3=experts(swap(np.concatenate([f["L2_ffn_we_up"], shared_u]))),
                    w2=experts(swap(np.concatenate([f["L2_ffn_we_down"], shared_d])))),
        "wf3": fill(WF3, NWF3, router=f["L3_ffn_gate_w"].T, w1=experts(swap(f["L3_ffn_w1"])),
                    w2=hidden(swap(f["L3_ffn_w2"]))),
        "rows": rows, "cols": cols, "consts": consts,
        "mask2": f["mask_BxS2_if0"], "qpos": tokens(f["itok_BxS_8_8191"].reshape(B * S, 1)),
        "kpos": f["itok_BxS2_1_8191"], "maskq": tokens(f["mask_BxSxS2_if1"].reshape(B * S, S)),
    }


def kernel(**inputs):
    import concourse.bacc as bacc
    from concourse.bass_utils import run_bass_kernel_spmd

    nc = bacc.Bacc("TRN2", target_bir_lowering=False, num_devices=1)
    arrays = {f"in_{k}": np.ascontiguousarray(v) for k, v in arrays_of(inputs).items()}
    args = [nc.dram_tensor(k, v.shape, mybir.dt.from_np(v.dtype), kind="ExternalInput").ap() for k, v in arrays.items()]
    out = nc.dram_tensor("out", (P, NT * D), F32, kind="ExternalOutput").ap()
    flamingo(nc, *args, out)
    got = run_bass_kernel_spmd(nc, [arrays], core_ids=[0]).results[0]["out"]
    return np.ascontiguousarray(got.reshape(P, NT, D).transpose(1, 0, 2)).reshape(B, S, D)
```

```python
from contextlib import ExitStack

import numpy as np
import concourse.bass as bass
from concourse import mybir

ALU = mybir.AluOpType
ACT = mybir.ActivationFunctionType
AX = mybir.AxisListType
F32 = mybir.dt.float32
I32 = mybir.dt.int32

P = 128
B, S, D = 64, 64, 128
NT = B * S // P
GT = 4
NG = NT // GT
GW = GT * P
H = 16
HP = H // 2
HD0 = 64
HD = 8
NK = 5
E = 8
CAP0, CAP2 = 512, 1280
F1 = 352
F1C = [(0, 128), (128, 128), (256, 96)]
EPS = 1e-5
MAGIC = 12582912.0
BIG = 1000.0


def layout(*fields):
    at, n = {}, 0
    for name, width in fields:
        at[name] = (n, n + width)
        n += width
    return at, n


CONST, NCONST = layout(("ident", P), ("before", P), ("ones", P), ("iota8", E), ("iota64", S),
                       ("slopes", H), ("headmask", 4), ("refloc", H * NK))
ROWS, NROWS = layout(("bv0", 1024), ("bu0", D), ("bv1", D), ("bo1", D), ("bv2", D), ("boff", H * NK),
                     ("bo2", D), ("g", 8))
COLS, NCOLS = layout(("bq0", 8), ("bk0", 8), ("bq1", 1), ("bk1", 1), ("bq2", 1), ("bk2", 1), ("rb1", 4),
                     ("rb2", 1), ("eb1", E * 4), ("gb3", 1), ("b13", E * 4), ("eb2", D), ("b23", D))
WA0, NWA0 = layout(("q", 1024), ("k", 1024), ("v", 1024), ("u", 1024))
WSA, NWSA = layout(("q1", D), ("k1", D), ("v1", D), ("o1", D), ("q2", D), ("k2", D), ("v2", D),
                   ("off2", H * NK), ("o2", D), ("q3", D), ("k3", D), ("v3", D), ("o3", D))
WF0, NWF0 = layout(("rw1", 512), ("rw2", 4 * E), ("w1", E * 512), ("w2", E * 512))
WF1, NWF1 = layout(("router", E), ("w1", 9 * F1), ("w3", 9 * F1), ("w2", 9 * 3 * D))
WF2, NWF2 = layout(("router", E), ("w1", 10 * D), ("w3", 10 * D), ("w2", 10 * D))
WF3, NWF3 = layout(("router", E), ("w1", E * 512), ("w2", E * 512))
SLAB0 = max(NWF0, NWF2 + H * NK * S)
SLAB1 = max(NWA0, NWF1, NWF3, 2 * H * NK * S)


class Ffn:

    def __init__(self, layer, experts, chunks, gated, sets, cap, softmax, topk, shared, bias):
        self.layer, self.experts, self.chunks, self.gated = layer, experts, chunks, gated
        self.sets, self.cap, self.softmax, self.topk = sets, cap, softmax, topk
        self.shared, self.bias = shared, bias
        self.jobs = experts * len(chunks)
        self.ys = experts + (1 if bias else 0)


FFNS = [
    Ffn(0, 8, [(128 * c, 128) for c in range(4)], False, 2, CAP0, "top", 2, 0, "eb2"),
    Ffn(1, 9, F1C, True, 3, None, None, 1, 1, None),
    Ffn(2, 10, [(0, 128)], True, 2, CAP2, "all", 2, 2, None),
    Ffn(3, 8, [(128 * c, 128) for c in range(4)], False, 2, None, None, 1, 0, "b23"),
]

SEMAPHORES = """x_loaded ctx_loaded wa0_loaded wsa_loaded rows_loaded cols_loaded consts_loaded
w0_loaded w1_loaded w2_loaded w3_loaded mask2_loaded qpos_loaded kpos_loaded maskq_loaded stored
gains_ready bias_ready lens_ready setup_steps route_exp_ready gates_ready
x_updated ln_stats_done ln_aggr_done ln_shifted ln_guessed newton_steps xn_centred xn_ready xn_turned xt_group_ready xt_tile_ready
ctx_staged q_projected k_projected v_projected q_ready k_ready v_ready kexp_ready scores_ready scores_copied
row_max_ready scores_centred exp_ready exp_sum_ready exp_recip_ready probs_ready probs_turned probs_t_ready
heads_summed heads_ready heads_scaled qs_ready ks_ready vs_projected cdup_staged vm_ready sum_plus_one heads_turned heads_t_ready out_projected x_biased
attention_zeroed dist_ready dist_steps bias_scaled biased_ready
qk_projected values_projected offsets_projected offsets_ready position_steps positions_ready distance_ready hat_abs_ready half_hat_ready
sampled_half sampled_max sampled_centred sampled_exp sampled_sum sampled_recip weights_ready hat_weighted_pool
hat_weighted_dve product_ready base_ready
hidden_full gate_silu_ready hidden_relu_ready hidden_gated_ready expert_summed expert_added
logits_t_full logits_t_ready logits_turned logits_ready comb_staged comb_turned comb_t_ready
route_steps mask_ready prefix_ready comb_ready xg_ready xg_turned xg_t_ready pe_passed dve_passed pool_passed""".split()


def flamingo(nc, x_in, ctx_t, wa0, wsa, wf0, wf1, wf2, wf3, rows_in, cols_in, consts_in, mask2, qpos, kpos, maskq,
             out, stop_after=8):
    with ExitStack() as stack:
        def sb(name, width, dt=F32):
            return stack.enter_context(nc.sbuf_tensor(name, [P, width], dt))

        sem = {n: stack.enter_context(nc.semaphore(n)) for n in SEMAPHORES}

        x_sb = sb("x_sb", NT * D)
        xt_sb = sb("xt_sb", NT * P)
        ctx_sb = sb("ctx_sb", NT * P)
        xn_sb = sb("xn_sb", NT * D)
        slab0 = sb("slab0", SLAB0)
        slab1 = sb("slab1", SLAB1)
        wsa_sb = sb("wsa_sb", NWSA)
        rows_sb = sb("rows_sb", NROWS)
        cols_sb = sb("cols_sb", NCOLS)
        const_sb = sb("const_sb", NCONST)
        gain_sb = sb("gain_sb", 8)
        gbias_sb = sb("gbias_sb", 3 * D)
        stats_sb = sb("stats_sb", GT * 6)
        moments_sb = sb("moments_sb", GT * 2)
        shift_sb = sb("shift_sb", GT, I32)
        rstd_sb = sb("rstd_sb", GT)
        newt_sb = sb("newt_sb", GT)
        xns_sb = sb("xns_sb", GW)
        comb_sb = sb("comb_sb", NT * E)
        m1_sb = sb("m1_sb", NT)
        rs_sb = sb("rs_sb", 4 * H)
        lens_sb = sb("lens_sb", NT)
        rlens_sb = sb("rlens_sb", NT)
        qpos_sb = sb("qpos_sb", NT, I32)
        xb_sb = sb("xb_sb", D)
        arena = sb("arena", 10700)
        ps = stack.enter_context(nc.psum_tensor("ps", [P, 4096], F32))

        def view(t, table, name):
            a, b = table[name]
            return t[:, a:b]

        def const(name):
            return view(const_sb, CONST, name)

        def row(name):
            return view(rows_sb, ROWS, name)

        def col(name):
            return view(cols_sb, COLS, name)

        ident = const("ident")

        def bank(n, a=0, b=512):
            return ps[:, 512 * n + a:512 * n + b]

        used = [0]

        def cut(width):
            used[0] += width
            assert used[0] <= 10700
            return arena[:, used[0] - width:used[0]]

        qt0 = [cut(1024) for _ in range(2)]
        kt0 = [cut(1024) for _ in range(2)]
        v0 = [cut(1024) for _ in range(2)]
        e0 = [cut(1024) for _ in range(2)]
        pt0, ot0 = cut(1024), cut(1024)
        c0 = [cut(P) for _ in range(2)]
        used[0] = 0
        qt = [cut(P) for _ in range(2)]
        kt = [cut(P) for _ in range(2)]
        kexp = [cut(512) for _ in range(2)]
        cdup = [cut(4 * S) for _ in range(2)]
        vm = [cut(HP * 32) for _ in range(2)]
        ex = [cut(1024) for _ in range(2)]
        pt, ob, obt = cut(1024), cut(P), cut(P)
        prod = [cut(1024) for _ in range(2)]
        o80 = [cut(H * NK) for _ in range(9)]
        used[0] = 0
        hid = [cut(512) for _ in range(9)]
        gate = [cut(512) for _ in range(2)]
        acc, xg, xgt, lgt, cbt = cut(512), cut(512), cut(512), cut(512), cut(512)
        combs = cut(GT * E)
        rt = [cut(NT * E) for _ in range(8)]
        logit_sb = cut(NT * E)
        small = [cut(NT) for _ in range(3)]

        hat = [slab1[:, 0:5120], slab1[:, 5120:10240]]
        hprod = slab0[:, NWF2:NWF2 + 5120]

        def positive(value):
            return not isinstance(value, int) or value > 0


        def x_tiles(t, w):
            return x_sb[:, bass.ds(t * D, w * D)]

        def ln_dve(dve, n, t, w, first=False):
            if isinstance(n, int) and n < NG or first:
                dve.wait_ge(sem["x_loaded"], 16)
            else:
                dve.wait_ge(sem["x_updated"], n - NG + 1)
            if positive(n):
                dve.wait_ge(sem["xn_ready"], n)
            dve.sem_inc(sem["dve_passed"], 1)
            for u in range(w):
                i = dve.bn_stats(stats_sb[:, 6 * u:6 * u + 6], x_sb[:, bass.ds((t + u) * D, D)])
            i.then_inc(sem["ln_stats_done"], 1)
            dve.wait_ge(sem["ln_stats_done"], n + 1)
            dve.sem_inc(sem["dve_passed"], 1)
            for u in range(w):
                i = dve.bn_aggr(moments_sb[:, 2 * u:2 * u + 2], stats_sb[:, 6 * u:6 * u + 6])
            i.then_inc(sem["ln_aggr_done"], 1)
            dve.wait_ge(sem["ln_aggr_done"], n + 1)
            var = moments_sb[:, 0:2 * w].rearrange("p (w c) -> p w c", c=2)[:, :, 1]
            dve.tensor_scalar(newt_sb[:, 0:w], var, EPS, None, ALU.add).then_inc(sem["ln_shifted"], 1)
            dve.wait_ge(sem["ln_shifted"], 2 * n + 1)
            dve.tensor_scalar(shift_sb[:, 0:w], newt_sb[:, 0:w].bitcast(I32), 1, None,
                              ALU.logical_shift_right).then_inc(sem["ln_shifted"], 1)
            dve.wait_ge(sem["ln_shifted"], 2 * n + 2)
            dve.tensor_scalar(rstd_sb[:, 0:w].bitcast(I32), shift_sb[:, 0:w], -1.0, float(0x5F3759DF),
                              ALU.mult, ALU.add).then_inc(sem["ln_guessed"], 1)

        def ln_pool(pool, n, t, w, keep=False):
            pool.wait_ge(sem["ln_guessed"], n + 1)
            y, v, a = rstd_sb[:, 0:w], newt_sb[:, 0:w], shift_sb[:, 0:w].bitcast(F32)
            for k in range(3):
                pool.tensor_tensor(a, y, y, ALU.mult).then_inc(sem["newton_steps"], 1)
                pool.wait_ge(sem["newton_steps"], 12 * n + 4 * k + 1)
                pool.tensor_tensor(a, a, v, ALU.mult).then_inc(sem["newton_steps"], 1)
                pool.wait_ge(sem["newton_steps"], 12 * n + 4 * k + 2)
                pool.sem_inc(sem["pool_passed"], 1)
                pool.tensor_scalar(a, a, -0.5, 1.5, ALU.mult, ALU.add).then_inc(sem["newton_steps"], 1)
                pool.wait_ge(sem["newton_steps"], 12 * n + 4 * k + 3)
                pool.tensor_tensor(y, y, a, ALU.mult).then_inc(sem["newton_steps"], 1)
                pool.wait_ge(sem["newton_steps"], 12 * n + 4 * k + 4)
            if positive(n):
                pool.wait_ge(sem["xn_turned"], n)
            pool.sem_inc(sem["pool_passed"], 1)

            def wide(a):
                return a.unsqueeze(2).broadcast_to([P, w, D])

            def rows_of(a):
                return a.rearrange("p (w d) -> p w d", d=D)

            mean = moments_sb[:, 0:2 * w].rearrange("p (w c) -> p w c", c=2)[:, :, 0]
            xns = rows_of(xns_sb[:, 0:w * D])
            pool.tensor_tensor(xns, rows_of(x_tiles(t, w)), wide(mean), ALU.subtract).then_inc(sem["xn_centred"], 1)
            pool.wait_ge(sem["xn_centred"], n + 1)
            if keep:
                pool.tensor_tensor(rows_of(xn_sb[:, bass.ds(t * D, w * D)]), xns, wide(y), ALU.mult)
            pool.tensor_tensor(xns, xns, wide(y), ALU.mult).then_inc(sem["xn_ready"], 1)

        def updates(n):
            return n - NG + 1

        def ln_pe(pe, n, out_ps, w):
            pe.wait_ge(sem["xn_ready"], n + 1)
            for u in range(w):
                i = pe.transpose(out_ps[:, u * P:(u + 1) * P], xns_sb[:, u * D:(u + 1) * D], ident)
            i.then_inc(sem["xn_turned"], 1)

        def ln_act(act, n, out_ps, t, w):
            act.wait_ge(sem["xn_turned"], n + 1)
            act.activation(xt_sb[:, bass.ds(t * P, w * P)], out_ps[:, 0:w * P], ACT.Copy).then_inc(
                sem["xt_group_ready" if w == GT else "xt_tile_ready"], w)

        def ln_number_attn(layer, t):
            return NG + (NT + NG) * layer + t

        def ln_number_ffn(layer, g):
            return NG + (NT + NG) * layer + NT + g

        def steps(eng, lag, step, ahead=0):
            first = lag + 1
            last = first + (NT - ahead - first) // 2 * 2
            for u in range(first):
                step(u, u % 2)
            with eng.Fori(0, (last - first) // 2) as i:
                u = i * 2 + first
                step(u, first % 2)
                step(u + 1, (first + 1) % 2)
            for u in range(last, NT + lag):
                step(u, u % 2)

        def on(u, back):
            return not isinstance(u, int) or 0 <= u - back < NT

        def a0_w(name):
            return view(slab1, WA0, name)

        Q0 = ps[:, 0:1024]
        K0 = ps[:, 1024:2048]
        T0 = ps[:, 2048:3072]
        S0 = ps[:, 3072:4096]

        def a0_pe(pe):
            pe.wait_ge(sem["wa0_loaded"], 16)

            def query(t):
                pe.wait_ge(sem["xt_group_ready"], t + 1)
                if positive(t):
                    pe.wait_ge(sem["v_ready"], t)
                for c in range(8):
                    i = pe.matmul(Q0[:, c * P:(c + 1) * P], a0_w("q")[:, c * P:(c + 1) * P],
                                  xt_sb[:, bass.ds(t * P, P)], start=True, stop=True)
                i.then_inc(sem["q_projected"], 1)

            def key(t, p):
                pe.wait_ge(sem["ctx_staged"], t + 1)
                if positive(t - 2):
                    pe.wait_ge(sem["heads_ready"], t - 2)
                for c in range(8):
                    i = pe.matmul(K0[:, c * P:(c + 1) * P], a0_w("k")[:, c * P:(c + 1) * P], c0[p],
                                  start=True, stop=True)
                i.then_inc(sem["k_projected"], 1)

            def value(t, p):
                pe.wait_ge(sem["q_ready"], t + 1)
                for j in range(2):
                    i = pe.matmul(Q0[:, j * 512:(j + 1) * 512], c0[p], a0_w("v")[:, j * 512:(j + 1) * 512],
                                  start=True, stop=True)
                i.then_inc(sem["v_projected"], 1)

            def step(u, p):
                t = u - 1
                if isinstance(u, int) and u == 0:
                    query(0)
                    key(0, 0)
                    value(0, 0)
                if on(u, 0):
                    pe.wait_ge(sem["q_ready"], u + 1)
                    pe.wait_ge(sem["k_ready"], u + 1)
                    if positive(u):
                        pe.wait_ge(sem["scores_centred"], u)
                    pe.sem_inc(sem["pe_passed"], 1)
                    for h2 in range(2):
                        h = slice(64 * h2, 64 * h2 + 64)
                        for c in range(8):
                            for b in range(2):
                                at = slice(c * P + b * 64, c * P + b * 64 + 64)
                                i = pe.matmul(S0[h, at], qt0[p][h, at], kt0[p][h, at], start=True, stop=True)
                    i.then_inc(sem["scores_ready"], 1)
                if on(u, -1):
                    query(u + 1)
                if on(u, 2):
                    pe.wait_ge(sem["heads_ready"], u - 1)
                    for c in range(8):
                        i = pe.matmul(T0[:, 0:P], ot0[:, c * P:(c + 1) * P],
                                      a0_w("u")[:, c * P:(c + 1) * P], start=c == 0, stop=c == 7)
                    i.then_inc(sem["out_projected"], 1)
                if on(u, -1):
                    key(u + 1, 1 - p)
                if on(u, 1):
                    pe.wait_ge(sem["probs_ready"], t + 1)
                    if positive(updates(ln_number_attn(0, t - 1))):
                        pe.wait_ge(sem["x_updated"], updates(ln_number_attn(0, t - 1)))
                    if positive(t - 1):
                        pe.wait_ge(sem["xt_tile_ready"], t - 1)
                    for c in range(8):
                        i = pe.transpose(T0[:, c * P:(c + 1) * P], e0[1 - p][:, c * P:(c + 1) * P], ident)
                    i.then_inc(sem["probs_turned"], 1)
                if on(u, -1):
                    value(u + 1, 1 - p)
                if on(u, 1):
                    pe.wait_ge(sem["v_ready"], t + 1)
                    pe.wait_ge(sem["probs_t_ready"], t + 1)
                    if on(u, -1):
                        pe.wait_ge(sem["k_ready"], u + 2)
                    else:
                        pe.wait_ge(sem["heads_ready"], t)
                    pe.sem_inc(sem["pe_passed"], 1)
                    for b in range(2):
                        r = slice(64 * b, 64 * b + 64)
                        for c in range(8):
                            for h2 in range(2):
                                i = pe.matmul(K0[64 * h2:64 * h2 + 64, b * 512 + c * 64:b * 512 + c * 64 + 64],
                                              v0[1 - p][r, c * P + h2 * 64:c * P + h2 * 64 + 64],
                                              pt0[r, c * P + h2 * 64:c * P + h2 * 64 + 64], start=True, stop=True)
                    i.then_inc(sem["heads_summed"], 1)
                if on(u, 2):
                    if not on(u, 1):
                        pe.wait_ge(sem["xt_tile_ready"], u - 2)
                    ln_pe(pe, ln_number_attn(0, u - 2), T0[:, 512:640], 1)
            steps(pe, 2, step, 2)

        def a0_dve(dve):
            def evict(src, dst, bias, ready, full, t):
                dve.wait_ge(sem[full], t + 1)
                dve.tensor_tensor(dst.rearrange("p (c t) -> p c t", c=8), src.rearrange("p (c t) -> p c t", c=8),
                                  bias, ALU.add).then_inc(sem[ready], 1)

            def evict_q(t, p):
                evict(Q0, qt0[p], col("bq0").unsqueeze(2).broadcast_to([P, 8, P]), "q_ready", "q_projected", t)

            def evict_k(t, p):
                evict(K0, kt0[p], col("bk0").unsqueeze(2).broadcast_to([P, 8, P]), "k_ready", "k_projected", t)

            def evict_v(t, p):
                evict(Q0, v0[p], row("bv0").rearrange("p (c t) -> p c t", c=8), "v_ready", "v_projected", t)

            def step(u, p):
                t = u - 1
                if isinstance(u, int) and u == 0:
                    evict_q(0, 0)
                    evict_k(0, 0)
                    evict_v(0, 0)
                if on(u, 1):
                    o = e0[1 - p].rearrange("p (h t) -> p h t", h=H)
                    dve.wait_ge(sem["exp_ready"], t + 1)
                    if positive(t):
                        dve.wait_ge(sem["probs_ready"], t)
                    dve.tensor_reduce(rs_sb[:, H:2 * H], o, AX.X, ALU.add).then_inc(sem["exp_sum_ready"], 1)
                    dve.wait_ge(sem["exp_sum_ready"], t + 1)
                    dve.reciprocal(rs_sb[:, 2 * H:3 * H], rs_sb[:, H:2 * H]).then_inc(sem["exp_recip_ready"], 1)
                if on(u, 0):
                    s = S0.rearrange("p (h t) -> p h t", h=H)
                    dve.wait_ge(sem["scores_ready"], u + 1)
                    dve.tensor_reduce(rs_sb[:, 0:H], s, AX.X, ALU.max).then_inc(sem["row_max_ready"], 1)
                    dve.wait_ge(sem["row_max_ready"], u + 1)
                    dve.tensor_tensor(e0[p].rearrange("p (h t) -> p h t", h=H), s,
                                      rs_sb[:, 0:H].unsqueeze(2).broadcast_to([P, H, S]),
                                      ALU.subtract).then_inc(sem["scores_centred"], 1)
                if on(u, -1):
                    evict_q(u + 1, 1 - p)
                if on(u, 2):
                    dve.wait_ge(sem["out_projected"], u - 1)
                    dve.wait_ge(sem["x_biased"], u - 1)
                    dve.scalar_tensor_tensor(x_tiles(u - 2, 1), T0[:, 0:P], gain_sb[:, 0:1], xb_sb[:], ALU.mult,
                                             ALU.add).then_inc(sem["x_updated"], 1)
                    ln_dve(dve, ln_number_attn(0, u - 2), u - 2, 1)
                if on(u, -1):
                    evict_k(u + 1, 1 - p)
                    if positive(u):
                        dve.wait_ge(sem["heads_summed"], u)
                    dve.sem_inc(sem["dve_passed"], 1)
                    evict_v(u + 1, 1 - p)
            steps(dve, 2, step, 2)

        def a0_act(act):
            def step(u, p):
                t = u - 1
                if on(u, 0):
                    act.wait_ge(sem["scores_centred"], u + 1)
                    act.activation(e0[p], e0[p], ACT.Exp, scale=HD0 ** -0.5).then_inc(sem["exp_ready"], 1)
                if on(u, 1):
                    act.wait_ge(sem["probs_turned"], t + 1)
                    act.activation(pt0, T0, ACT.Copy).then_inc(sem["probs_t_ready"], 1)
                    act.wait_ge(sem["heads_summed"], t + 1)
                    act.activation(ot0.rearrange("p (c b q) -> p b c q", c=8, b=2),
                                   K0.rearrange("p (b c q) -> p b c q", b=2, c=8),
                                   ACT.Copy).then_inc(sem["heads_ready"], 1)
                if on(u, 2):
                    ln_act(act, ln_number_attn(0, u - 2), T0[:, 512:640], u - 2, 1)
            steps(act, 2, step, 2)

        def a0_pool(pool):
            def stage(t, p):
                if positive(t - 1):
                    pool.wait_ge(sem["v_projected"], t - 1)
                pool.tensor_copy(c0[p], ctx_sb[:, bass.ds(t * P, P)]).then_inc(sem["ctx_staged"], 1)

            def step(u, p):
                if isinstance(u, int) and u == 0:
                    stage(0, 0)
                    stage(1, 1)
                if on(u, 1):
                    t, o = u - 1, e0[1 - p].rearrange("p (h t) -> p h t", h=H)
                    pool.wait_ge(sem["exp_recip_ready"], t + 1)
                    pool.tensor_tensor(o, o, rs_sb[:, 2 * H:3 * H].unsqueeze(2).broadcast_to([P, H, S]),
                                       ALU.mult).then_inc(sem["probs_ready"], 1)
                if on(u, -2):
                    stage(u + 2, p)
                if on(u, 2):
                    ln_pool(pool, ln_number_attn(0, u - 2), u - 2, 1)
                if on(u, 1):
                    if positive(updates(ln_number_attn(0, t - 1))):
                        pool.wait_ge(sem["x_updated"], updates(ln_number_attn(0, t - 1)))
                    pool.sem_inc(sem["pool_passed"], 1)
                    pool.tensor_tensor(xb_sb[:], x_sb[:, bass.ds(t * D, D)], gbias_sb[:, 0:D],
                                       ALU.add).then_inc(sem["x_biased"], 1)
            steps(pool, 2, step, 2)

        USED_IN = dict(qs_ready=(1, 2, 3), ks_ready=(1, 2, 3), kexp_ready=(1, 2, 3), heads_scaled=(1, 2, 3),
                       heads_turned=(1, 2, 3), heads_t_ready=(1, 2, 3), biased_ready=(3,), bias_scaled=(3,),
                       vs_projected=(1, 3), cdup_staged=(1, 2, 3), vm_ready=(1, 2, 3), scores_centred=(0, 1, 3),
                       scores_ready=(0, 1, 2, 3), row_max_ready=(0, 1, 3), exp_ready=(0, 1, 3),
                       exp_sum_ready=(0, 1, 3), exp_recip_ready=(0, 1, 3), probs_turned=(0, 1, 2, 3),
                       probs_t_ready=(0, 1, 2, 3), heads_summed=(0, 1, 2, 3), out_projected=(0, 1, 2, 3),
                       x_biased=(0, 1, 2), sum_plus_one=(3,),
                       **{n: (2,) for n in ("qk_projected", "values_projected", "offsets_projected", "offsets_ready", "positions_ready",
                                            "distance_ready", "hat_abs_ready", "half_hat_ready", "scores_copied",
                                            "sampled_half", "sampled_max", "sampled_centred", "sampled_exp",
                                            "sampled_sum", "sampled_recip", "weights_ready", "hat_weighted_pool",
                                            "hat_weighted_dve", "product_ready")})

        def past(layer, name):
            return NT * sum(l < layer for l in USED_IN[name])

        XB = bank(0)
        SB = ps[:, 512:2560].rearrange("p (r x) -> p r x", r=4)[:, :, 0:256]
        PTB = ps[:, 2560:3584]
        OB = bank(7)

        def w_attn(layer, name):
            return view(wsa_sb, WSA, f"{name}{layer}")

        def halves():
            return [slice(0, 64), slice(64, 128)]

        def narrow_project(pe, L, u, p):
            pe.matmul(XB[:, 0:P], w_attn(L, "q"), xt_sb[:, bass.ds(u * P, P)], start=True, stop=True)
            pe.matmul(XB[:, P:2 * P], w_attn(L, "k"), ctx_sb[:, bass.ds(u * P, P)], start=True, stop=True)
            for b in range(2):
                i = pe.matmul(XB[:, 256 + b * P:256 + (b + 1) * P], cdup[p][:, b * P:(b + 1) * P],
                              w_attn(L, "v"), start=True, stop=True)
            i.then_inc(sem["vs_projected"], 1)

        def narrow_scores(pe, p):
            for r in range(4):
                rows = slice(32 * r, 32 * r + 32)
                for b in range(2):
                    i = pe.matmul(SB[64 * b:64 * b + 64, r, :], qt[p][rows, 64 * b:64 * b + 64],
                                  kexp[p][rows, 256 * b:256 * b + 256], start=True, stop=True)
            i.then_inc(sem["scores_ready"], 1)

        def narrow_heads(pe, L, t, old_p):
            pe.wait_ge(sem["vm_ready"], t + 1 + past(L, "vm_ready"))
            pe.wait_ge(sem["x_updated"], updates(ln_number_attn(L, t - 1)))
            for c in range(HP):
                i = pe.matmul(OB[:, c * 32:(c + 1) * 32], pt[:, c * P:(c + 1) * P],
                              vm[old_p][:, c * 32:(c + 1) * 32], start=True, stop=True)
            i.then_inc(sem["heads_summed"], 1)

        def narrow_turn_heads(pe, L, t):
            pe.wait_ge(sem["heads_scaled"], t + 1 + past(L, "heads_scaled"))
            pe.transpose(OB[:, 256:384], ob, ident).then_inc(sem["heads_turned"], 1)

        def narrow_output(pe, L, t):
            pe.wait_ge(sem["heads_t_ready"], t + 1 + past(L, "heads_t_ready"))
            pe.matmul(OB[:, 384:512], obt, w_attn(L, "o"), start=True, stop=True).then_inc(sem["out_projected"], 1)

        def narrow_evict_qk(act, L, u, p):
            act.wait_ge(sem["vs_projected"], u + 1 + past(L, "vs_projected"))
            for dst, at, name, done in ((qt[p], 0, "bq", "qs_ready"), (kt[p], P, "bk", "ks_ready")):
                if L == 3:
                    i = act.activation(dst, XB[:, at:at + P], ACT.Copy)
                else:
                    i = act.activation(dst, XB[:, at:at + P], ACT.Identity, bias=col(f"{name}{L}"))
                i.then_inc(sem[done], 1)

        def narrow_values(dve, L, u, p):
            dve.wait_ge(sem["ks_ready"], u + 1 + past(L, "ks_ready"))
            dve.sem_inc(sem["dve_passed"], 1)
            for h2, r in enumerate(halves()):
                dst = vm[p][r].rearrange("p (c b h d) -> p h b c d", c=HP, b=2, h=2)[:, h2]
                src = XB[r, 256:512].rearrange("p (b c h d) -> p h b c d", b=2, c=HP, h=2)[:, h2]
                if L == 3:
                    i = dve.tensor_copy(dst, src)
                else:
                    bv = row(f"bv{L}")[r].rearrange("p (c h d) -> p h c d", c=HP, h=2)[:, h2]
                    i = dve.tensor_tensor(dst, src, bv.unsqueeze(1).broadcast_to([64, 2, HP, HD]), ALU.add)
            i.then_inc(sem["vm_ready"], 1)

        def narrow_scale(dve, L, t, recip):
            dve.wait_ge(sem["heads_summed"], t + 1 + past(L, "heads_summed"))
            for b, r in enumerate(halves()):
                i = dve.tensor_tensor(ob[r].rearrange("p (c h d) -> p c h d", c=HP, h=2),
                                      OB[r, 0:256].rearrange("p (c b h d) -> p b c h d", c=HP, b=2, h=2)[:, b],
                                      recip[r].rearrange("p (c h) -> p c h", h=2).unsqueeze(3).broadcast_to(
                                          [64, HP, 2, HD]), ALU.mult)
            i.then_inc(sem["heads_scaled"], 1)

        def narrow_update(dve, L, t):
            dve.wait_ge(sem["out_projected"], t + 1 + past(L, "out_projected"))
            if L == 3:
                res = x_tiles(t, 1)
            else:
                dve.wait_ge(sem["x_biased"], t + 1 + past(L, "x_biased"))
                res = xb_sb[:]
            dve.scalar_tensor_tensor(x_tiles(t, 1), OB[:, 384:512], gain_sb[:, L:L + 1], res, ALU.mult,
                                     ALU.add).then_inc(sem["x_updated"], 1)
            ln_dve(dve, ln_number_attn(L, t), t, 1)

        def narrow_stage(pool, L, t, p):
            if positive(t - 1 + past(L, "vs_projected")):
                pool.wait_ge(sem["vs_projected"], t - 1 + past(L, "vs_projected"))
            pool.tensor_copy(cdup[p].rearrange("p (b c t) -> p b c t", b=2, c=2),
                             ctx_sb[:, bass.ds(t * P, P)].rearrange("p (b t) -> p b t", b=2).unsqueeze(2).broadcast_to(
                                 [P, 2, 2, S])).then_inc(sem["cdup_staged"], 1)

        def narrow_expand(pool, L, u, p):
            pool.wait_ge(sem["ks_ready"], u + 1 + past(L, "ks_ready"))
            pool.tensor_tensor(kexp[p].rearrange("p (b h t) -> p b h t", b=2, h=4),
                               kt[p].rearrange("p (b t) -> p b t", b=2).unsqueeze(2).broadcast_to([P, 2, 4, S]),
                               const("headmask").unsqueeze(1).unsqueeze(3).broadcast_to([P, 2, 4, S]),
                               ALU.mult).then_inc(sem["kexp_ready"], 1)

        def narrow_bias_rows(pool, L, t):
            pool.wait_ge(sem["x_updated"], updates(ln_number_attn(L, t - 1)))
            pool.sem_inc(sem["pool_passed"], 1)
            pool.tensor_tensor(xb_sb[:], x_sb[:, bass.ds(t * D, D)], gbias_sb[:, L * D:(L + 1) * D],
                               ALU.add).then_inc(sem["x_biased"], 1)

        def zero_values(dve):
            dve.memset(vm[0], 0.0)
            dve.memset(vm[1], 0.0).then_inc(sem["attention_zeroed"], 1)

        def a13_pe(L):
            def program(pe):
                pe.wait_ge(sem["wsa_loaded"], 16)
                pe.wait_ge(sem["xt_group_ready"], (L + 1) * NT)

                def project(t, p):
                    pe.wait_ge(sem["cdup_staged"], t + 1 + past(L, "cdup_staged"))
                    if positive(t + past(L, "ks_ready")):
                        pe.wait_ge(sem["ks_ready"], t + past(L, "ks_ready"))
                    if positive(t + past(L, "vm_ready")):
                        pe.wait_ge(sem["vm_ready"], t + past(L, "vm_ready"))
                    narrow_project(pe, L, t, p)

                def step(u, p):
                    if isinstance(u, int) and u == 0:
                        project(0, 0)
                    if on(u, 0):
                        pe.wait_ge(sem["qs_ready"], u + 1 + past(L, "qs_ready"))
                        pe.wait_ge(sem["kexp_ready"], u + 1 + past(L, "kexp_ready"))
                        if positive(u + past(L, "biased_ready" if L == 3 else "scores_centred")):
                            pe.wait_ge(sem["biased_ready" if L == 3 else "scores_centred"], u + past(L, "biased_ready" if L == 3 else "scores_centred"))
                        pe.sem_inc(sem["pe_passed"], 1)
                        narrow_scores(pe, p)
                    if on(u, 2):
                        narrow_turn_heads(pe, L, u - 2)
                    if on(u, 1):
                        t = u - 1
                        pe.wait_ge(sem["exp_ready"], t + 1 + past(L, "exp_ready"))
                        pe.wait_ge(sem["xt_tile_ready"], u - 3 + L * NT)
                        for c in range(HP):
                            i = pe.transpose(PTB[:, c * P:(c + 1) * P], ex[1 - p][:, c * P:(c + 1) * P], ident)
                        i.then_inc(sem["probs_turned"], 1)
                    if on(u, 2):
                        narrow_output(pe, L, u - 2)
                    if on(u, -1):
                        project(u + 1, 1 - p)
                    if on(u, 1):
                        pe.wait_ge(sem["probs_t_ready"], u + past(L, "probs_t_ready"))
                        narrow_heads(pe, L, u - 1, 1 - p)
                    if on(u, 3):
                        if not on(u, 1):
                            pe.wait_ge(sem["xt_tile_ready"], u - 3 + L * NT)
                        ln_pe(pe, ln_number_attn(L, u - 3), PTB, 1)
                steps(pe, 3, step, 2)
            return program

        def a13_act(L):
            def program(act):
                def step(u, p):
                    if isinstance(u, int) and u == 0:
                        narrow_evict_qk(act, L, 0, 0)
                    if on(u, 2):
                        act.wait_ge(sem["heads_turned"], u - 1 + past(L, "heads_turned"))
                        act.activation(obt, OB[:, 256:384], ACT.Copy).then_inc(sem["heads_t_ready"], 1)
                    if on(u, 1):
                        act.wait_ge(sem["probs_turned"], u + past(L, "probs_turned"))
                        act.activation(pt, PTB, ACT.Copy).then_inc(sem["probs_t_ready"], 1)
                    if on(u, 0):
                        act.wait_ge(sem["scores_centred"], u + 1 + past(L, "scores_centred"))
                        act.activation(ex[p], ex[p], ACT.Exp, scale=1.0 if L == 3 else HD ** -0.5).then_inc(
                            sem["exp_ready"], 1)
                    if on(u, -1):
                        narrow_evict_qk(act, L, u + 1, 1 - p)
                    if on(u, 3):
                        ln_act(act, ln_number_attn(L, u - 3), PTB, u - 3, 1)
                steps(act, 3, step, 2)
            return program

        def a13_dve(L):
            def program(dve):
                zero_values(dve)
                dve.wait_ge(sem["attention_zeroed"], {1: 1, 3: 3}[L])

                def step(u, p):
                    t = u - 1
                    if isinstance(u, int) and u == 0:
                        narrow_values(dve, L, 0, 0)
                    if on(u, 1):
                        dve.wait_ge(sem["exp_ready"], t + 1 + past(L, "exp_ready"))
                        dve.tensor_reduce(rs_sb[:, H:2 * H], ex[1 - p].rearrange("p (h t) -> p h t", h=H), AX.X,
                                          ALU.add).then_inc(sem["exp_sum_ready"], 1)
                        dve.wait_ge(sem["exp_sum_ready"], t + 1 + past(L, "exp_sum_ready"))
                        if L == 3:
                            dve.tensor_scalar(rs_sb[:, H:2 * H], rs_sb[:, H:2 * H], 1.0, None, ALU.add).then_inc(
                                sem["sum_plus_one"], 1)
                            dve.wait_ge(sem["sum_plus_one"], t + 1 + past(L, "sum_plus_one"))
                        dve.reciprocal(rs_sb[:, 2 * H:3 * H], rs_sb[:, H:2 * H]).then_inc(sem["exp_recip_ready"], 1)
                    if on(u, 0):
                        dve.wait_ge(sem["scores_ready"], u + 1 + past(L, "scores_ready"))
                        s4 = SB
                        flat = ex[p].rearrange("p (r x) -> p r x", r=4)
                        if L == 3:
                            dve.wait_ge(sem["bias_scaled"], u + 1 + past(L, "bias_scaled"))
                            dve.scalar_tensor_tensor(flat, s4, float(np.float32(HD ** -0.5)),
                                                     prod[p].rearrange("p (r x) -> p r x", r=4), ALU.mult,
                                                     ALU.add).then_inc(sem["biased_ready"], 1)
                            dve.wait_ge(sem["biased_ready"], u + 1 + past(L, "biased_ready"))
                            s4 = flat
                        heads = s4.rearrange("p r (h t) -> p r h t", h=4)
                        dve.tensor_reduce(rs_sb[:, 0:H].rearrange("p (r h) -> p r h", r=4), heads, AX.X,
                                          ALU.max).then_inc(sem["row_max_ready"], 1)
                        dve.wait_ge(sem["row_max_ready"], u + 1 + past(L, "row_max_ready"))
                        dve.tensor_tensor(ex[p].rearrange("p (r h t) -> p r h t", r=4, h=4), heads,
                                          rs_sb[:, 0:H].rearrange("p (r h) -> p r h", r=4).unsqueeze(3).broadcast_to(
                                              [P, 4, 4, S]), ALU.subtract).then_inc(sem["scores_centred"], 1)
                    if on(u, 2):
                        narrow_update(dve, L, u - 2)
                    if on(u, 1):
                        dve.wait_ge(sem["exp_recip_ready"], t + 1 + past(L, "exp_recip_ready"))
                        narrow_scale(dve, L, t, rs_sb[:, 2 * H:3 * H])
                    if on(u, -1):
                        narrow_values(dve, L, u + 1, 1 - p)
                steps(dve, 3, step, 2)
            return program

        def a13_pool(L):
            def bias_of(pool, t, p):
                if positive(t - 1 + past(L, "biased_ready")):
                    pool.wait_ge(sem["biased_ready"], t - 1 + past(L, "biased_ready"))
                pool.sem_inc(sem["pool_passed"], 1)
                pool.tensor_tensor(prod[p].rearrange("p (h t) -> p h t", h=H),
                                   const("slopes").unsqueeze(2).broadcast_to([P, H, S]),
                                   xn_sb[:, bass.ds(t * S, S)].unsqueeze(1).broadcast_to([P, H, S]),
                                   ALU.mult).then_inc(sem["bias_scaled"], 1)

            def program(pool):
                if L == 3:
                    pool.wait_ge(sem["dist_steps"], 4)

                def step(u, p):
                    if isinstance(u, int) and u == 0:
                        narrow_stage(pool, L, 0, 0)
                        narrow_expand(pool, L, 0, 0)
                        narrow_stage(pool, L, 1, 1)
                        if L == 3:
                            bias_of(pool, 0, 0)
                    if on(u, -2):
                        narrow_stage(pool, L, u + 2, p)
                    if on(u, -1):
                        if L == 3:
                            bias_of(pool, u + 1, 1 - p)
                        narrow_expand(pool, L, u + 1, 1 - p)
                    if on(u, 2):
                        ln_pool(pool, ln_number_attn(L, u - 2), u - 2, 1, keep=L == 1)
                    if on(u, 1) and L != 3:
                        narrow_bias_rows(pool, L, u - 1)
                steps(pool, 3, step, 2)
            return program

        PAIRS_POOL = 7
        NSAMP = H * NK
        wbuf = slab0[:, NWF2:NWF2 + NSAMP * S]
        product = xn_sb[:, 0:NSAMP * S // 2]
        pos, samp, wgt, offs, base = o80[0], o80[1], o80[2], o80[3], o80[4]
        tmp = [o80[5], o80[6]]
        kscore = prod

        def a2_pe(pe):
            pe.wait_ge(sem["wsa_loaded"], 16)
            pe.wait_ge(sem["xt_group_ready"], 3 * NT)

            def queries_keys(t):
                if positive(t + past(2, "offsets_ready")):
                    pe.wait_ge(sem["offsets_ready"], t + past(2, "offsets_ready"))
                pe.matmul(XB[:, 0:P], w_attn(2, "q"), xt_sb[:, bass.ds(t * P, P)], start=True, stop=True)
                pe.matmul(XB[:, P:2 * P], w_attn(2, "k"), ctx_sb[:, bass.ds(t * P, P)], start=True,
                          stop=True).then_inc(sem["qk_projected"], 1)

            def offsets(t, p):
                pe.wait_ge(sem["ks_ready"], t + 1 + past(2, "ks_ready"))
                pe.sem_inc(sem["pe_passed"], 1)
                pe.matmul(XB[:, 0:NSAMP], qt[p], w_attn(2, "off"), start=True, stop=True).then_inc(
                    sem["offsets_projected"], 1)

            def step(u, p):
                if isinstance(u, int) and u == 0:
                    queries_keys(0)
                    offsets(0, 0)
                if on(u, 0):
                    pe.wait_ge(sem["qs_ready"], u + 1 + past(2, "qs_ready"))
                    pe.wait_ge(sem["kexp_ready"], u + 1 + past(2, "kexp_ready"))
                    if positive(u + past(2, "scores_copied")):
                        pe.wait_ge(sem["scores_copied"], u + past(2, "scores_copied"))
                    pe.sem_inc(sem["pe_passed"], 1)
                    narrow_scores(pe, p)
                if on(u, 3):
                    narrow_turn_heads(pe, 2, u - 3)
                pe.wait_ge(sem["xt_tile_ready"], u - 3 + 2 * NT)
                if on(u, 1):
                    pe.wait_ge(sem["cdup_staged"], u + past(2, "cdup_staged"))
                    pe.wait_ge(sem["offsets_ready"], u + 1 if on(u, 0) else NT + past(2, "offsets_ready"))
                    pe.sem_inc(sem["pe_passed"], 1)
                    for b in range(2):
                        i = pe.matmul(XB[:, 256 + b * P:256 + (b + 1) * P], cdup[1 - p][:, b * P:(b + 1) * P],
                                      w_attn(2, "v"), start=True, stop=True)
                    i.then_inc(sem["values_projected"], 1)
                if on(u, -1):
                    queries_keys(u + 1)
                if on(u, 3):
                    narrow_output(pe, 2, u - 3)
                if on(u, -1):
                    if on(u, 1):
                        pe.wait_ge(sem["vm_ready"], u + past(2, "vm_ready"))
                    offsets(u + 1, 1 - p)
                if on(u, 2):
                    pe.wait_ge(sem["hat_weighted_pool"], u - 1 + past(2, "hat_weighted_pool"))
                    pe.wait_ge(sem["hat_weighted_dve"], u - 1 + past(2, "hat_weighted_dve"))
                    pe.wait_ge(sem["probs_t_ready"], u - 2 + past(2, "probs_t_ready"))
                    for c in range(HP):
                        for k in range(NK):
                            at = (c * NK + k) * P
                            i = pe.matmul(PTB[:, c * P:(c + 1) * P], wbuf[:, at:at + P], ident, start=k == 0,
                                          stop=k == NK - 1)
                    i.then_inc(sem["probs_turned"], 1)
                    pe.wait_ge(sem["probs_t_ready"], u - 1 + past(2, "probs_t_ready"))
                    narrow_heads(pe, 2, u - 2, p)
                if on(u, 3):
                    if on(u, -1):
                        pe.wait_ge(sem["offsets_ready"], u + 2 + past(2, "offsets_ready"))
                    elif on(u, 1):
                        pe.wait_ge(sem["vm_ready"], u + past(2, "vm_ready"))
                    ln_pe(pe, ln_number_attn(2, u - 3), XB, 1)
            steps(pe, 3, step, 1)

        def a2_act(act):
            def queries_keys(t, p):
                act.wait_ge(sem["qk_projected"], t + 1 + past(2, "qk_projected"))
                act.activation(qt[p], XB[:, 0:P], ACT.Identity, bias=col("bq2")).then_inc(sem["qs_ready"], 1)
                act.activation(kt[p], XB[:, P:2 * P], ACT.Identity, bias=col("bk2")).then_inc(sem["ks_ready"], 1)

            def step(u, p):
                if isinstance(u, int) and u == 0:
                    queries_keys(0, 0)
                if on(u, 0):
                    act.wait_ge(sem["scores_ready"], u + 1 + past(2, "scores_ready"))
                    if positive(2 * (u - 1) + past(2, "product_ready")):
                        act.wait_ge(sem["product_ready"], 2 * (u - 1) + past(2, "product_ready"))
                    act.activation(kscore[p].rearrange("p (r x) -> p r x", r=4), SB, ACT.Copy,
                                   scale=float(np.float32(0.5 * HD ** -0.5))).then_inc(sem["scores_copied"], 1)
                if on(u, 3):
                    act.wait_ge(sem["heads_turned"], u - 2 + past(2, "heads_turned"))
                    act.activation(obt, OB[:, 256:384], ACT.Copy).then_inc(sem["heads_t_ready"], 1)
                if on(u, -1):
                    queries_keys(u + 1, 1 - p)
                if on(u, 0):
                    act.wait_ge(sem["distance_ready"], u + 1 + past(2, "distance_ready"))
                    act.activation(hat[p], hat[p], ACT.Abs).then_inc(sem["hat_abs_ready"], 1)
                if on(u, 2):
                    act.wait_ge(sem["probs_turned"], u - 1 + past(2, "probs_turned"))
                    act.activation(pt, PTB, ACT.Copy).then_inc(sem["probs_t_ready"], 1)
                if on(u, 1):
                    act.wait_ge(sem["sampled_centred"], u + past(2, "sampled_centred"))
                    act.activation(samp, samp, ACT.Exp).then_inc(sem["sampled_exp"], 1)
                if on(u, 0):
                    act.wait_ge(sem["hat_abs_ready"], u + 1 + past(2, "hat_abs_ready"))
                    for half in range(2):
                        part = hat[p][:, half * (NSAMP * S // 2):(half + 1) * (NSAMP * S // 2)]
                        act.activation(part, part, ACT.Relu, scale=-1.0, bias=1.0).then_inc(
                            sem["half_hat_ready"], 1)
                if on(u, 3):
                    ln_act(act, ln_number_attn(2, u - 3), XB, u - 3, 1)
            steps(act, 3, step, 1)

        def a2_dve(dve):
            zero_values(dve)
            dve.tensor_tensor(base, row("boff"), const("refloc"), ALU.add).then_inc(sem["base_ready"], 1)
            dve.wait_ge(sem["attention_zeroed"], 2)
            dve.wait_ge(sem["base_ready"], 1)

            def samples(u, p, half):
                n = NSAMP // 2
                hs = slice(half * n * S, (half + 1) * n * S)
                dve.tensor_tensor(product.rearrange("p (h k j) -> p h k j", h=HP, k=NK),
                                  hat[1 - p][:, hs].rearrange("p (h k j) -> p h k j", h=HP, k=NK),
                                  kscore[1 - p][:, half * 512:half * 512 + 512].rearrange(
                                      "p (h j) -> p h j", h=HP).unsqueeze(2).broadcast_to([P, HP, NK, S]),
                                  ALU.mult).then_inc(sem["product_ready"], 1)
                dve.wait_ge(sem["product_ready"], (u - 1) * 2 + half + 1)
                dve.tensor_reduce(samp[:, half * n:(half + 1) * n], product.rearrange("p (s j) -> p s j", j=S), AX.X,
                                  ALU.add).then_inc(sem["sampled_half"], 1)

            def take_offsets(t):
                dve.wait_ge(sem["offsets_projected"], t + 1 + past(2, "offsets_projected"))
                if positive(t + past(2, "positions_ready")):
                    dve.wait_ge(sem["positions_ready"], t + past(2, "positions_ready"))
                dve.tensor_tensor(offs, XB[:, 0:NSAMP], base, ALU.add).then_inc(sem["offsets_ready"], 1)

            def step(u, p):
                if isinstance(u, int) and u == 0:
                    take_offsets(0)
                if on(u, 1):
                    dve.wait_ge(sem["half_hat_ready"], 2 * u - 1)
                    dve.wait_ge(sem["scores_copied"], u + past(2, "scores_copied"))
                    samples(u, p, 0)
                    dve.wait_ge(sem["values_projected"], u + past(2, "values_projected"))
                    if on(u, -1):
                        dve.wait_ge(sem["ks_ready"], u + 2 + past(2, "ks_ready"))
                    dve.sem_inc(sem["dve_passed"], 1)
                    for h2, r in enumerate(halves()):
                        dst = vm[1 - p][r].rearrange("p (c b h d) -> p h b c d", c=HP, b=2, h=2)[:, h2]
                        src = XB[r, 256:512].rearrange("p (b c h d) -> p h b c d", b=2, c=HP, h=2)[:, h2]
                        bv = row("bv2")[r].rearrange("p (c h d) -> p h c d", c=HP, h=2)[:, h2]
                        i = dve.tensor_tensor(dst, src, bv.unsqueeze(1).broadcast_to([64, 2, HP, HD]), ALU.add)
                    i.then_inc(sem["vm_ready"], 1)
                if on(u, 3):
                    narrow_update(dve, 2, u - 3)
                if on(u, 0):
                    dve.wait_ge(sem["positions_ready"], u + 1 + past(2, "positions_ready"))
                    if positive(u - 1 + past(2, "hat_weighted_pool")):
                        dve.wait_ge(sem["hat_weighted_pool"], u - 1 + past(2, "hat_weighted_pool"))
                    dve.tensor_tensor(hat[p].rearrange("p (s j) -> p s j", j=S),
                                      const("iota64").unsqueeze(1).broadcast_to([P, NSAMP, S]),
                                      pos.unsqueeze(2).broadcast_to([P, NSAMP, S]), ALU.subtract).then_inc(
                        sem["distance_ready"], 1)
                if on(u, -1):
                    take_offsets(u + 1)
                if on(u, 1):
                    dve.wait_ge(sem["half_hat_ready"], 2 * u)
                    dve.wait_ge(sem["sampled_half"], u * 2 - 1)
                    samples(u, p, 1)
                    dve.wait_ge(sem["sampled_half"], u * 2)
                    s3 = samp.rearrange("p (h k) -> p h k", k=NK)

                    def wide(a):
                        return a.unsqueeze(2).broadcast_to([P, H, NK])

                    dve.tensor_reduce(rs_sb[:, 0:H], s3, AX.X, ALU.max).then_inc(sem["sampled_max"], 1)
                    dve.wait_ge(sem["sampled_max"], u + past(2, "sampled_max"))
                    dve.tensor_tensor(s3, s3, wide(rs_sb[:, 0:H]), ALU.subtract).then_inc(sem["sampled_centred"], 1)
                    dve.wait_ge(sem["sampled_exp"], u + past(2, "sampled_exp"))
                    dve.tensor_reduce(rs_sb[:, H:2 * H], s3, AX.X, ALU.add).then_inc(sem["sampled_sum"], 1)
                    dve.wait_ge(sem["sampled_sum"], u + past(2, "sampled_sum"))
                    dve.reciprocal(rs_sb[:, 2 * H:3 * H], rs_sb[:, H:2 * H]).then_inc(sem["sampled_recip"], 1)
                    dve.wait_ge(sem["sampled_recip"], u + past(2, "sampled_recip"))
                    if positive(u - 1 + past(2, "hat_weighted_pool")):
                        dve.wait_ge(sem["hat_weighted_pool"], u - 1 + past(2, "hat_weighted_pool"))
                    dve.scalar_tensor_tensor(wgt.rearrange("p (h k) -> p h k", k=NK), s3, 0.5,
                                             wide(rs_sb[:, 2 * H:3 * H]), ALU.mult, ALU.mult).then_inc(
                        sem["weights_ready"], 1)
                    dve.wait_ge(sem["weights_ready"], u + past(2, "weights_ready"))
                    dve.wait_ge(sem["probs_turned"], u - 1 + past(2, "probs_turned"))
                    weight(dve, 1 - p, PAIRS_POOL, HP).then_inc(sem["hat_weighted_dve"], 1)
                if on(u, 2):
                    dve.wait_ge(sem["heads_summed"], u - 1 + past(2, "heads_summed"))
                    for b, r in enumerate(halves()):
                        i = dve.tensor_copy(ob[r].rearrange("p (c h d) -> p c h d", c=HP, h=2),
                                            OB[r, 0:256].rearrange("p (c b h d) -> p b c h d", c=HP, b=2, h=2)[:, b])
                    i.then_inc(sem["heads_scaled"], 1)
            steps(dve, 3, step, 1)

        def weight(eng, p, c0, c1):
            for h2 in range(2):
                def part(a, order):
                    return a.rearrange(order, c=HP, h=2, k=NK)[:, c0:c1, h2]
                i = eng.tensor_tensor(part(wbuf, "p (c k h j) -> p c h k j"),
                                      part(hat[p], "p (c h k j) -> p c h k j"),
                                      part(wgt, "p (c h k) -> p c h k").unsqueeze(3).broadcast_to(
                                          [P, c1 - c0, NK, S]), ALU.mult)
            return i

        def a2_pool(pool):
            def positions(u):
                k = [0]

                def done(ins):
                    ins.then_inc(sem["position_steps"], 1)
                    k[0] += 1
                    pool.wait_ge(sem["position_steps"], u * 8 + k[0])

                m = lens_sb[:, bass.ds(u, 1)].broadcast_to([P, NSAMP])
                rm = rlens_sb[:, bass.ds(u, 1)].broadcast_to([P, NSAMP])
                a, b = tmp
                pool.wait_ge(sem["offsets_ready"], u + 1 + past(2, "offsets_ready"))
                if positive(u + past(2, "distance_ready")):
                    pool.wait_ge(sem["distance_ready"], u + past(2, "distance_ready"))
                pool.sem_inc(sem["pool_passed"], 1)
                done(pool.tensor_tensor(a, offs, rm, ALU.mult))
                pool.sem_inc(sem["pool_passed"], 1)
                done(pool.tensor_scalar(a, a, MAGIC, -MAGIC, ALU.add, ALU.add))
                pool.sem_inc(sem["pool_passed"], 1)
                done(pool.tensor_tensor(a, a, m, ALU.mult))
                done(pool.tensor_tensor(a, offs, a, ALU.subtract))
                pool.sem_inc(sem["pool_passed"], 1)
                done(pool.tensor_tensor(b, a, m, ALU.mult))
                pool.sem_inc(sem["pool_passed"], 1)
                done(pool.tensor_scalar(b, b, 0.0, None, ALU.is_lt))
                pool.sem_inc(sem["pool_passed"], 1)
                done(pool.tensor_tensor(b, b, m, ALU.mult))
                done(pool.tensor_tensor(a, a, b, ALU.add))
                pool.sem_inc(sem["pool_passed"], 1)
                pool.tensor_scalar(pos, a, float(np.float32(S / (S - 1))), -0.5, ALU.mult, ALU.add).then_inc(
                    sem["positions_ready"], 1)

            def step(u, p):
                if isinstance(u, int) and u == 0:
                    narrow_expand(pool, 2, 0, 0)
                    positions(0)
                if on(u, -1):
                    narrow_expand(pool, 2, u + 1, 1 - p)
                if on(u, 0):
                    if positive(u - 1 + past(2, "values_projected")):
                        pool.wait_ge(sem["values_projected"], u - 1 + past(2, "values_projected"))
                    pool.tensor_copy(cdup[p].rearrange("p (b c t) -> p b c t", b=2, c=2),
                                     ctx_sb[:, bass.ds(u * P, P)].rearrange("p (b t) -> p b t", b=2).unsqueeze(
                                         2).broadcast_to([P, 2, 2, S])).then_inc(sem["cdup_staged"], 1)
                if on(u, 3):
                    ln_pool(pool, ln_number_attn(2, u - 3), u - 3, 1)
                if on(u, 2):
                    pool.wait_ge(sem["x_updated"], updates(ln_number_attn(2, u - 3)))
                    pool.sem_inc(sem["pool_passed"], 1)
                    pool.tensor_tensor(xb_sb[:], x_sb[:, bass.ds((u - 2) * D, D)], gbias_sb[:, 2 * D:3 * D],
                                       ALU.add).then_inc(sem["x_biased"], 1)
                if on(u, -1):
                    positions(u + 1)
                if on(u, 1):
                    pool.wait_ge(sem["weights_ready"], u + past(2, "weights_ready"))
                    pool.wait_ge(sem["probs_turned"], u - 1 + past(2, "probs_turned"))
                    pool.sem_inc(sem["pool_passed"], 1)
                    weight(pool, 1 - p, 0, PAIRS_POOL).then_inc(sem["hat_weighted_pool"], 1)
            steps(pool, 3, step, 1)

        def distances(dve):
            dve.wait_ge(sem["kpos_loaded"], 32)
            dve.wait_ge(sem["maskq_loaded"], 16)
            dve.wait_ge(sem["qpos_loaded"], 16)
            keys, masked = xn_sb[:, 0:NT * S], xn_sb[:, NT * S:]
            dve.tensor_scalar(masked, masked.bitcast(I32), 0.0, -3.0e38, ALU.is_equal, ALU.mult).then_inc(
                sem["dist_steps"], 1)
            dve.tensor_tensor(keys.rearrange("p (n t) -> p n t", t=S),
                               keys.bitcast(I32).rearrange("p (n t) -> p n t", t=S),
                               qpos_sb[:].unsqueeze(2).broadcast_to([P, NT, S]), ALU.subtract).then_inc(
                sem["dist_steps"], 1)
            dve.wait_ge(sem["dist_steps"], 1)
            dve.tensor_scalar(masked, masked, 10.0, None, ALU.mult).then_inc(sem["dist_steps"], 1)
            dve.wait_ge(sem["dist_steps"], 3)
            dve.tensor_tensor(keys, keys, masked, ALU.add).then_inc(sem["dist_steps"], 1)
            dve.wait_ge(sem["dist_steps"], 4)

        JOB0 = {0: 0}
        Y0 = {0: 0}
        for f in FFNS:
            JOB0[f.layer + 1] = JOB0[f.layer] + f.jobs * NG + (4 * NG if f.layer == 0 else 0)
            Y0[f.layer + 1] = Y0[f.layer] + f.ys * NG
        gated_before = {0: 0, 1: 0, 2: FFNS[1].jobs * NG, 3: (FFNS[1].jobs + FFNS[2].jobs) * NG}
        plain_before = {0: 0, 1: JOB0[1], 2: JOB0[1], 3: JOB0[1]}
        bias_before = {0: 0, 3: NG}
        LT, TT = bank(6), bank(7)

        def slab_of(f):
            return slab1 if f.layer in (1, 3) else slab0

        def w_of(f, name):
            return view(slab_of(f), [WF0, WF1, WF2, WF3][f.layer], name)

        def hidden_bank(f, k):
            return (bank(2 * (k % 2)), bank(2 * (k % 2) + 1)) if f.gated else (bank(k % 4), None)

        def ring(f):
            return 2 if f.gated else 4

        def hidden_set_free(f, g, e):
            if isinstance(g, int) and g == 0 and e < f.sets:
                return Y0[f.layer]
            n = Y0[f.layer] + (1 if f.bias else 0) + e - f.sets + 1
            return g * f.ys + (n if e >= f.sets or not f.bias else n - 1)

        def ready_name(f):
            return "hidden_gated_ready" if f.gated else "hidden_relu_ready"

        def own(f, k):
            return (gated_before if f.gated else plain_before)[f.layer] + k

        def route_pe(pe, f):
            L = f.layer
            pe.wait_ge(sem[f"w{L}_loaded"], 16)
            pe.wait_ge(sem["xt_tile_ready"], (L + 1) * NT)
            with pe.Fori(0, NG) as g:
                G = g + L * NG
                if L == 0:
                    for c in range(4):
                        i = pe.matmul(bank(c), w_of(f, "rw1")[:, c * P:(c + 1) * P],
                                      xt_sb[:, bass.ds(g * GW, GW)], start=True, stop=True)
                        i.then_inc(sem["hidden_full"], 1)
                    for c in range(4):
                        pe.wait_ge(sem["hidden_relu_ready"], g * 4 + (c + 1))
                        i = pe.matmul(LT[0:E, :], w_of(f, "rw2")[:, c * E:(c + 1) * E], hid[c],
                                      start=c == 0, stop=c == 3)
                else:
                    i = pe.matmul(LT[0:E, :], w_of(f, "router"), xt_sb[:, bass.ds(g * GW, GW)], start=True, stop=True)
                i.then_inc(sem["logits_t_full"], 1)
                pe.wait_ge(sem["logits_t_ready"], G + 1)
                pe.sem_inc(sem["pe_passed"], 1)
                for u in range(GT):
                    i = pe.transpose(TT[:, u * E:(u + 1) * E], lgt[0:E, u * P:(u + 1) * P], ident[0:E, 0:E])
                i.then_inc(sem["logits_turned"], 1)
                pe.wait_ge(sem["logits_ready"], G + 1)
            if f.cap:
                n = 1 if L == 0 else 2
                pe.wait_ge(sem["mask_ready"], n)
                pe.matmul(LT[:, 0:NT * E], const("before"), rt[3], start=True, stop=True)
                pe.matmul(TT[:, 0:NT * E], const("ones"), rt[3], start=True, stop=True).then_inc(
                    sem["prefix_ready"], 1)

        def route_act(act, f):
            L = f.layer
            with act.Fori(0, NG) as g:
                G = g + L * NG
                if L == 0:
                    for c in range(4):
                        act.wait_ge(sem["hidden_full"], g * 4 + (c + 1))
                        act.activation(hid[c], bank(c), ACT.Relu, bias=col("rb1")[:, c:c + 1]).then_inc(
                            sem["hidden_relu_ready"], 1)
                act.wait_ge(sem["logits_t_full"], G + 1)
                if L in (0, 3):
                    act.activation(lgt[0:E, :], LT[0:E, :], ACT.Identity,
                                   bias=col("rb2" if L == 0 else "gb3")[0:E, :]).then_inc(sem["logits_t_ready"], 1)
                else:
                    act.activation(lgt[0:E, :], LT[0:E, :], ACT.Copy).then_inc(sem["logits_t_ready"], 1)
            if f.softmax:
                act.wait_ge(sem["route_steps"], ROUTE0[L] + 2)
                act.activation(rt[1], rt[1], ACT.Exp).then_inc(sem["route_exp_ready"], 1)
            if L == 1:
                act.wait_ge(sem["route_steps"], ROUTE0[L] + 1)
                act.activation(m1_sb[:], small[0], ACT.Sigmoid).then_inc(sem["gates_ready"], 1)

        ROUTE0 = {}

        def route_dve(dve, f):
            L = f.layer
            with dve.Fori(0, NG) as g:
                dve.wait_ge(sem["logits_turned"], g + (L * NG + 1))
                dve.tensor_copy(logit_sb[:, bass.ds(g * (GT * E), GT * E)], TT[:, 0:GT * E]).then_inc(
                    sem["logits_ready"], 1)
            dve.wait_ge(sem["logits_ready"], (L + 1) * NG)
            n = [ROUTE0[L]]

            def link(ins):
                ins.then_inc(sem["route_steps"], 1)
                n[0] += 1
                dve.wait_ge(sem["route_steps"], n[0])

            def v(a):
                return a.rearrange("p (t e) -> p t e", e=E)

            def wide(a):
                return a.unsqueeze(2).broadcast_to([P, NT, E])

            iota = const("iota8").unsqueeze(1).broadcast_to([P, NT, E])
            link(dve.tensor_reduce(small[0], v(logit_sb), AX.X, ALU.max))
            keys = logit_sb
            if f.softmax:
                link(dve.tensor_tensor(v(rt[1]), v(logit_sb), wide(small[0]), ALU.subtract))
                dve.wait_ge(sem["route_exp_ready"], 1 if L == 0 else 2)
                if f.softmax == "all":
                    link(dve.tensor_reduce(small[1], v(rt[1]), AX.X, ALU.add))
                    link(dve.reciprocal(small[2], small[1]))
                    link(dve.tensor_tensor(v(rt[1]), v(rt[1]), wide(small[2]), ALU.mult))
                    keys = rt[1]
                    link(dve.tensor_reduce(small[0], v(keys), AX.X, ALU.max))

            def one_hot(dst, values):
                link(dve.tensor_tensor(v(rt[4]), v(values), wide(small[0]), ALU.is_lt))
                link(dve.scalar_tensor_tensor(v(rt[5]), v(rt[4]), BIG, iota, ALU.mult, ALU.add))
                link(dve.tensor_reduce(small[1], v(rt[5]), AX.X, ALU.min))
                link(dve.tensor_tensor(v(dst), iota, wide(small[1]), ALU.is_equal))

            one_hot(rt[2], keys)
            chosen = rt[2]
            if f.topk == 2:
                link(dve.scalar_tensor_tensor(v(rt[6]), v(rt[2]), -3.0e38, v(keys), ALU.mult, ALU.add))
                link(dve.tensor_reduce(small[0], v(rt[6]), AX.X, ALU.max))
                one_hot(rt[7], rt[6])
                dve.tensor_tensor(rt[3], rt[2], rt[7], ALU.add).then_inc(sem["mask_ready"], 1)
                dve.wait_ge(sem["mask_ready"], 1 if L == 0 else 2)
                chosen = rt[3]
            if not f.softmax:
                dve.tensor_copy(comb_sb[:], chosen).then_inc(sem["comb_ready"], 1)
                return
            link(dve.tensor_tensor(rt[4], rt[1], rt[3], ALU.mult))
            link(dve.tensor_reduce(small[1], v(rt[4]), AX.X, ALU.add))
            if f.softmax == "all":
                link(dve.tensor_scalar(small[1], small[1], 1e-20, None, ALU.add))
            link(dve.reciprocal(small[2], small[1]))
            link(dve.tensor_tensor(v(rt[4]), v(rt[4]), wide(small[2]), ALU.mult))
            dve.wait_ge(sem["prefix_ready"], 1 if L == 0 else 2)
            link(dve.memset(rt[5][:, 0:E], 0.0))
            link(dve.tensor_copy(rt[5][:, E:], TT[:, 0:(NT - 1) * E]))
            a, b, s = rt[5], rt[6], 1
            while s < NT:
                link(dve.tensor_tensor(b[:, s * E:], a[:, s * E:], a[:, :(NT - s) * E], ALU.add))
                link(dve.tensor_copy(b[:, :s * E], a[:, :s * E]))
                a, b, s = b, a, 2 * s
            link(dve.tensor_tensor(a, a, LT[:, 0:NT * E], ALU.add))
            link(dve.tensor_scalar(a, a, float(f.cap), None, ALU.is_lt))
            dve.tensor_tensor(comb_sb[:], rt[4], a, ALU.mult).then_inc(sem["comb_ready"], 1)

        def count_route(f):
            n = 1 + 4
            if f.softmax:
                n += 1 + (4 if f.softmax == "all" else 0)
            if f.topk == 2:
                n += 2 + 4
            if f.softmax:
                n += 4 + (1 if f.softmax == "all" else 0) + 2 + 10 + 2
            return n

        total = 0
        for f in FFNS:
            ROUTE0[f.layer] = total
            total += count_route(f)

        def groups(eng, body):
            body(0)
            with eng.Fori(1, NG) as g:
                body(g)

        def ffn_pe(pe, f):
            L, nc_, J = f.layer, len(f.chunks), f.jobs
            k0 = 4 * NG if L == 0 else 0
            src_full = JOB0[L] + k0

            def turn(g):
                pe.wait_ge(sem["xt_group_ready"], g * GT + (L + 1) * NT)
                ln_pe(pe, ln_number_ffn(L, g), LT, GT)

            def body(g):
                G = g + L * NG
                y = [0]

                def y_slot():
                    n = g * f.ys + (Y0[L] + y[0])
                    if positive(n if y[0] == 0 else n - 1):
                        pe.wait_ge(sem["expert_added"], n if y[0] == 0 else n - 1)
                    k = y[0]
                    y[0] += 1
                    return k

                def first(e):
                    for c, (c0_, w) in enumerate(f.chunks):
                        j = e * nc_ + c
                        a, b = hidden_bank(f, j)
                        back = ring(f) if j >= ring(f) or J % ring(f) == 0 else 1
                        if positive(g * J + (own(f, k0 + j) - back + 1)):
                            pe.wait_ge(sem[ready_name(f)], g * J + (own(f, k0 + j) - back + 1))
                        rhs = xgt if (L == 1 and e < E) else xt_sb[:, bass.ds(g * GW, GW)]
                        fw = F1 if L == 1 else (P if L == 2 else 512)
                        i = pe.matmul(a[0:w, :], w_of(f, "w1")[:, e * fw + c0_:e * fw + c0_ + w], rhs,
                                      start=True, stop=True)
                        if f.gated:
                            i = pe.matmul(b[0:w, :], w_of(f, "w3")[:, e * fw + c0_:e * fw + c0_ + w], rhs,
                                          start=True, stop=True)
                        i.then_inc(sem["hidden_full"], 1)

                def second(e):
                    k = y_slot()
                    yb = bank(4 + k % 2)
                    pe.wait_ge(sem[ready_name(f)], g * J + own(f, k0 + (e + 1) * nc_))
                    for u in range(GT):
                        for c, (_, w) in enumerate(f.chunks):
                            i = pe.matmul(yb[:, u * P:(u + 1) * P],
                                          hid[(e % f.sets) * nc_ + c][0:w, u * P:(u + 1) * P],
                                          w_of(f, "w2")[0:w, (e * nc_ + c) * D:(e * nc_ + c + 1) * D],
                                          start=c == 0, stop=c == nc_ - 1)
                    i.then_inc(sem["expert_summed"], 1)

                if f.bias:
                    n = g + bias_before[L]
                    pe.wait_ge(sem["comb_staged"], G + 1)
                    for u in range(GT):
                        i = pe.transpose(TT[0:E, u * P:(u + 1) * P], combs[:, u * E:(u + 1) * E], ident)
                    i.then_inc(sem["comb_turned"], 1)
                    pe.wait_ge(sem["comb_t_ready"], n + 1)
                    k = y_slot()
                    for u in range(GT):
                        i = pe.matmul(bank(4 + k % 2)[:, u * P:(u + 1) * P], cbt[0:E, u * P:(u + 1) * P],
                                      col(f.bias)[0:E, :], start=True, stop=True)
                    i.then_inc(sem["expert_summed"], 1)
                if L == 1:
                    pe.wait_ge(sem["xg_ready"], g + 1)
                    for u in range(GT):
                        i = pe.transpose(TT[:, u * P:(u + 1) * P], xg[:, u * P:(u + 1) * P], ident)
                    i.then_inc(sem["xg_turned"], 1)
                    pe.wait_ge(sem["xg_t_ready"], g + 1)
                order = list(range(f.experts))
                for m, e in enumerate(order):
                    first(e)
                    if m:
                        second(order[m - 1])
                    if m == 2 and L != 3 and not (isinstance(g, int) and g == 0):
                        turn(g - 1)
                second(order[-1])

            groups(pe, body)
            if L != 3:
                turn(NG - 1)

        def ffn_act(act, f):
            L, nc_, J = f.layer, len(f.chunks), f.jobs
            k0 = 4 * NG if L == 0 else 0
            full0 = JOB0[L] + k0

            def body(g):
                G = g + L * NG
                if f.bias:
                    n = g + bias_before[L]
                    act.wait_ge(sem["comb_turned"], n + 1)
                    act.activation(cbt[0:E, :], TT[0:E, :], ACT.Copy).then_inc(sem["comb_t_ready"], 1)
                if L == 1:
                    act.wait_ge(sem["xg_turned"], g + 1)
                    act.activation(xgt, TT, ACT.Copy).then_inc(sem["xg_t_ready"], 1)
                for e in range(f.experts):
                    for c, (_, w) in enumerate(f.chunks):
                        j = e * nc_ + c
                        a, b = hidden_bank(f, j)
                        act.wait_ge(sem["hidden_full"], g * J + (full0 + j + 1))
                        if f.gated:
                            if positive(g * J + (own(f, k0 + j) - (0 if j == 0 else 1))):
                                act.wait_ge(sem[ready_name(f)], g * J + (own(f, k0 + j) - (0 if j == 0 else 1)))
                            act.activation(gate[j % 2][0:w, :], a[0:w, :], ACT.Silu).then_inc(
                                sem["gate_silu_ready"], 1)
                        else:
                            if positive(hidden_set_free(f, g, e)):
                                act.wait_ge(sem["expert_summed"], hidden_set_free(f, g, e))
                            act.activation(hid[(e % f.sets) * nc_ + c][0:w, :], a[0:w, :], ACT.Relu,
                                           bias=col("eb1" if L == 0 else "b13")[:, e * 4 + c:e * 4 + c + 1]).then_inc(
                                sem["hidden_relu_ready"], 1)
                    if e == 2 and not (isinstance(g, int) and g == 0) and L != 3:
                        ln_act(act, ln_number_ffn(L, g - 1), LT, (g - 1) * GT, GT)

            groups(act, body)
            if L != 3:
                ln_act(act, ln_number_ffn(L, NG - 1), LT, (NG - 1) * GT, GT)

        def ffn_dve(dve, f):
            L, nc_, J = f.layer, len(f.chunks), f.jobs
            k0 = 4 * NG if L == 0 else 0

            def body(g):
                G = g + L * NG
                y = [0]
                dve.wait_ge(sem["comb_ready"], L + 1)
                if f.bias:
                    if positive(g + bias_before[L]):
                        dve.wait_ge(sem["comb_turned"], g + bias_before[L])
                dve.tensor_copy(combs[:], comb_sb[:, bass.ds(g * (GT * E), GT * E)]).then_inc(sem["comb_staged"], 1)
                dve.wait_ge(sem["comb_staged"], G + 1)

                def mult(e):
                    for c, (_, w) in enumerate(f.chunks):
                        j = e * nc_ + c
                        _, b = hidden_bank(f, j)
                        dve.wait_ge(sem["gate_silu_ready"], g * J + (own(f, k0 + j) + 1))
                        dve.wait_ge(sem["expert_summed"], hidden_set_free(f, g, e))
                        dve.tensor_tensor(hid[(e % f.sets) * nc_ + c][0:w, :], gate[j % 2][0:w, :], b[0:w, :],
                                          ALU.mult).then_inc(sem["hidden_gated_ready"], 1)

                def add(e):
                    n = g * f.ys + (Y0[L] + y[0])
                    yb = bank(4 + y[0] % 2)
                    dve.wait_ge(sem["expert_summed"], n + 1)
                    if positive(n):
                        dve.wait_ge(sem["expert_added"], n)
                    if e is None:
                        dve.tensor_copy(acc, yb).then_inc(sem["expert_added"], 1)
                    else:
                        for u in range(GT):
                            a, yy = acc[:, u * P:(u + 1) * P], yb[:, u * P:(u + 1) * P]
                            w = combs[:, u * E + e:u * E + e + 1] if e < E else 1.0
                            if y[0] == 0:
                                i = dve.tensor_scalar(a, yy, w, None, ALU.mult)
                            else:
                                i = dve.scalar_tensor_tensor(a, yy, w, a, ALU.mult, ALU.add)
                        i.then_inc(sem["expert_added"], 1)
                    y[0] += 1

                if f.bias:
                    add(None)
                for e in range(f.experts):
                    if f.gated:
                        mult(e)
                    if e:
                        add(e - 1)
                add(f.experts - 1)
                dve.wait_ge(sem["expert_added"], (g + 1) * f.ys + Y0[L])
                xs = x_tiles(g * GT, GT)
                dve.scalar_tensor_tensor(xs, acc, gain_sb[:, 4 + L:5 + L], xs, ALU.mult, ALU.add).then_inc(
                    sem["x_updated"], 1)
                if L != 3:
                    ln_dve(dve, ln_number_ffn(L, g), g * GT, GT)

            groups(dve, body)
            if L == 2:
                distances(dve)

        def ffn_pool(pool, f):
            L = f.layer

            def body(g):
                if L == 1:
                    pool.wait_ge(sem["gates_ready"], 1)
                    if positive(g):
                        pool.wait_ge(sem["xg_turned"], g)
                    pool.sem_inc(sem["pool_passed"], 1)
                    pool.tensor_tensor(xg.rearrange("p (w d) -> p w d", d=D),
                                       xn_sb[:, bass.ds(g * GW, GW)].rearrange("p (w d) -> p w d", d=D),
                                       m1_sb[:, bass.ds(g * GT, GT)].unsqueeze(2).broadcast_to([P, GT, D]),
                                       ALU.mult).then_inc(sem["xg_ready"], 1)
                if L != 3:
                    ln_pool(pool, ln_number_ffn(L, g), g * GT, GT)

            if L != 3:
                groups(pool, body)

        def setup_act(act):
            act.wait_ge(sem["rows_loaded"], 16)
            act.activation(gain_sb[:], row("g"), ACT.Tanh).then_inc(sem["gains_ready"], 1)

        def setup_dve(dve):
            dve.wait_ge(sem["gains_ready"], 1)
            for k, name in enumerate(("bu0", "bo1", "bo2")):
                i = dve.tensor_scalar(gbias_sb[:, k * D:(k + 1) * D], row(name), gain_sb[:, k:k + 1], None, ALU.mult)
            i.then_inc(sem["bias_ready"], 1)

        def setup_lens(dve):
            dve.wait_ge(sem["mask2_loaded"], 32)
            dve.tensor_reduce(lens_sb[:], xn_sb[:, 0:NT * S].bitcast(I32).rearrange("p (n t) -> p n t", t=S), AX.X,
                              ALU.add).then_inc(sem["setup_steps"], 1)
            dve.wait_ge(sem["setup_steps"], 1)
            dve.tensor_scalar(lens_sb[:], lens_sb[:], -1.0, float(S - 1), ALU.mult, ALU.add).then_inc(
                sem["setup_steps"], 1)
            dve.wait_ge(sem["setup_steps"], 2)
            dve.reciprocal(rlens_sb[:], lens_sb[:]).then_inc(sem["lens_ready"], 1)

        ATT_PE = {1: a13_pe(1), 2: a2_pe, 3: a13_pe(3)}
        ATT_ACT = {1: a13_act(1), 2: a2_act, 3: a13_act(3)}
        ATT_DVE = {1: a13_dve(1), 2: a2_dve, 3: a13_dve(3)}
        ATT_POOL = {1: a13_pool(1), 2: a2_pool, 3: a13_pool(3)}
        block = stack.enter_context(nc.Block())

        @block.sync
        def _(sp):
            for dst, src, name in ((x_sb, x_in, "x_loaded"), (const_sb, consts_in, "consts_loaded"),
                                   (slab1[:, 0:NWA0], wa0, "wa0_loaded"), (ctx_sb, ctx_t, "ctx_loaded"),
                                   (cols_sb, cols_in, "cols_loaded"), (slab0[:, 0:NWF0], wf0, "w0_loaded"),
                                   (wsa_sb, wsa, "wsa_loaded")):
                sp.dma_start(dst[:], src).then_inc(sem[name], 16)
            mask2b = mask2.rearrange("(n b) t -> b n t", b=2)
            for b, r in enumerate(halves()):
                sp.dma_start(xn_sb[r, 0:NT * S].bitcast(I32).rearrange("p (n t) -> p n t", t=S),
                             mask2b[b].unsqueeze(0).broadcast_to([64, NT, S])).then_inc(sem["mask2_loaded"], 16)
            sp.dma_start(qpos_sb[:], qpos).then_inc(sem["qpos_loaded"], 16)
            if stop_after >= 2:
                sp.wait_ge(sem["xt_tile_ready"], NT)
                sp.dma_start(slab1[:, 0:NWF1], wf1).then_inc(sem["w1_loaded"], 16)
            if stop_after > 3:
                sp.wait_ge(sem["xt_group_ready"], 2 * NT)
                sp.dma_start(slab0[:, 0:NWF2], wf2).then_inc(sem["w2_loaded"], 16)
            if stop_after > 5:
                sp.wait_ge(sem["xt_tile_ready"], 3 * NT)
                kposb = kpos.rearrange("(n b) t -> b n t", b=2)
                for b, r in enumerate(halves()):
                    sp.dma_start(xn_sb[r, 0:NT * S].bitcast(I32).rearrange("p (n t) -> p n t", t=S),
                                 kposb[b].unsqueeze(0).broadcast_to([64, NT, S])).then_inc(sem["kpos_loaded"], 16)
                sp.dma_start(xn_sb[:, NT * S:].bitcast(I32), maskq).then_inc(sem["maskq_loaded"], 16)
                sp.dma_start(slab1[:, 0:NWF3], wf3).then_inc(sem["w3_loaded"], 16)
            base = updates(ln_number_ffn(3, 0)) if stop_after == 8 else None
            if base:
                with sp.Fori(0, NG) as g:
                    sp.wait_ge(sem["x_updated"], g + base)
                    sp.dma_start(out[:, bass.ds(g * GW, GW)], x_sb[:, bass.ds(g * GW, GW)]).then_inc(
                        sem["stored"], 16)
                sp.wait_ge(sem["stored"], 16 * NG)
            else:
                n = updates(ln_number_attn(stop_after // 2, NT - 1) if stop_after % 2 else
                            ln_number_ffn(stop_after // 2 - 1, NG - 1)) if stop_after else 0
                sp.wait_ge(sem["x_updated"], n)
                sp.dma_start(out, x_sb[:]).then_inc(sem["stored"], 16)
                sp.wait_ge(sem["stored"], 16)

        @block.tensor
        def _(pe):
            pe.wait_ge(sem["consts_loaded"], 16)

            def first(g):
                if positive(g * GT):
                    pe.wait_ge(sem["xt_group_ready"], g * GT)
                ln_pe(pe, g, bank(7), GT)
            groups(pe, first)
            pe.wait_ge(sem["xt_group_ready"], NT)
            if stop_after > 0:
                a0_pe(pe)
            for f in FFNS:
                if f.layer:
                    if stop_after > 2 * f.layer:
                        ATT_PE[f.layer](pe)
                if stop_after > 2 * f.layer + 1:
                    route_pe(pe, f)
                    ffn_pe(pe, f)

        @block.scalar
        def _(act):
            act.dma_start(rows_sb[:], rows_in.broadcast_to([P, NROWS])).then_inc(sem["rows_loaded"], 16)
            setup_act(act)
            groups(act, lambda g: ln_act(act, g, bank(7), g * GT, GT))
            act.wait_ge(sem["cols_loaded"], 16)
            if stop_after > 0:
                a0_act(act)
            for f in FFNS:
                if f.layer:
                    if stop_after > 2 * f.layer:
                        ATT_ACT[f.layer](act)
                if stop_after > 2 * f.layer + 1:
                    route_act(act, f)
                    ffn_act(act, f)

        @block.vector
        def _(dve):
            setup_dve(dve)
            dve.wait_ge(sem["x_loaded"], 16)
            groups(dve, lambda g: ln_dve(dve, g, g * GT, GT, True))
            dve.wait_ge(sem["cols_loaded"], 16)
            dve.wait_ge(sem["consts_loaded"], 16)
            if stop_after > 0:
                a0_dve(dve)
                setup_lens(dve)
            for f in FFNS:
                if f.layer:
                    if stop_after > 2 * f.layer:
                        ATT_DVE[f.layer](dve)
                if stop_after > 2 * f.layer + 1:
                    route_dve(dve, f)
                    ffn_dve(dve, f)

        @block.gpsimd
        def _(pool):
            pool.wait_ge(sem["x_loaded"], 16)
            groups(pool, lambda g: ln_pool(pool, g, g * GT, GT))
            pool.wait_ge(sem["bias_ready"], 1)
            pool.wait_ge(sem["ctx_loaded"], 16)
            if stop_after > 0:
                a0_pool(pool)
            for f in FFNS:
                if f.layer:
                    if stop_after > 2 * f.layer:
                        ATT_POOL[f.layer](pool)
                if stop_after > 2 * f.layer + 1:
                    ffn_pool(pool, f)


def arrays_of(inputs):
    f = {k: np.asarray(v) for k, v in inputs.items()}

    def fill(table, width, **fields):
        a = np.zeros((P, width), np.float32)
        for name, v in fields.items():
            lo, hi = table[name]
            v = v.reshape(v.shape[0], -1)
            assert v.shape[1] == hi - lo, (name, v.shape, hi - lo)
            a[:v.shape[0], lo:hi] = v
        return a

    def tokens(a):
        return np.ascontiguousarray(a.reshape(NT, P, -1).transpose(1, 0, 2).reshape(P, -1))

    def chunks(a):
        return a.reshape(-1, P, a.shape[-1]).transpose(1, 0, 2)

    def experts(a):
        return a.transpose(1, 0, 2)

    def hidden(a):
        return a.reshape(a.shape[0], -1, P, a.shape[-1]).transpose(2, 0, 1, 3)

    def padded(a):
        z = np.zeros((a.shape[0], 3 * P, D), np.float32)
        z[:, :F1] = a
        return z

    i, j = np.arange(P)[:, None], np.arange(P)[None, :]
    consts = fill(CONST, NCONST, ident=(i == j), before=(i < j), ones=np.ones((P, P)),
                  iota8=np.tile(np.arange(E), (P, 1)), iota64=np.tile(np.arange(S), (P, 1)),
                  slopes=np.tile(np.float32(2.0 ** -0.5) ** np.arange(1, H + 1), (P, 1)),
                  headmask=(i % 32 // HD == np.arange(4)[None]),
                  refloc=np.tile((i % S + np.arange(-3, 2)[None]), (1, H)))
    rows = np.concatenate([f["L0_xattn_bv"], f["L0_xattn_bu"], f["L1_xattn_b_v"], f["L1_xattn_b_o"],
                           f["L2_xattn_bv"], f["L2_xattn_boff"], f["L2_xattn_bo"], f["g_xattn"], f["g_ffn"]])[None]
    cols = fill(COLS, NCOLS, bq0=f["L0_xattn_bq"].reshape(8, P).T, bk0=f["L0_xattn_bk"].reshape(8, P).T,
                bq1=f["L1_xattn_b_q"][:, None], bk1=f["L1_xattn_b_k"][:, None], bq2=f["L2_xattn_bq"][:, None],
                bk2=f["L2_xattn_bk"][:, None], rb1=f["L0_ffn_rb1"].reshape(4, P).T, rb2=f["L0_ffn_rb2"][:, None],
                eb1=f["L0_ffn_eb1"].reshape(E * 4, P).T, gb3=f["L3_ffn_gate_b"][:, None],
                b13=f["L3_ffn_b1"].reshape(E * 4, P).T, eb2=f["L0_ffn_eb2"], b23=f["L3_ffn_b2"])
    shared_g = f["L2_ffn_ws_gate"].reshape(2, P, D)
    shared_u = f["L2_ffn_ws_up"].reshape(2, P, D)
    shared_d = f["L2_ffn_ws_down"].reshape(D, 2, P).transpose(1, 0, 2)

    def swap(a):
        return a.transpose(0, 2, 1)

    return {
        "x": tokens(f["x"].reshape(B * S, D)),
        "ctx_t": np.ascontiguousarray(f["ctx_1024"].reshape(B * S, D).T),
        "wa0": fill(WA0, NWA0, q=f["L0_xattn_Wq"], k=f["L0_xattn_Wk"], v=f["L0_xattn_Wv"], u=chunks(f["L0_xattn_Wu"])),
        "wsa": fill(WSA, NWSA, q1=f["L1_xattn_w_q"].T, k1=f["L1_xattn_w_k"].T, v1=f["L1_xattn_w_v"].T,
                    o1=f["L1_xattn_w_o"].T, q2=f["L2_xattn_Wq"].T, k2=f["L2_xattn_Wk"].T, v2=f["L2_xattn_Wv"].T,
                    off2=f["L2_xattn_Woff"].T, o2=f["L2_xattn_Wo"].T, q3=f["L3_xattn_W_q"].T,
                    k3=f["L3_xattn_W_k"].T, v3=f["L3_xattn_W_v"].T, o3=f["L3_xattn_W_o"].T),
        "wf0": fill(WF0, NWF0, rw1=f["L0_ffn_rw1"], rw2=chunks(f["L0_ffn_rw2"]), w1=experts(f["L0_ffn_ew1"]),
                    w2=hidden(f["L0_ffn_ew2"])),
        "wf1": fill(WF1, NWF1, router=f["L1_ffn_router_DE"],
                    w1=experts(np.concatenate([f["L1_ffn_w1_eDF"], f["L1_ffn_ws1_DF"][None]])),
                    w3=experts(np.concatenate([f["L1_ffn_w3_eDF"], f["L1_ffn_ws3_DF"][None]])),
                    w2=hidden(padded(np.concatenate([f["L1_ffn_w2_eFD"], f["L1_ffn_ws2_FD"][None]])))),
        "wf2": fill(WF2, NWF2, router=f["L2_ffn_gate_w"].T,
                    w1=experts(swap(np.concatenate([f["L2_ffn_we_gate"], shared_g]))),
                    w3=experts(swap(np.concatenate([f["L2_ffn_we_up"], shared_u]))),
                    w2=experts(swap(np.concatenate([f["L2_ffn_we_down"], shared_d])))),
        "wf3": fill(WF3, NWF3, router=f["L3_ffn_gate_w"].T, w1=experts(swap(f["L3_ffn_w1"])),
                    w2=hidden(swap(f["L3_ffn_w2"]))),
        "rows": rows, "cols": cols, "consts": consts,
        "mask2": f["mask_BxS2_if0"], "qpos": tokens(f["itok_BxS_8_8191"].reshape(B * S, 1)),
        "kpos": f["itok_BxS2_1_8191"], "maskq": tokens(f["mask_BxSxS2_if1"].reshape(B * S, S)),
    }


def kernel(**inputs):
    import concourse.bacc as bacc
    from concourse.bass_utils import run_bass_kernel_spmd

    nc = bacc.Bacc("TRN2", target_bir_lowering=False, num_devices=1)
    arrays = {f"in_{k}": np.ascontiguousarray(v) for k, v in arrays_of(inputs).items()}
    args = [nc.dram_tensor(k, v.shape, mybir.dt.from_np(v.dtype), kind="ExternalInput").ap() for k, v in arrays.items()]
    out = nc.dram_tensor("out", (P, NT * D), F32, kind="ExternalOutput").ap()
    flamingo(nc, *args, out)
    got = run_bass_kernel_spmd(nc, [arrays], core_ids=[0]).results[0]["out"]
    return np.ascontiguousarray(got.reshape(P, NT, D).transpose(1, 0, 2)).reshape(B, S, D)
```

```python
from contextlib import ExitStack

import numpy as np
import concourse.bass as bass
from concourse import mybir

ALU = mybir.AluOpType
ACT = mybir.ActivationFunctionType
AX = mybir.AxisListType
F32 = mybir.dt.float32
I32 = mybir.dt.int32

P = 128
B, S, D = 64, 64, 128
NT = B * S // P
GT = 4
NG = NT // GT
GW = GT * P
H = 16
HP = H // 2
HD0 = 64
HD = 8
NK = 5
E = 8
CAP0, CAP2 = 512, 1280
F1 = 352
F1C = [(0, 128), (128, 128), (256, 96)]
EPS = 1e-5
MAGIC = 12582912.0
BIG = 1000.0


def layout(*fields):
    at, n = {}, 0
    for name, width in fields:
        at[name] = (n, n + width)
        n += width
    return at, n


CONST, NCONST = layout(("part", 1), ("ident", P), ("before", P), ("ones", P), ("iota8", E), ("iota64", S),
                       ("slopes", H), ("headmask", 4), ("refloc", H * NK))
ROWS, NROWS = layout(("bv0", 1024), ("bu0", D), ("bv1", D), ("bo1", D), ("bv2", D), ("boff", H * NK),
                     ("bo2", D), ("g", 8))
COLS, NCOLS = layout(("bq0", 8), ("bk0", 8), ("bq1", 1), ("bk1", 1), ("bq2", 1), ("bk2", 1), ("rb1", 4),
                     ("rb2", 1), ("gb3", 1))
WA0, NWA0 = layout(("q", 1024), ("k", 1024), ("v", 1024), ("u", 1024))
WSA, NWSA = layout(("q1", D), ("k1", D), ("v1", D), ("o1", D), ("q2", D), ("k2", D), ("v2", D),
                   ("off2", H * NK), ("o2", D), ("q3", D), ("k3", D), ("v3", D), ("o3", D))
WF2, NWF2 = layout(("router", E), ("w1", 10 * D), ("w3", 10 * D), ("w2", 10 * D))

BT = 2
BW = BT * P
NB = -(-(NT // BT + E - 1) // 4) * 4
NB0 = E * CAP0 // BW
WX1, NWX1 = layout(("w1", F1), ("w3", F1), ("w2", 3 * D))
WS1, NWS1 = layout(("router", E), ("w1", F1), ("w3", F1), ("w2", 3 * D))
WF1, NWF1 = layout(("slots", NB * BW), ("wa", NWX1), ("wb", NWX1), ("router", E), ("w1", F1), ("w3", F1),
                   ("w2", 3 * D))
WY1, NWY1 = layout(("back", NT * D), ("wc", NWX1), ("wd", NWX1))
WX3, NWX3 = layout(("w1", 512), ("w2", 512), ("b1", 4), ("b2", D))
WS0, NWS0 = layout(("rw1", 512), ("rw2", 4 * E))
WF0, NWF0 = layout(("slots", NB0 * BW), ("rw1", 512), ("rw2", 4 * E), ("wa", NWX3), ("wb", NWX3),
                   ("wc", NWX3))
WY0, NWY0 = layout(("back", 2 * NT * D), ("wd", NWX3))
WF3, NWF3 = layout(("slots", NB * BW), ("wa", NWX3), ("wb", NWX3), ("router", E))
WY3, NWY3 = layout(("back", NT * D), ("wc", NWX3), ("wd", NWX3))
SLAB0 = max(NWF0, NWF2 + H * NK * S, NWY1, NWY3)
SLAB1 = max(NWA0, NWY0, NWF1, NWF3, 2 * H * NK * S)


class Ffn:

    def __init__(self, layer, experts, chunks, gated, sets, cap, softmax, topk):
        self.layer, self.experts, self.chunks, self.gated = layer, experts, chunks, gated
        self.sets, self.cap, self.softmax, self.topk = sets, cap, softmax, topk
        self.jobs = experts * len(chunks)
        self.ys = experts


FFNS = [
    Ffn(0, 0, [(128 * c, 128) for c in range(4)], False, 2, CAP0, "top", 2),
    Ffn(1, 1, F1C, True, 1, None, None, 1),
    Ffn(2, 10, [(0, 128)], True, 2, CAP2, "all", 2),
    Ffn(3, 8, [(128 * c, 128) for c in range(4)], False, 2, None, None, 1),
]

SEMAPHORES = """x_start_loaded x_loaded ctx_loaded wa0_loaded wsa_loaded rows_loaded cols_loaded consts_loaded
w0_loaded w1_loaded w2_loaded w3_loaded mask2_loaded qpos_loaded kpos_loaded maskq_loaded stored
gains_ready bias_ready lens_ready setup_steps route_exp_ready gates_ready
x_updated ln_stats_done ln_aggr_done ln_shifted ln_guessed newton_steps xn_centred xn_ready xn_turned xt_group_ready xt_tile_ready
ctx_staged q_projected k_projected v_projected q_ready k_ready v_ready kexp_ready scores_ready scores_copied
row_max_ready scores_centred exp_ready exp_sum_ready exp_recip_ready probs_ready probs_turned probs_t_ready
heads_summed heads_ready heads_scaled qs_ready ks_ready vs_projected cdup_staged vm_ready sum_plus_one heads_turned heads_t_ready out_projected x_biased
attention_zeroed dist_ready dist_steps bias_scaled biased_ready
qk_projected values_projected offsets_projected offsets_ready position_steps positions_ready distance_ready near_ready hat_abs_ready half_hat_ready
sampled_half sampled_max sampled_centred sampled_exp sampled_sum sampled_recip weights_ready hat_weighted_pool
hat_weighted_dve product_ready base_ready
hidden_full gate_silu_ready hidden_relu_ready hidden_gated_ready expert_summed expert_added
logits_t_full logits_t_ready logits_turned logits_ready comb_staged
route_steps mask_ready prefix_ready comb_ready pe_passed dve_passed act_passed pool_passed
block_silu_ready block_gated_ready rows_scaled shared_added newton_steps_dve rows_normalised rows_kept first_choice_added zeros_ready slots_zeroed slots_ready rows_scattered block_turned block_t_ready block_hidden_full block_relu_ready block_chunk_full
block_summed block_copied sums_stored rows_loaded_0 rows_loaded_1 rows_loaded_2 rows_loaded_3
weights_gathered_0 weights_gathered_1 weights_gathered_2 weights_gathered_3""".split() + [
    f"rows_back_{g}" for g in range(NG)]


def flamingo(nc, x_in, ctx_t, wa0, wsa, ws0, ws1, wf2, experts0, experts1, router3, experts3, rows_in, cols_in, consts_in, mask2, qpos, kpos, maskq,
             out, stop_after=8):
    with ExitStack() as stack:
        def sb(name, width, dt=F32):
            return stack.enter_context(nc.sbuf_tensor(name, [P, width], dt))

        sem = {n: stack.enter_context(nc.semaphore(n)) for n in SEMAPHORES}

        x_sb = sb("x_sb", NT * D)
        xt_sb = sb("xt_sb", NT * P)
        ctx_sb = sb("ctx_sb", NT * P)
        xn_sb = sb("xn_sb", NT * D)
        slab0 = sb("slab0", SLAB0)
        slab1 = sb("slab1", SLAB1)
        wsa_sb = sb("wsa_sb", NWSA)
        rows_sb = sb("rows_sb", NROWS)
        cols_sb = sb("cols_sb", NCOLS)
        const_sb = sb("const_sb", NCONST)
        gain_sb = sb("gain_sb", 8)
        gbias_sb = sb("gbias_sb", 3 * D)
        stats_sb = sb("stats_sb", GT * 6)
        moments_sb = sb("moments_sb", GT * 2)
        shift_sb = sb("shift_sb", GT, I32)
        rstd_sb = sb("rstd_sb", GT)
        newt_sb = sb("newt_sb", GT)
        xns_sb = sb("xns_sb", GW)
        comb_sb = sb("comb_sb", NT * E)
        m1_sb = sb("m1_sb", NT)
        rs_sb = sb("rs_sb", 4 * H)
        lens_sb = sb("lens_sb", NT)
        rlens_sb = sb("rlens_sb", NT)
        qpos_sb = sb("qpos_sb", NT, I32)
        xb_sb = sb("xb_sb", D)
        arena = sb("arena", 10700)
        zeros_sb = sb("zeros_sb", D)
        slot_sb = sb("slot_sb", NT, I32)
        wrow_sb = sb("wrow_sb", NB, I32)
        ps = stack.enter_context(nc.psum_tensor("ps", [P, 4096], F32))
        slot0_sb = sb("slot0_sb", 2 * NT, I32)
        from0_sb = sb("from0_sb", 2 * NT, I32)
        weight0_sb = sb("weight0_sb", 2 * NT)
        slots_x = nc.dram_tensor("slots_x", (NB0 * BW + 2 * NT * P, D), F32, kind="Internal").ap()
        slots_y = nc.dram_tensor("slots_y", (NB * BW, D), F32, kind="Internal").ap()

        def view(t, table, name):
            a, b = table[name]
            return t[:, a:b]

        def const(name):
            return view(const_sb, CONST, name)

        def row(name):
            return view(rows_sb, ROWS, name)

        def col(name):
            return view(cols_sb, COLS, name)

        ident = const("ident")

        def bank(n, a=0, b=512):
            return ps[:, 512 * n + a:512 * n + b]

        used = [0]

        def cut(width):
            used[0] += width
            assert used[0] <= 10700
            return arena[:, used[0] - width:used[0]]

        qt0 = [cut(1024) for _ in range(2)]
        kt0 = [cut(1024) for _ in range(2)]
        v0 = [cut(1024) for _ in range(2)]
        e0 = [cut(1024) for _ in range(2)]
        pt0, ot0 = cut(1024), cut(1024)
        c0 = [cut(P) for _ in range(2)]
        used[0] = 0
        qt = [cut(P) for _ in range(2)]
        kt = [cut(P) for _ in range(2)]
        kexp = [cut(512) for _ in range(2)]
        cdup = [cut(4 * S) for _ in range(2)]
        vm = [cut(HP * 32) for _ in range(2)]
        ex = [cut(1024) for _ in range(2)]
        pt, ob, obt = cut(1024), cut(P), cut(P)
        prod = [cut(1024) for _ in range(2)]
        o80 = [cut(H * NK) for _ in range(9)]
        used[0] = 0
        hid = [cut(512) for _ in range(9)]
        gate = [cut(512) for _ in range(2)]
        acc, hid1c, gates, lgt = cut(512), cut(512), cut(512), cut(512)
        combs = cut(GT * E)
        rt = [cut(NT * E) for _ in range(8)]
        logit_sb = cut(NT * E)
        small = [cut(NT) for _ in range(3)]
        used[0] = 0
        xblk = [cut(BW) for _ in range(4)]
        xbt = [cut(BW) for _ in range(2)]
        hid3 = [cut(4 * BW) for _ in range(2)]
        assert used[0] <= 7 * 512
        hid1 = [hid[7], hid[8], hid1c]
        gate3 = [gates[:, 0:BW], gates[:, BW:]]

        hat = [slab1[:, 0:5120], slab1[:, 5120:10240]]

        def positive(value):
            return not isinstance(value, int) or value > 0


        def x_tiles(t, w):
            return x_sb[:, bass.ds(t * D, w * D)]

        def ln_dve(dve, n, t, w, first=False, own=False):
            if isinstance(n, int) and n == 0:
                dve.wait_ge(sem["x_start_loaded"], 16)
            elif first:
                dve.wait_ge(sem["x_loaded"], 16)
            else:
                dve.wait_ge(sem["x_updated"], n - NG + 1)
            if not own:
                dve.wait_ge(sem["xn_ready"], n)
                dve.sem_inc(sem["dve_passed"], 1)
            for u in range(w):
                i = dve.bn_stats(stats_sb[:, 6 * u:6 * u + 6], x_sb[:, bass.ds((t + u) * D, D)])
            i.then_inc(sem["ln_stats_done"], 1)
            dve.wait_ge(sem["ln_stats_done"], n + 1)
            dve.sem_inc(sem["dve_passed"], 1)
            for u in range(w):
                i = dve.bn_aggr(moments_sb[:, 2 * u:2 * u + 2], stats_sb[:, 6 * u:6 * u + 6])
            i.then_inc(sem["ln_aggr_done"], 1)
            dve.wait_ge(sem["ln_aggr_done"], n + 1)
            var = moments_sb[:, 0:2 * w].rearrange("p (w c) -> p w c", c=2)[:, :, 1]
            dve.tensor_scalar(newt_sb[:, 0:w], var, EPS, None, ALU.add).then_inc(sem["ln_shifted"], 1)
            dve.wait_ge(sem["ln_shifted"], 2 * n + 1)
            dve.tensor_scalar(shift_sb[:, 0:w], newt_sb[:, 0:w].bitcast(I32), 1, None,
                              ALU.logical_shift_right).then_inc(sem["ln_shifted"], 1)
            dve.wait_ge(sem["ln_shifted"], 2 * n + 2)
            dve.tensor_scalar(rstd_sb[:, 0:w].bitcast(I32), shift_sb[:, 0:w], -1.0, float(0x5F3759DF),
                              ALU.mult, ALU.add).then_inc(sem["ln_guessed"], 1)

        def ln_pool(pool, n, t, w, keep=None):
            pool.wait_ge(sem["ln_guessed"], n + 1)
            y, v, a = rstd_sb[:, 0:w], newt_sb[:, 0:w], shift_sb[:, 0:w].bitcast(F32)
            for k in range(3):
                pool.tensor_tensor(a, y, y, ALU.mult).then_inc(sem["newton_steps"], 1)
                pool.wait_ge(sem["newton_steps"], 12 * n + 4 * k + 1)
                pool.tensor_tensor(a, a, v, ALU.mult).then_inc(sem["newton_steps"], 1)
                pool.wait_ge(sem["newton_steps"], 12 * n + 4 * k + 2)
                pool.sem_inc(sem["pool_passed"], 1)
                pool.tensor_scalar(a, a, -0.5, 1.5, ALU.mult, ALU.add).then_inc(sem["newton_steps"], 1)
                pool.wait_ge(sem["newton_steps"], 12 * n + 4 * k + 3)
                pool.tensor_tensor(y, y, a, ALU.mult).then_inc(sem["newton_steps"], 1)
                pool.wait_ge(sem["newton_steps"], 12 * n + 4 * k + 4)
            pool.wait_ge(sem["xn_turned"], n)
            pool.sem_inc(sem["pool_passed"], 1)

            def wide(a):
                return a.unsqueeze(2).broadcast_to([P, w, D])

            def rows_of(a):
                return a.rearrange("p (w d) -> p w d", d=D)

            mean = moments_sb[:, 0:2 * w].rearrange("p (w c) -> p w c", c=2)[:, :, 0]
            xns = rows_of(xns_sb[:, 0:w * D])
            pool.tensor_tensor(xns, rows_of(x_tiles(t, w)), wide(mean), ALU.subtract).then_inc(sem["xn_centred"], 1)
            pool.wait_ge(sem["xn_centred"], n + 1)
            pool.tensor_tensor(xns, xns, wide(y), ALU.mult).then_inc(sem["xn_ready"], 1)
            if keep is not None:
                pool.wait_ge(sem["xn_ready"], n + 1)
                pool.sem_inc(sem["pool_passed"], 1)
                pool.tensor_copy(rows_of(keep[:, bass.ds(t * D, w * D)]), xns).then_inc(sem["rows_kept"], 1)

        def ln_all_dve(dve, m, n, t, w):
            y, v, a = rstd_sb[:, 0:w], newt_sb[:, 0:w], shift_sb[:, 0:w].bitcast(F32)
            dve.wait_ge(sem["ln_guessed"], n + 1)
            for k in range(3):
                dve.tensor_tensor(a, y, y, ALU.mult).then_inc(sem["newton_steps_dve"], 1)
                dve.wait_ge(sem["newton_steps_dve"], 12 * m + 4 * k + 1)
                dve.tensor_tensor(a, a, v, ALU.mult).then_inc(sem["newton_steps_dve"], 1)
                dve.wait_ge(sem["newton_steps_dve"], 12 * m + 4 * k + 2)
                dve.tensor_scalar(a, a, -0.5, 1.5, ALU.mult, ALU.add).then_inc(sem["newton_steps_dve"], 1)
                dve.wait_ge(sem["newton_steps_dve"], 12 * m + 4 * k + 3)
                dve.tensor_tensor(y, y, a, ALU.mult).then_inc(sem["newton_steps_dve"], 1)
                dve.wait_ge(sem["newton_steps_dve"], 12 * m + 4 * k + 4)
            if positive(n):
                dve.wait_ge(sem["xn_turned"], n)
            dve.sem_inc(sem["dve_passed"], 1)
            for u in range(w):
                i = dve.tensor_scalar(xns_sb[:, u * D:(u + 1) * D], x_tiles(t + u, 1),
                                      moments_sb[:, 2 * u:2 * u + 1], rstd_sb[:, u:u + 1], ALU.subtract, ALU.mult)
            i.then_inc(sem["rows_normalised"], 1)

        def updates(n):
            return n - NG + 1

        def ln_pe(pe, n, out_ps, w):
            pe.wait_ge(sem["xn_ready"], n + 1)
            for u in range(w):
                i = pe.transpose(out_ps[:, u * P:(u + 1) * P], xns_sb[:, u * D:(u + 1) * D], ident)
            i.then_inc(sem["xn_turned"], 1)

        def ln_act(act, n, out_ps, t, w):
            act.wait_ge(sem["xn_turned"], n + 1)
            act.activation(xt_sb[:, bass.ds(t * P, w * P)], out_ps[:, 0:w * P], ACT.Copy).then_inc(
                sem["xt_group_ready" if w == GT else "xt_tile_ready"], w)

        def ln_number_attn(layer, t):
            return NG + (NT + NG) * layer + t

        def ln_number_ffn(layer, g):
            return NG + (NT + NG) * layer + NT + g

        def steps(eng, lag, step, ahead=0):
            first = lag + 1
            last = first + (NT - ahead - first) // 2 * 2
            for u in range(first):
                step(u, u % 2)
            with eng.Fori(0, (last - first) // 2) as i:
                u = i * 2 + first
                step(u, first % 2)
                step(u + 1, (first + 1) % 2)
            for u in range(last, NT + lag):
                step(u, u % 2)

        def on(u, back):
            return not isinstance(u, int) or 0 <= u - back < NT

        def a0_w(name):
            return view(slab1, WA0, name)

        Q0 = ps[:, 0:1024]
        K0 = ps[:, 1024:2048]
        T0 = ps[:, 2048:3072]
        S0 = ps[:, 3072:4096]

        def a0_pe(pe):
            pe.wait_ge(sem["wa0_loaded"], 16)

            def query(t):
                pe.wait_ge(sem["xt_group_ready"], t + 1)
                if positive(t):
                    pe.wait_ge(sem["v_ready"], t)
                for c in range(8):
                    i = pe.matmul(Q0[:, c * P:(c + 1) * P], a0_w("q")[:, c * P:(c + 1) * P],
                                  xt_sb[:, bass.ds(t * P, P)], start=True, stop=True)
                i.then_inc(sem["q_projected"], 1)

            def key(t, p):
                pe.wait_ge(sem["ctx_staged"], t + 1)
                if positive(t - 2):
                    pe.wait_ge(sem["heads_ready"], t - 2)
                for c in range(8):
                    i = pe.matmul(K0[:, c * P:(c + 1) * P], a0_w("k")[:, c * P:(c + 1) * P], c0[p],
                                  start=True, stop=True)
                i.then_inc(sem["k_projected"], 1)

            def value(t, p):
                pe.wait_ge(sem["q_ready"], t + 1)
                for j in range(2):
                    i = pe.matmul(Q0[:, j * 512:(j + 1) * 512], c0[p], a0_w("v")[:, j * 512:(j + 1) * 512],
                                  start=True, stop=True)
                i.then_inc(sem["v_projected"], 1)

            def step(u, p):
                t = u - 1
                if isinstance(u, int) and u == 0:
                    query(0)
                    key(0, 0)
                    value(0, 0)
                if on(u, 0):
                    pe.wait_ge(sem["q_ready"], u + 1)
                    pe.wait_ge(sem["k_ready"], u + 1)
                    if positive(u):
                        pe.wait_ge(sem["scores_centred"], u)
                    pe.sem_inc(sem["pe_passed"], 1)
                    for h2 in range(2):
                        h = slice(64 * h2, 64 * h2 + 64)
                        for c in range(8):
                            for b in range(2):
                                at = slice(c * P + b * 64, c * P + b * 64 + 64)
                                i = pe.matmul(S0[h, at], qt0[p][h, at], kt0[p][h, at], start=True, stop=True)
                    i.then_inc(sem["scores_ready"], 1)
                if on(u, -1):
                    query(u + 1)
                if on(u, 2):
                    pe.wait_ge(sem["heads_ready"], u - 1)
                    for c in range(8):
                        i = pe.matmul(T0[:, 0:P], ot0[:, c * P:(c + 1) * P],
                                      a0_w("u")[:, c * P:(c + 1) * P], start=c == 0, stop=c == 7)
                    i.then_inc(sem["out_projected"], 1)
                if on(u, -1):
                    key(u + 1, 1 - p)
                if on(u, 1):
                    pe.wait_ge(sem["probs_ready"], t + 1)
                    if positive(updates(ln_number_attn(0, t - 1))):
                        pe.wait_ge(sem["x_updated"], updates(ln_number_attn(0, t - 1)))
                    if positive(t - 1):
                        pe.wait_ge(sem["xt_tile_ready"], t - 1)
                    for c in range(8):
                        i = pe.transpose(T0[:, c * P:(c + 1) * P], e0[1 - p][:, c * P:(c + 1) * P], ident)
                    i.then_inc(sem["probs_turned"], 1)
                if on(u, -1):
                    value(u + 1, 1 - p)
                if on(u, 1):
                    pe.wait_ge(sem["v_ready"], t + 1)
                    pe.wait_ge(sem["probs_t_ready"], t + 1)
                    if on(u, -1):
                        pe.wait_ge(sem["k_ready"], u + 2)
                    else:
                        pe.wait_ge(sem["heads_ready"], t)
                    pe.sem_inc(sem["pe_passed"], 1)
                    for b in range(2):
                        r = slice(64 * b, 64 * b + 64)
                        for c in range(8):
                            for h2 in range(2):
                                i = pe.matmul(K0[64 * h2:64 * h2 + 64, b * 512 + c * 64:b * 512 + c * 64 + 64],
                                              v0[1 - p][r, c * P + h2 * 64:c * P + h2 * 64 + 64],
                                              pt0[r, c * P + h2 * 64:c * P + h2 * 64 + 64], start=True, stop=True)
                    i.then_inc(sem["heads_summed"], 1)
                if on(u, 2):
                    if not on(u, 1):
                        pe.wait_ge(sem["xt_tile_ready"], u - 2)
                    ln_pe(pe, ln_number_attn(0, u - 2), T0[:, 512:640], 1)
            steps(pe, 2, step, 2)

        def a0_dve(dve):
            def evict(src, dst, bias, ready, full, t):
                dve.wait_ge(sem[full], t + 1)
                dve.tensor_tensor(dst.rearrange("p (c t) -> p c t", c=8), src.rearrange("p (c t) -> p c t", c=8),
                                  bias, ALU.add).then_inc(sem[ready], 1)

            def evict_q(t, p):
                evict(Q0, qt0[p], col("bq0").unsqueeze(2).broadcast_to([P, 8, P]), "q_ready", "q_projected", t)

            def evict_k(t, p):
                evict(K0, kt0[p], col("bk0").unsqueeze(2).broadcast_to([P, 8, P]), "k_ready", "k_projected", t)

            def evict_v(t, p):
                evict(Q0, v0[p], row("bv0").rearrange("p (c t) -> p c t", c=8), "v_ready", "v_projected", t)

            def step(u, p):
                t = u - 1
                if isinstance(u, int) and u == 0:
                    evict_q(0, 0)
                    evict_k(0, 0)
                    evict_v(0, 0)
                if on(u, 1):
                    o = e0[1 - p].rearrange("p (h t) -> p h t", h=H)
                    dve.wait_ge(sem["exp_ready"], t + 1)
                    if positive(t):
                        dve.wait_ge(sem["probs_ready"], t)
                    dve.tensor_reduce(rs_sb[:, H:2 * H], o, AX.X, ALU.add).then_inc(sem["exp_sum_ready"], 1)
                    dve.wait_ge(sem["exp_sum_ready"], t + 1)
                    dve.reciprocal(rs_sb[:, 2 * H:3 * H], rs_sb[:, H:2 * H]).then_inc(sem["exp_recip_ready"], 1)
                if on(u, 0):
                    s = S0.rearrange("p (h t) -> p h t", h=H)
                    dve.wait_ge(sem["scores_ready"], u + 1)
                    dve.tensor_reduce(rs_sb[:, 0:H], s, AX.X, ALU.max).then_inc(sem["row_max_ready"], 1)
                    dve.wait_ge(sem["row_max_ready"], u + 1)
                    dve.tensor_tensor(e0[p].rearrange("p (h t) -> p h t", h=H), s,
                                      rs_sb[:, 0:H].unsqueeze(2).broadcast_to([P, H, S]),
                                      ALU.subtract).then_inc(sem["scores_centred"], 1)
                if on(u, -1):
                    evict_q(u + 1, 1 - p)
                if on(u, 2):
                    dve.wait_ge(sem["out_projected"], u - 1)
                    dve.wait_ge(sem["x_biased"], u - 1)
                    dve.scalar_tensor_tensor(x_tiles(u - 2, 1), T0[:, 0:P], gain_sb[:, 0:1], xb_sb[:], ALU.mult,
                                             ALU.add).then_inc(sem["x_updated"], 1)
                    ln_dve(dve, ln_number_attn(0, u - 2), u - 2, 1)
                if on(u, -1):
                    evict_k(u + 1, 1 - p)
                    if positive(u):
                        dve.wait_ge(sem["heads_summed"], u)
                    dve.sem_inc(sem["dve_passed"], 1)
                    evict_v(u + 1, 1 - p)
            steps(dve, 2, step, 2)

        def a0_act(act):
            def step(u, p):
                t = u - 1
                if on(u, 0):
                    act.wait_ge(sem["scores_centred"], u + 1)
                    act.activation(e0[p], e0[p], ACT.Exp, scale=HD0 ** -0.5).then_inc(sem["exp_ready"], 1)
                if on(u, 1):
                    act.wait_ge(sem["probs_turned"], t + 1)
                    act.activation(pt0, T0, ACT.Copy).then_inc(sem["probs_t_ready"], 1)
                    act.wait_ge(sem["heads_summed"], t + 1)
                    act.activation(ot0.rearrange("p (c b q) -> p b c q", c=8, b=2),
                                   K0.rearrange("p (b c q) -> p b c q", b=2, c=8),
                                   ACT.Copy).then_inc(sem["heads_ready"], 1)
                if on(u, 2):
                    ln_act(act, ln_number_attn(0, u - 2), T0[:, 512:640], u - 2, 1)
            steps(act, 2, step, 2)

        def a0_pool(pool):
            def stage(t, p):
                if positive(t - 1):
                    pool.wait_ge(sem["v_projected"], t - 1)
                pool.tensor_copy(c0[p], ctx_sb[:, bass.ds(t * P, P)]).then_inc(sem["ctx_staged"], 1)

            def step(u, p):
                if isinstance(u, int) and u == 0:
                    pool.wait_ge(sem["lens_ready"], 1)
                    stage(0, 0)
                    stage(1, 1)
                if on(u, 1):
                    t, o = u - 1, e0[1 - p].rearrange("p (h t) -> p h t", h=H)
                    pool.wait_ge(sem["exp_recip_ready"], t + 1)
                    pool.tensor_tensor(o, o, rs_sb[:, 2 * H:3 * H].unsqueeze(2).broadcast_to([P, H, S]),
                                       ALU.mult).then_inc(sem["probs_ready"], 1)
                if on(u, -2):
                    stage(u + 2, p)
                if on(u, 2):
                    ln_pool(pool, ln_number_attn(0, u - 2), u - 2, 1, keep=xn_sb)
                if on(u, 1):
                    if positive(updates(ln_number_attn(0, t - 1))):
                        pool.wait_ge(sem["x_updated"], updates(ln_number_attn(0, t - 1)))
                    pool.sem_inc(sem["pool_passed"], 1)
                    pool.tensor_tensor(xb_sb[:], x_sb[:, bass.ds(t * D, D)], gbias_sb[:, 0:D],
                                       ALU.add).then_inc(sem["x_biased"], 1)
            steps(pool, 2, step, 2)

        USED_IN = dict(qs_ready=(1, 2, 3), ks_ready=(1, 2, 3), kexp_ready=(1, 2, 3), heads_scaled=(1, 2, 3),
                       heads_turned=(1, 2, 3), heads_t_ready=(1, 2, 3), biased_ready=(3,), bias_scaled=(3,),
                       vs_projected=(1, 3), cdup_staged=(1, 2, 3), vm_ready=(1, 2, 3), scores_centred=(0, 1, 3),
                       scores_ready=(0, 1, 2, 3), row_max_ready=(0, 1, 3), exp_ready=(0, 1, 3),
                       exp_sum_ready=(0, 1, 3), exp_recip_ready=(0, 1, 3), probs_turned=(0, 1, 2, 3),
                       probs_t_ready=(0, 1, 2, 3), heads_summed=(0, 1, 2, 3), out_projected=(0, 1, 2, 3),
                       x_biased=(0, 1, 2), sum_plus_one=(3,),
                       **{n: (2,) for n in ("qk_projected", "values_projected", "offsets_projected", "offsets_ready", "positions_ready",
                                            "distance_ready", "near_ready", "hat_abs_ready", "half_hat_ready", "scores_copied",
                                            "sampled_half", "sampled_max", "sampled_centred", "sampled_exp",
                                            "sampled_sum", "sampled_recip", "weights_ready", "hat_weighted_pool",
                                            "hat_weighted_dve", "product_ready")})

        def past(layer, name):
            return NT * sum(l < layer for l in USED_IN[name])

        XB = bank(0)
        SB = ps[:, 512:2560].rearrange("p (r x) -> p r x", r=4)[:, :, 0:256]
        PTB = ps[:, 2560:3584]
        OB = bank(7)

        def w_attn(layer, name):
            return view(wsa_sb, WSA, f"{name}{layer}")

        def halves():
            return [slice(0, 64), slice(64, 128)]

        def narrow_project(pe, L, u, p):
            pe.matmul(XB[:, 0:P], w_attn(L, "q"), xt_sb[:, bass.ds(u * P, P)], start=True, stop=True)
            pe.matmul(XB[:, P:2 * P], w_attn(L, "k"), ctx_sb[:, bass.ds(u * P, P)], start=True, stop=True)
            for b in range(2):
                i = pe.matmul(XB[:, 256 + b * P:256 + (b + 1) * P], cdup[p][:, b * P:(b + 1) * P],
                              w_attn(L, "v"), start=True, stop=True)
            i.then_inc(sem["vs_projected"], 1)

        def narrow_scores(pe, p):
            for r in range(4):
                rows = slice(32 * r, 32 * r + 32)
                for b in range(2):
                    i = pe.matmul(SB[64 * b:64 * b + 64, r, :], qt[p][rows, 64 * b:64 * b + 64],
                                  kexp[p][rows, 256 * b:256 * b + 256], start=True, stop=True)
            i.then_inc(sem["scores_ready"], 1)

        def narrow_heads(pe, L, t, old_p):
            pe.wait_ge(sem["vm_ready"], t + 1 + past(L, "vm_ready"))
            pe.wait_ge(sem["x_updated"], updates(ln_number_attn(L, t - 1)))
            for c in range(HP):
                i = pe.matmul(OB[:, c * 32:(c + 1) * 32], pt[:, c * P:(c + 1) * P],
                              vm[old_p][:, c * 32:(c + 1) * 32], start=True, stop=True)
            i.then_inc(sem["heads_summed"], 1)

        def narrow_turn_heads(pe, L, t):
            pe.wait_ge(sem["heads_scaled"], t + 1 + past(L, "heads_scaled"))
            pe.transpose(OB[:, 256:384], ob, ident).then_inc(sem["heads_turned"], 1)

        def narrow_output(pe, L, t):
            pe.wait_ge(sem["heads_t_ready"], t + 1 + past(L, "heads_t_ready"))
            pe.matmul(OB[:, 384:512], obt, w_attn(L, "o"), start=True, stop=True).then_inc(sem["out_projected"], 1)

        def narrow_evict_qk(act, L, u, p):
            act.wait_ge(sem["vs_projected"], u + 1 + past(L, "vs_projected"))
            for dst, at, name, done in ((qt[p], 0, "bq", "qs_ready"), (kt[p], P, "bk", "ks_ready")):
                if L == 3:
                    i = act.activation(dst, XB[:, at:at + P], ACT.Copy)
                else:
                    i = act.activation(dst, XB[:, at:at + P], ACT.Identity, bias=col(f"{name}{L}"))
                i.then_inc(sem[done], 1)

        def narrow_values(dve, L, u, p):
            dve.wait_ge(sem["ks_ready"], u + 1 + past(L, "ks_ready"))
            dve.sem_inc(sem["dve_passed"], 1)
            for h2, r in enumerate(halves()):
                dst = vm[p][r].rearrange("p (c b h d) -> p h b c d", c=HP, b=2, h=2)[:, h2]
                src = XB[r, 256:512].rearrange("p (b c h d) -> p h b c d", b=2, c=HP, h=2)[:, h2]
                if L == 3:
                    i = dve.tensor_copy(dst, src)
                else:
                    bv = row(f"bv{L}")[r].rearrange("p (c h d) -> p h c d", c=HP, h=2)[:, h2]
                    i = dve.tensor_tensor(dst, src, bv.unsqueeze(1).broadcast_to([64, 2, HP, HD]), ALU.add)
            i.then_inc(sem["vm_ready"], 1)

        def narrow_scale(dve, L, t, recip):
            dve.wait_ge(sem["heads_summed"], t + 1 + past(L, "heads_summed"))
            for b, r in enumerate(halves()):
                i = dve.tensor_tensor(ob[r].rearrange("p (c h d) -> p c h d", c=HP, h=2),
                                      OB[r, 0:256].rearrange("p (c b h d) -> p b c h d", c=HP, b=2, h=2)[:, b],
                                      recip[r].rearrange("p (c h) -> p c h", h=2).unsqueeze(3).broadcast_to(
                                          [64, HP, 2, HD]), ALU.mult)
            i.then_inc(sem["heads_scaled"], 1)

        def narrow_update(dve, L, t):
            dve.wait_ge(sem["out_projected"], t + 1 + past(L, "out_projected"))
            if L == 3:
                res = x_tiles(t, 1)
            else:
                dve.wait_ge(sem["x_biased"], t + 1 + past(L, "x_biased"))
                res = xb_sb[:]
            dve.scalar_tensor_tensor(x_tiles(t, 1), OB[:, 384:512], gain_sb[:, L:L + 1], res, ALU.mult,
                                     ALU.add).then_inc(sem["x_updated"], 1)
            ln_dve(dve, ln_number_attn(L, t), t, 1)

        def narrow_stage(pool, L, t, p):
            if positive(t - 1 + past(L, "vs_projected")):
                pool.wait_ge(sem["vs_projected"], t - 1 + past(L, "vs_projected"))
            pool.tensor_copy(cdup[p].rearrange("p (b c t) -> p b c t", b=2, c=2),
                             ctx_sb[:, bass.ds(t * P, P)].rearrange("p (b t) -> p b t", b=2).unsqueeze(2).broadcast_to(
                                 [P, 2, 2, S])).then_inc(sem["cdup_staged"], 1)

        def narrow_expand(pool, L, u, p):
            pool.wait_ge(sem["ks_ready"], u + 1 + past(L, "ks_ready"))
            pool.tensor_tensor(kexp[p].rearrange("p (b h t) -> p b h t", b=2, h=4),
                               kt[p].rearrange("p (b t) -> p b t", b=2).unsqueeze(2).broadcast_to([P, 2, 4, S]),
                               const("headmask").unsqueeze(1).unsqueeze(3).broadcast_to([P, 2, 4, S]),
                               ALU.mult).then_inc(sem["kexp_ready"], 1)

        def narrow_bias_rows(pool, L, t):
            pool.wait_ge(sem["x_updated"], updates(ln_number_attn(L, t - 1)))
            pool.sem_inc(sem["pool_passed"], 1)
            pool.tensor_tensor(xb_sb[:], x_sb[:, bass.ds(t * D, D)], gbias_sb[:, L * D:(L + 1) * D],
                               ALU.add).then_inc(sem["x_biased"], 1)

        def zero_values(dve):
            dve.memset(vm[0], 0.0)
            dve.memset(vm[1], 0.0).then_inc(sem["attention_zeroed"], 1)

        def a13_pe(L):
            def program(pe):
                pe.wait_ge(sem["wsa_loaded"], 16)
                pe.wait_ge(sem["xt_group_ready"], (L + 1) * NT)

                def project(t, p):
                    pe.wait_ge(sem["cdup_staged"], t + 1 + past(L, "cdup_staged"))
                    if positive(t + past(L, "ks_ready")):
                        pe.wait_ge(sem["ks_ready"], t + past(L, "ks_ready"))
                    if positive(t + past(L, "vm_ready")):
                        pe.wait_ge(sem["vm_ready"], t + past(L, "vm_ready"))
                    narrow_project(pe, L, t, p)

                def step(u, p):
                    if isinstance(u, int) and u == 0:
                        project(0, 0)
                    if on(u, 0):
                        pe.wait_ge(sem["qs_ready"], u + 1 + past(L, "qs_ready"))
                        pe.wait_ge(sem["kexp_ready"], u + 1 + past(L, "kexp_ready"))
                        if positive(u + past(L, "biased_ready" if L == 3 else "scores_centred")):
                            pe.wait_ge(sem["biased_ready" if L == 3 else "scores_centred"], u + past(L, "biased_ready" if L == 3 else "scores_centred"))
                        pe.sem_inc(sem["pe_passed"], 1)
                        narrow_scores(pe, p)
                    if on(u, 2):
                        narrow_turn_heads(pe, L, u - 2)
                    if on(u, 1):
                        t = u - 1
                        pe.wait_ge(sem["exp_ready"], t + 1 + past(L, "exp_ready"))
                        pe.wait_ge(sem["xt_tile_ready"], u - 3 + L * NT)
                        for c in range(HP):
                            i = pe.transpose(PTB[:, c * P:(c + 1) * P], ex[1 - p][:, c * P:(c + 1) * P], ident)
                        i.then_inc(sem["probs_turned"], 1)
                    if on(u, 2):
                        narrow_output(pe, L, u - 2)
                    if on(u, -1):
                        project(u + 1, 1 - p)
                    if on(u, 1):
                        pe.wait_ge(sem["probs_t_ready"], u + past(L, "probs_t_ready"))
                        narrow_heads(pe, L, u - 1, 1 - p)
                    if on(u, 3):
                        if not on(u, 1):
                            pe.wait_ge(sem["xt_tile_ready"], u - 3 + L * NT)
                        ln_pe(pe, ln_number_attn(L, u - 3), PTB, 1)
                steps(pe, 3, step, 2)
            return program

        def a13_act(L):
            def program(act):
                def step(u, p):
                    if isinstance(u, int) and u == 0:
                        narrow_evict_qk(act, L, 0, 0)
                    if on(u, 2):
                        act.wait_ge(sem["heads_turned"], u - 1 + past(L, "heads_turned"))
                        act.activation(obt, OB[:, 256:384], ACT.Copy).then_inc(sem["heads_t_ready"], 1)
                    if on(u, 1):
                        act.wait_ge(sem["probs_turned"], u + past(L, "probs_turned"))
                        act.activation(pt, PTB, ACT.Copy).then_inc(sem["probs_t_ready"], 1)
                    if on(u, 0):
                        act.wait_ge(sem["scores_centred"], u + 1 + past(L, "scores_centred"))
                        act.activation(ex[p], ex[p], ACT.Exp, scale=1.0 if L == 3 else HD ** -0.5).then_inc(
                            sem["exp_ready"], 1)
                    if on(u, -1):
                        narrow_evict_qk(act, L, u + 1, 1 - p)
                    if on(u, 3):
                        ln_act(act, ln_number_attn(L, u - 3), PTB, u - 3, 1)
                steps(act, 3, step, 2)
            return program

        def a13_dve(L):
            def program(dve):
                zero_values(dve)
                dve.wait_ge(sem["attention_zeroed"], {1: 1, 3: 3}[L])

                def step(u, p):
                    t = u - 1
                    if isinstance(u, int) and u == 0:
                        narrow_values(dve, L, 0, 0)
                    if on(u, 1):
                        dve.wait_ge(sem["exp_ready"], t + 1 + past(L, "exp_ready"))
                        dve.tensor_reduce(rs_sb[:, H:2 * H], ex[1 - p].rearrange("p (h t) -> p h t", h=H), AX.X,
                                          ALU.add).then_inc(sem["exp_sum_ready"], 1)
                        dve.wait_ge(sem["exp_sum_ready"], t + 1 + past(L, "exp_sum_ready"))
                        if L == 3:
                            dve.tensor_scalar(rs_sb[:, H:2 * H], rs_sb[:, H:2 * H], 1.0, None, ALU.add).then_inc(
                                sem["sum_plus_one"], 1)
                            dve.wait_ge(sem["sum_plus_one"], t + 1 + past(L, "sum_plus_one"))
                        dve.reciprocal(rs_sb[:, 2 * H:3 * H], rs_sb[:, H:2 * H]).then_inc(sem["exp_recip_ready"], 1)
                    if on(u, 0):
                        dve.wait_ge(sem["scores_ready"], u + 1 + past(L, "scores_ready"))
                        s4 = SB
                        flat = ex[p].rearrange("p (r x) -> p r x", r=4)
                        if L == 3:
                            dve.wait_ge(sem["bias_scaled"], u + 1 + past(L, "bias_scaled"))
                            dve.scalar_tensor_tensor(flat, s4, float(np.float32(HD ** -0.5)),
                                                     prod[p].rearrange("p (r x) -> p r x", r=4), ALU.mult,
                                                     ALU.add).then_inc(sem["biased_ready"], 1)
                            dve.wait_ge(sem["biased_ready"], u + 1 + past(L, "biased_ready"))
                            s4 = flat
                        heads = s4.rearrange("p r (h t) -> p r h t", h=4)
                        dve.tensor_reduce(rs_sb[:, 0:H].rearrange("p (r h) -> p r h", r=4), heads, AX.X,
                                          ALU.max).then_inc(sem["row_max_ready"], 1)
                        dve.wait_ge(sem["row_max_ready"], u + 1 + past(L, "row_max_ready"))
                        dve.tensor_tensor(ex[p].rearrange("p (r h t) -> p r h t", r=4, h=4), heads,
                                          rs_sb[:, 0:H].rearrange("p (r h) -> p r h", r=4).unsqueeze(3).broadcast_to(
                                              [P, 4, 4, S]), ALU.subtract).then_inc(sem["scores_centred"], 1)
                    if on(u, 2):
                        narrow_update(dve, L, u - 2)
                    if on(u, 1):
                        dve.wait_ge(sem["exp_recip_ready"], t + 1 + past(L, "exp_recip_ready"))
                        narrow_scale(dve, L, t, rs_sb[:, 2 * H:3 * H])
                    if on(u, -1):
                        narrow_values(dve, L, u + 1, 1 - p)
                steps(dve, 3, step, 2)
            return program

        def a13_pool(L):
            def bias_of(pool, t, p):
                if positive(t - 1 + past(L, "biased_ready")):
                    pool.wait_ge(sem["biased_ready"], t - 1 + past(L, "biased_ready"))
                pool.sem_inc(sem["pool_passed"], 1)
                pool.tensor_tensor(prod[p].rearrange("p (h t) -> p h t", h=H),
                                   const("slopes").unsqueeze(2).broadcast_to([P, H, S]),
                                   xn_sb[:, bass.ds(t * S, S)].unsqueeze(1).broadcast_to([P, H, S]),
                                   ALU.mult).then_inc(sem["bias_scaled"], 1)

            def program(pool):
                if L == 3:
                    pool.wait_ge(sem["dist_steps"], 4)

                def step(u, p):
                    if isinstance(u, int) and u == 0:
                        narrow_stage(pool, L, 0, 0)
                        narrow_expand(pool, L, 0, 0)
                        narrow_stage(pool, L, 1, 1)
                        if L == 3:
                            bias_of(pool, 0, 0)
                    if on(u, -2):
                        narrow_stage(pool, L, u + 2, p)
                    if on(u, -1):
                        if L == 3:
                            bias_of(pool, u + 1, 1 - p)
                        narrow_expand(pool, L, u + 1, 1 - p)
                    if on(u, 2):
                        ln_pool(pool, ln_number_attn(L, u - 2), u - 2, 1, keep={1: xn_sb, 3: slab1}[L])
                    if on(u, 1) and L != 3:
                        narrow_bias_rows(pool, L, u - 1)
                steps(pool, 3, step, 2)
            return program

        PAIRS_POOL = 7
        NSAMP = H * NK
        NEAR = 16
        wbuf = slab0[:, NWF2:NWF2 + NSAMP * S]
        product = xn_sb[:, 0:NSAMP * S // 2]
        pos, samp, wgt, offs, base = o80[0], o80[1], o80[2], o80[3], o80[4]
        tmp = [o80[5], o80[6]]
        kscore = prod

        def a2_pe(pe):
            pe.wait_ge(sem["wsa_loaded"], 16)
            pe.wait_ge(sem["xt_group_ready"], 3 * NT)

            def queries_keys(t):
                if positive(t + past(2, "offsets_ready")):
                    pe.wait_ge(sem["offsets_ready"], t + past(2, "offsets_ready"))
                pe.matmul(XB[:, 0:P], w_attn(2, "q"), xt_sb[:, bass.ds(t * P, P)], start=True, stop=True)
                pe.matmul(XB[:, P:2 * P], w_attn(2, "k"), ctx_sb[:, bass.ds(t * P, P)], start=True,
                          stop=True).then_inc(sem["qk_projected"], 1)

            def offsets(t, p):
                pe.wait_ge(sem["ks_ready"], t + 1 + past(2, "ks_ready"))
                pe.sem_inc(sem["pe_passed"], 1)
                pe.matmul(XB[:, 0:NSAMP], qt[p], w_attn(2, "off"), start=True, stop=True).then_inc(
                    sem["offsets_projected"], 1)

            def step(u, p):
                if isinstance(u, int) and u == 0:
                    queries_keys(0)
                    offsets(0, 0)
                if on(u, 0):
                    pe.wait_ge(sem["qs_ready"], u + 1 + past(2, "qs_ready"))
                    pe.wait_ge(sem["kexp_ready"], u + 1 + past(2, "kexp_ready"))
                    if positive(u + past(2, "scores_copied")):
                        pe.wait_ge(sem["scores_copied"], u + past(2, "scores_copied"))
                    pe.sem_inc(sem["pe_passed"], 1)
                    narrow_scores(pe, p)
                if on(u, 3):
                    narrow_turn_heads(pe, 2, u - 3)
                pe.wait_ge(sem["xt_tile_ready"], u - 3 + 2 * NT)
                if on(u, 1):
                    pe.wait_ge(sem["cdup_staged"], u + past(2, "cdup_staged"))
                    pe.wait_ge(sem["offsets_ready"], u + 1 if on(u, 0) else NT + past(2, "offsets_ready"))
                    pe.sem_inc(sem["pe_passed"], 1)
                    for b in range(2):
                        i = pe.matmul(XB[:, 256 + b * P:256 + (b + 1) * P], cdup[1 - p][:, b * P:(b + 1) * P],
                                      w_attn(2, "v"), start=True, stop=True)
                    i.then_inc(sem["values_projected"], 1)
                if on(u, -1):
                    queries_keys(u + 1)
                if on(u, 3):
                    narrow_output(pe, 2, u - 3)
                if on(u, -1):
                    if on(u, 1):
                        pe.wait_ge(sem["vm_ready"], u + past(2, "vm_ready"))
                    offsets(u + 1, 1 - p)
                if on(u, 2):
                    pe.wait_ge(sem["hat_weighted_pool"], u - 1 + past(2, "hat_weighted_pool"))
                    pe.wait_ge(sem["hat_weighted_dve"], u - 1 + past(2, "hat_weighted_dve"))
                    pe.wait_ge(sem["probs_t_ready"], u - 2 + past(2, "probs_t_ready"))
                    for c in range(HP):
                        for k in range(NK):
                            at = (c * NK + k) * P
                            i = pe.matmul(PTB[:, c * P:(c + 1) * P], wbuf[:, at:at + P], ident, start=k == 0,
                                          stop=k == NK - 1)
                    i.then_inc(sem["probs_turned"], 1)
                    pe.wait_ge(sem["probs_t_ready"], u - 1 + past(2, "probs_t_ready"))
                    narrow_heads(pe, 2, u - 2, p)
                if on(u, 3):
                    if on(u, -1):
                        pe.wait_ge(sem["offsets_ready"], u + 2 + past(2, "offsets_ready"))
                    elif on(u, 1):
                        pe.wait_ge(sem["vm_ready"], u + past(2, "vm_ready"))
                    ln_pe(pe, ln_number_attn(2, u - 3), XB, 1)
            steps(pe, 3, step, 1)

        def a2_act(act):
            def queries_keys(t, p):
                act.wait_ge(sem["qk_projected"], t + 1 + past(2, "qk_projected"))
                act.activation(qt[p], XB[:, 0:P], ACT.Identity, bias=col("bq2")).then_inc(sem["qs_ready"], 1)
                act.activation(kt[p], XB[:, P:2 * P], ACT.Identity, bias=col("bk2")).then_inc(sem["ks_ready"], 1)

            def step(u, p):
                if isinstance(u, int) and u == 0:
                    queries_keys(0, 0)
                if on(u, 0):
                    act.wait_ge(sem["scores_ready"], u + 1 + past(2, "scores_ready"))
                    if positive(2 * (u - 1) + past(2, "product_ready")):
                        act.wait_ge(sem["product_ready"], 2 * (u - 1) + past(2, "product_ready"))
                    act.activation(kscore[p].rearrange("p (r x) -> p r x", r=4), SB, ACT.Copy,
                                   scale=float(np.float32(0.5 * HD ** -0.5))).then_inc(sem["scores_copied"], 1)
                if on(u, 3):
                    act.wait_ge(sem["heads_turned"], u - 2 + past(2, "heads_turned"))
                    act.activation(obt, OB[:, 256:384], ACT.Copy).then_inc(sem["heads_t_ready"], 1)
                if on(u, -1):
                    queries_keys(u + 1, 1 - p)
                if on(u, 0):
                    act.wait_ge(sem["positions_ready"], u + 1 + past(2, "positions_ready"))
                    if positive(u - 1 + past(2, "hat_weighted_pool")):
                        act.wait_ge(sem["hat_weighted_pool"], u - 1 + past(2, "hat_weighted_pool"))
                    if positive(u - 1 + past(2, "hat_weighted_dve")):
                        act.wait_ge(sem["hat_weighted_dve"], u - 1 + past(2, "hat_weighted_dve"))
                    act.sem_inc(sem["act_passed"], 1)
                    for k in range(NSAMP - NEAR, NSAMP):
                        i = act.activation(hat[p][:, k * S:(k + 1) * S], const("iota64"), ACT.Abs, scale=-1.0,
                                           bias=pos[:, k:k + 1])
                    i.then_inc(sem["near_ready"], 1)
                    far = hat[p][:, 0:(NSAMP - NEAR) * S]
                    act.wait_ge(sem["distance_ready"], u + 1 + past(2, "distance_ready"))
                    act.activation(far, far, ACT.Abs).then_inc(sem["hat_abs_ready"], 1)
                if on(u, 2):
                    act.wait_ge(sem["probs_turned"], u - 1 + past(2, "probs_turned"))
                    act.activation(pt, PTB, ACT.Copy).then_inc(sem["probs_t_ready"], 1)
                if on(u, 1):
                    act.wait_ge(sem["sampled_centred"], u + past(2, "sampled_centred"))
                    act.activation(samp, samp, ACT.Exp).then_inc(sem["sampled_exp"], 1)
                if on(u, 0):
                    act.wait_ge(sem["hat_abs_ready"], u + 1 + past(2, "hat_abs_ready"))
                    for half in range(2):
                        part = hat[p][:, half * (NSAMP * S // 2):(half + 1) * (NSAMP * S // 2)]
                        act.activation(part, part, ACT.Relu, scale=-1.0, bias=1.0).then_inc(
                            sem["half_hat_ready"], 1)
                if on(u, 3):
                    ln_act(act, ln_number_attn(2, u - 3), XB, u - 3, 1)
            steps(act, 3, step, 1)

        def a2_dve(dve):
            zero_values(dve)
            dve.tensor_tensor(base, row("boff"), const("refloc"), ALU.add).then_inc(sem["base_ready"], 1)
            dve.wait_ge(sem["attention_zeroed"], 2)
            dve.wait_ge(sem["base_ready"], 1)

            def samples(u, p, half):
                n = NSAMP // 2
                hs = slice(half * n * S, (half + 1) * n * S)
                dve.tensor_tensor(product.rearrange("p (h k j) -> p h k j", h=HP, k=NK),
                                  hat[1 - p][:, hs].rearrange("p (h k j) -> p h k j", h=HP, k=NK),
                                  kscore[1 - p][:, half * 512:half * 512 + 512].rearrange(
                                      "p (h j) -> p h j", h=HP).unsqueeze(2).broadcast_to([P, HP, NK, S]),
                                  ALU.mult).then_inc(sem["product_ready"], 1)
                dve.wait_ge(sem["product_ready"], (u - 1) * 2 + half + 1)
                dve.tensor_reduce(samp[:, half * n:(half + 1) * n], product.rearrange("p (s j) -> p s j", j=S), AX.X,
                                  ALU.add).then_inc(sem["sampled_half"], 1)

            def take_offsets(t):
                dve.wait_ge(sem["offsets_projected"], t + 1 + past(2, "offsets_projected"))
                if positive(t + past(2, "positions_ready")):
                    dve.wait_ge(sem["positions_ready"], t + past(2, "positions_ready"))
                dve.tensor_tensor(offs, XB[:, 0:NSAMP], base, ALU.add).then_inc(sem["offsets_ready"], 1)

            def step(u, p):
                if isinstance(u, int) and u == 0:
                    take_offsets(0)
                if on(u, 1):
                    dve.wait_ge(sem["half_hat_ready"], 2 * u - 1)
                    dve.wait_ge(sem["scores_copied"], u + past(2, "scores_copied"))
                    samples(u, p, 0)
                    dve.wait_ge(sem["values_projected"], u + past(2, "values_projected"))
                    if on(u, -1):
                        dve.wait_ge(sem["ks_ready"], u + 2 + past(2, "ks_ready"))
                    dve.sem_inc(sem["dve_passed"], 1)
                    for h2, r in enumerate(halves()):
                        dst = vm[1 - p][r].rearrange("p (c b h d) -> p h b c d", c=HP, b=2, h=2)[:, h2]
                        src = XB[r, 256:512].rearrange("p (b c h d) -> p h b c d", b=2, c=HP, h=2)[:, h2]
                        bv = row("bv2")[r].rearrange("p (c h d) -> p h c d", c=HP, h=2)[:, h2]
                        i = dve.tensor_tensor(dst, src, bv.unsqueeze(1).broadcast_to([64, 2, HP, HD]), ALU.add)
                    i.then_inc(sem["vm_ready"], 1)
                if on(u, 3):
                    narrow_update(dve, 2, u - 3)
                if on(u, 0):
                    dve.wait_ge(sem["positions_ready"], u + 1 + past(2, "positions_ready"))
                    if positive(u - 1 + past(2, "hat_weighted_pool")):
                        dve.wait_ge(sem["hat_weighted_pool"], u - 1 + past(2, "hat_weighted_pool"))
                    far = NSAMP - NEAR
                    dve.tensor_tensor(hat[p][:, 0:far * S].rearrange("p (s j) -> p s j", j=S),
                                      const("iota64").unsqueeze(1).broadcast_to([P, far, S]),
                                      pos[:, 0:far].unsqueeze(2).broadcast_to([P, far, S]), ALU.subtract).then_inc(
                        sem["distance_ready"], 1)
                if on(u, -1):
                    take_offsets(u + 1)
                if on(u, 1):
                    dve.wait_ge(sem["half_hat_ready"], 2 * u)
                    dve.wait_ge(sem["sampled_half"], u * 2 - 1)
                    samples(u, p, 1)
                    dve.wait_ge(sem["sampled_half"], u * 2)
                    s3 = samp.rearrange("p (h k) -> p h k", k=NK)

                    def wide(a):
                        return a.unsqueeze(2).broadcast_to([P, H, NK])

                    dve.tensor_reduce(rs_sb[:, 0:H], s3, AX.X, ALU.max).then_inc(sem["sampled_max"], 1)
                    dve.wait_ge(sem["sampled_max"], u + past(2, "sampled_max"))
                    dve.tensor_tensor(s3, s3, wide(rs_sb[:, 0:H]), ALU.subtract).then_inc(sem["sampled_centred"], 1)
                    dve.wait_ge(sem["sampled_exp"], u + past(2, "sampled_exp"))
                    dve.tensor_reduce(rs_sb[:, H:2 * H], s3, AX.X, ALU.add).then_inc(sem["sampled_sum"], 1)
                    dve.wait_ge(sem["sampled_sum"], u + past(2, "sampled_sum"))
                    dve.reciprocal(rs_sb[:, 2 * H:3 * H], rs_sb[:, H:2 * H]).then_inc(sem["sampled_recip"], 1)
                    dve.wait_ge(sem["sampled_recip"], u + past(2, "sampled_recip"))
                    if positive(u - 1 + past(2, "hat_weighted_pool")):
                        dve.wait_ge(sem["hat_weighted_pool"], u - 1 + past(2, "hat_weighted_pool"))
                    dve.scalar_tensor_tensor(wgt.rearrange("p (h k) -> p h k", k=NK), s3, 0.5,
                                             wide(rs_sb[:, 2 * H:3 * H]), ALU.mult, ALU.mult).then_inc(
                        sem["weights_ready"], 1)
                    dve.wait_ge(sem["weights_ready"], u + past(2, "weights_ready"))
                    dve.wait_ge(sem["probs_turned"], u - 1 + past(2, "probs_turned"))
                    weight(dve, 1 - p, PAIRS_POOL, HP).then_inc(sem["hat_weighted_dve"], 1)
                if on(u, 2):
                    dve.wait_ge(sem["heads_summed"], u - 1 + past(2, "heads_summed"))
                    for b, r in enumerate(halves()):
                        i = dve.tensor_copy(ob[r].rearrange("p (c h d) -> p c h d", c=HP, h=2),
                                            OB[r, 0:256].rearrange("p (c b h d) -> p b c h d", c=HP, b=2, h=2)[:, b])
                    i.then_inc(sem["heads_scaled"], 1)
            steps(dve, 3, step, 1)

        def weight(eng, p, c0, c1):
            for h2 in range(2):
                def part(a, order):
                    return a.rearrange(order, c=HP, h=2, k=NK)[:, c0:c1, h2]
                i = eng.tensor_tensor(part(wbuf, "p (c k h j) -> p c h k j"),
                                      part(hat[p], "p (c h k j) -> p c h k j"),
                                      part(wgt, "p (c h k) -> p c h k").unsqueeze(3).broadcast_to(
                                          [P, c1 - c0, NK, S]), ALU.mult)
            return i

        def a2_pool(pool):
            def positions(u):
                k = [0]

                def done(ins):
                    ins.then_inc(sem["position_steps"], 1)
                    k[0] += 1
                    pool.wait_ge(sem["position_steps"], u * 8 + k[0])

                m = lens_sb[:, bass.ds(u, 1)].broadcast_to([P, NSAMP])
                rm = rlens_sb[:, bass.ds(u, 1)].broadcast_to([P, NSAMP])
                a, b = tmp
                pool.wait_ge(sem["offsets_ready"], u + 1 + past(2, "offsets_ready"))
                if positive(u + past(2, "distance_ready")):
                    pool.wait_ge(sem["distance_ready"], u + past(2, "distance_ready"))
                if positive(u + past(2, "near_ready")):
                    pool.wait_ge(sem["near_ready"], u + past(2, "near_ready"))
                pool.sem_inc(sem["pool_passed"], 1)
                done(pool.tensor_tensor(a, offs, rm, ALU.mult))
                pool.sem_inc(sem["pool_passed"], 1)
                done(pool.tensor_scalar(a, a, MAGIC, -MAGIC, ALU.add, ALU.add))
                pool.sem_inc(sem["pool_passed"], 1)
                done(pool.tensor_tensor(a, a, m, ALU.mult))
                done(pool.tensor_tensor(a, offs, a, ALU.subtract))
                pool.sem_inc(sem["pool_passed"], 1)
                done(pool.tensor_tensor(b, a, m, ALU.mult))
                pool.sem_inc(sem["pool_passed"], 1)
                done(pool.tensor_scalar(b, b, 0.0, None, ALU.is_lt))
                pool.sem_inc(sem["pool_passed"], 1)
                done(pool.tensor_tensor(b, b, m, ALU.mult))
                done(pool.tensor_tensor(a, a, b, ALU.add))
                pool.sem_inc(sem["pool_passed"], 1)
                pool.tensor_scalar(pos, a, float(np.float32(S / (S - 1))), -0.5, ALU.mult, ALU.add).then_inc(
                    sem["positions_ready"], 1)

            def step(u, p):
                if isinstance(u, int) and u == 0:
                    narrow_expand(pool, 2, 0, 0)
                    positions(0)
                if on(u, -1):
                    narrow_expand(pool, 2, u + 1, 1 - p)
                if on(u, 0):
                    if positive(u - 1 + past(2, "values_projected")):
                        pool.wait_ge(sem["values_projected"], u - 1 + past(2, "values_projected"))
                    pool.tensor_copy(cdup[p].rearrange("p (b c t) -> p b c t", b=2, c=2),
                                     ctx_sb[:, bass.ds(u * P, P)].rearrange("p (b t) -> p b t", b=2).unsqueeze(
                                         2).broadcast_to([P, 2, 2, S])).then_inc(sem["cdup_staged"], 1)
                if on(u, 3):
                    ln_pool(pool, ln_number_attn(2, u - 3), u - 3, 1)
                if on(u, 2):
                    pool.wait_ge(sem["x_updated"], updates(ln_number_attn(2, u - 3)))
                    pool.sem_inc(sem["pool_passed"], 1)
                    pool.tensor_tensor(xb_sb[:], x_sb[:, bass.ds((u - 2) * D, D)], gbias_sb[:, 2 * D:3 * D],
                                       ALU.add).then_inc(sem["x_biased"], 1)
                if on(u, -1):
                    positions(u + 1)
                if on(u, 1):
                    pool.wait_ge(sem["weights_ready"], u + past(2, "weights_ready"))
                    pool.wait_ge(sem["probs_turned"], u - 1 + past(2, "probs_turned"))
                    pool.sem_inc(sem["pool_passed"], 1)
                    weight(pool, 1 - p, 0, PAIRS_POOL).then_inc(sem["hat_weighted_pool"], 1)
            steps(pool, 3, step, 1)

        def distances(dve):
            dve.wait_ge(sem["kpos_loaded"], 32)
            dve.wait_ge(sem["maskq_loaded"], 16)
            dve.wait_ge(sem["qpos_loaded"], 16)
            keys, masked = xn_sb[:, 0:NT * S], xn_sb[:, NT * S:]
            dve.tensor_scalar(masked, masked.bitcast(I32), 0.0, -3.0e38, ALU.is_equal, ALU.mult).then_inc(
                sem["dist_steps"], 1)
            dve.tensor_tensor(keys.rearrange("p (n t) -> p n t", t=S),
                               keys.bitcast(I32).rearrange("p (n t) -> p n t", t=S),
                               qpos_sb[:].unsqueeze(2).broadcast_to([P, NT, S]), ALU.subtract).then_inc(
                sem["dist_steps"], 1)
            dve.wait_ge(sem["dist_steps"], 1)
            dve.tensor_scalar(masked, masked, 10.0, None, ALU.mult).then_inc(sem["dist_steps"], 1)
            dve.wait_ge(sem["dist_steps"], 3)
            dve.tensor_tensor(keys, keys, masked, ALU.add).then_inc(sem["dist_steps"], 1)
            dve.wait_ge(sem["dist_steps"], 4)

        JOB0 = {0: 0}
        Y0 = {0: 0}
        for f in FFNS:
            JOB0[f.layer + 1] = JOB0[f.layer] + f.jobs * NG + (4 * NG if f.layer == 0 else 0)
            Y0[f.layer + 1] = Y0[f.layer] + f.ys * NG
        gated_before = {0: 0, 1: 0, 2: FFNS[1].jobs * NG, 3: (FFNS[1].jobs + FFNS[2].jobs) * NG}
        LT, TT = bank(6), bank(7)

        def slab_of(f):
            return slab1 if f.layer in (1, 3) else slab0

        def w_of(f, name):
            return view(slab_of(f), [WF0, WF1, WF2, WF3][f.layer], name)

        def hidden_bank(f, k):
            return (bank(2 * (k % 2)), bank(2 * (k % 2) + 1)) if f.gated else (bank(k % 4), None)

        def ring(f):
            return 2 if f.gated else 4

        def hidden_set_free(f, g, e):
            if isinstance(g, int) and g == 0 and e < f.sets:
                return Y0[f.layer]
            n = Y0[f.layer] + e - f.sets + 1
            return g * f.ys + n

        def own(f, k):
            return gated_before[f.layer] + k

        def route_pe(pe, f):
            L = f.layer
            pe.wait_ge(sem[f"w{L}_loaded"], 16)
            pe.wait_ge(sem["xt_tile_ready"], (L + 1) * NT)

            def turn_logits(g):
                pe.wait_ge(sem["logits_t_ready"], g + (L * NG + 1))
                if positive(g + L * NG):
                    pe.wait_ge(sem["logits_ready"], g + L * NG)
                pe.sem_inc(sem["pe_passed"], 1)
                for u in range(GT):
                    i = pe.transpose(TT[:, u * E:(u + 1) * E], lgt[0:E, u * P:(u + 1) * P], ident[0:E, 0:E])
                i.then_inc(sem["logits_turned"], 1)

            def group(g):
                if L == 0:
                    for c in range(4):
                        i = pe.matmul(bank(c), w_of(f, "rw1")[:, c * P:(c + 1) * P],
                                      xt_sb[:, bass.ds(g * GW, GW)], start=True, stop=True)
                        i.then_inc(sem["hidden_full"], 1)
                if not (isinstance(g, int) and g == 0):
                    turn_logits(g - 1)
                if L == 0:
                    for c in range(4):
                        pe.wait_ge(sem["hidden_relu_ready"], g * 4 + (c + 1))
                        i = pe.matmul(LT[0:E, :], w_of(f, "rw2")[:, c * E:(c + 1) * E], hid[c],
                                      start=c == 0, stop=c == 3)
                else:
                    i = pe.matmul(LT[0:E, :], w_of(f, "router"), xt_sb[:, bass.ds(g * GW, GW)], start=True, stop=True)
                i.then_inc(sem["logits_t_full"], 1)

            group(0)
            group(1)
            with pe.Fori(2, NG) as g:
                group(g)
            turn_logits(NG - 1)
            pe.wait_ge(sem["mask_ready"], L + 1)
            pe.matmul(LT[:, 0:NT * E], const("before"), rt[3], start=True, stop=True)
            pe.matmul(TT[:, 0:NT * E], const("ones"), rt[3], start=True, stop=True).then_inc(
                sem["prefix_ready"], 1)

        def route_act(act, f):
            L = f.layer

            def group(g):
                G = g + L * NG
                if L == 0:
                    for c in range(4):
                        act.wait_ge(sem["hidden_full"], g * 4 + (c + 1))
                        act.activation(hid[c], bank(c), ACT.Relu, bias=col("rb1")[:, c:c + 1]).then_inc(
                            sem["hidden_relu_ready"], 1)
                act.wait_ge(sem["logits_t_full"], G + 1)
                if positive(G):
                    act.wait_ge(sem["logits_turned"], G)
                act.sem_inc(sem["act_passed"], 1)
                if L in (0, 3):
                    act.activation(lgt[0:E, :], LT[0:E, :], ACT.Identity,
                                   bias=col("rb2" if L == 0 else "gb3")[0:E, :]).then_inc(sem["logits_t_ready"], 1)
                else:
                    act.activation(lgt[0:E, :], LT[0:E, :], ACT.Copy).then_inc(sem["logits_t_ready"], 1)
            groups(act, group)
            if f.softmax:
                act.wait_ge(sem["route_steps"], ROUTE0[L] + 2)
                act.activation(rt[1], rt[1], ACT.Exp).then_inc(sem["route_exp_ready"], 1)
            if L == 1:
                act.wait_ge(sem["route_steps"], ROUTE0[L] + 1)
                act.activation(m1_sb[:], small[0], ACT.Sigmoid).then_inc(sem["gates_ready"], 1)

        ROUTE0 = {}

        def running_sum(dve, link):
            link(dve.memset(rt[5][:, 0:E], 0.0))
            link(dve.tensor_copy(rt[5][:, E:], TT[:, 0:(NT - 1) * E]))
            a, b, s = rt[5], rt[6], 1
            while s < NT:
                link(dve.tensor_tensor(b[:, s * E:], a[:, s * E:], a[:, :(NT - s) * E], ALU.add))
                link(dve.tensor_copy(b[:, :s * E], a[:, :s * E]))
                a, b, s = b, a, 2 * s
            return a

        def choices(dve, link, v, place, kept):
            link(dve.tensor_scalar(kept, place, float(CAP0), None, ALU.is_lt))
            link(dve.tensor_tensor(comb_sb[:], rt[4], kept, ALU.mult))
            link(dve.scalar_tensor_tensor(v(rt[1]), const("iota8").unsqueeze(1).broadcast_to([P, NT, E]),
                                          float(CAP0), v(place), ALU.mult, ALU.add))
            link(dve.tensor_tensor(rt[1], rt[1], kept, ALU.mult))
            for k, chosen in enumerate((rt[2], rt[7])):
                here = slice(k * NT, (k + 1) * NT)
                link(dve.tensor_tensor(rt[4], rt[1], chosen, ALU.mult))
                link(dve.tensor_reduce(small[1], v(rt[4]), AX.X, ALU.add))
                link(dve.tensor_copy(from0_sb[:, here], small[1]))
                link(dve.tensor_tensor(rt[4], comb_sb[:], chosen, ALU.mult))
                link(dve.tensor_reduce(small[2], v(rt[4]), AX.X, ALU.add))
                link(dve.tensor_scalar(weight0_sb[:, here], small[2], gain_sb[:, 4:5], None, ALU.mult))
                link(dve.tensor_tensor(rt[4], kept, chosen, ALU.mult))
                link(dve.tensor_reduce(small[2], v(rt[4]), AX.X, ALU.add))
                link(dve.tensor_scalar(small[2], small[2], -1.0, 1.0, ALU.mult, ALU.add))
                link(dve.tensor_scalar(small[0], const("iota64")[:, 0:NT], 2.0 * P, float(NB0 * BW + k * P),
                                       ALU.mult, ALU.add))
                link(dve.tensor_tensor(small[0], small[0], const("part").broadcast_to([P, NT]), ALU.add))
                link(dve.tensor_tensor(small[0], small[0], small[2], ALU.mult))
                link(dve.tensor_tensor(small[1], small[1], small[0], ALU.add))
                i = dve.tensor_copy(slot0_sb[:, here], small[1])
            i.then_inc(sem["slots_ready"], 1)

        def slots(dve, link, v):
            a = running_sum(dve, link)
            blocks, ends, other, base = (rt[7][:, k * E:(k + 1) * E] for k in range(4))
            link(dve.tensor_tensor(blocks, a[:, (NT - 1) * E:], TT[:, (NT - 1) * E:NT * E], ALU.add))
            link(dve.tensor_scalar(blocks, blocks, 1.0 / BW, (BW - 1) / (2.0 * BW), ALU.mult, ALU.add))
            link(dve.tensor_scalar(blocks, blocks, MAGIC, None, ALU.add))
            link(dve.tensor_scalar(blocks, blocks, -MAGIC, None, ALU.add))
            link(dve.tensor_copy(ends, blocks))
            for s in (1, 2, 4):
                link(dve.tensor_tensor(other[:, s:], ends[:, s:], ends[:, :E - s], ALU.add))
                link(dve.tensor_copy(other[:, :s], ends[:, :s]))
                ends, other = other, ends
            experts = rt[0][:, 0:NB]
            link(dve.tensor_tensor(rt[4][:, 0:NB * E].rearrange("p (b e) -> p b e", e=E),
                                   const("iota64")[:, 0:NB].unsqueeze(2).broadcast_to([P, NB, E]),
                                   ends.unsqueeze(1).broadcast_to([P, NB, E]), ALU.is_ge))
            link(dve.tensor_reduce(experts, rt[4][:, 0:NB * E].rearrange("p (b e) -> p b e", e=E), AX.X, ALU.add))
            link(dve.tensor_scalar(experts, experts, float(E - 1), float(P), ALU.min, ALU.mult))
            link(dve.tensor_tensor(experts, experts, const("part").broadcast_to([P, NB]), ALU.add))
            link(dve.tensor_copy(wrow_sb[:], experts))
            link(dve.tensor_tensor(base, ends, blocks, ALU.subtract))
            link(dve.tensor_scalar(base, base, float(BW), None, ALU.mult))
            link(dve.tensor_tensor(a, a, LT[:, 0:NT * E], ALU.add))
            link(dve.tensor_tensor(v(a), v(a), base.unsqueeze(1).broadcast_to([P, NT, E]), ALU.add))
            link(dve.tensor_tensor(a, a, rt[3], ALU.mult))
            link(dve.tensor_reduce(small[1], v(a), AX.X, ALU.add))
            dve.tensor_copy(slot_sb[:], small[1]).then_inc(sem["slots_ready"], 1)

        def route_dve(dve, f):
            L = f.layer
            with dve.Fori(0, NG) as g:
                dve.wait_ge(sem["logits_turned"], g + (L * NG + 1))
                dve.tensor_copy(logit_sb[:, bass.ds(g * (GT * E), GT * E)], TT[:, 0:GT * E]).then_inc(
                    sem["logits_ready"], 1)
            dve.wait_ge(sem["logits_ready"], (L + 1) * NG)
            n = [ROUTE0[L]]

            def link(ins):
                ins.then_inc(sem["route_steps"], 1)
                n[0] += 1
                dve.wait_ge(sem["route_steps"], n[0])

            def v(a):
                return a.rearrange("p (t e) -> p t e", e=E)

            def wide(a):
                return a.unsqueeze(2).broadcast_to([P, NT, E])

            iota = const("iota8").unsqueeze(1).broadcast_to([P, NT, E])
            link(dve.tensor_reduce(small[0], v(logit_sb), AX.X, ALU.max))
            keys = logit_sb
            if f.softmax:
                link(dve.tensor_tensor(v(rt[1]), v(logit_sb), wide(small[0]), ALU.subtract))
                dve.wait_ge(sem["route_exp_ready"], 1 if L == 0 else 2)
                if f.softmax == "all":
                    link(dve.tensor_reduce(small[1], v(rt[1]), AX.X, ALU.add))
                    link(dve.reciprocal(small[2], small[1]))
                    link(dve.tensor_tensor(v(rt[1]), v(rt[1]), wide(small[2]), ALU.mult))
                    keys = rt[1]
                    link(dve.tensor_reduce(small[0], v(keys), AX.X, ALU.max))

            def one_hot(dst, values):
                link(dve.tensor_tensor(v(rt[4]), v(values), wide(small[0]), ALU.is_lt))
                link(dve.scalar_tensor_tensor(v(rt[5]), v(rt[4]), BIG, iota, ALU.mult, ALU.add))
                link(dve.tensor_reduce(small[1], v(rt[5]), AX.X, ALU.min))
                link(dve.tensor_tensor(v(dst), iota, wide(small[1]), ALU.is_equal))

            one_hot(rt[2], keys)
            if f.topk == 2:
                link(dve.scalar_tensor_tensor(v(rt[6]), v(rt[2]), -3.0e38, v(keys), ALU.mult, ALU.add))
                link(dve.tensor_reduce(small[0], v(rt[6]), AX.X, ALU.max))
                one_hot(rt[7], rt[6])
                dve.tensor_tensor(rt[3], rt[2], rt[7], ALU.add).then_inc(sem["mask_ready"], 1)
                dve.wait_ge(sem["mask_ready"], L + 1)
            if f.topk == 1:
                dve.tensor_copy(rt[3], rt[2]).then_inc(sem["mask_ready"], 1)
                dve.wait_ge(sem["prefix_ready"], L + 1)
                slots(dve, link, v)
                assert n[0] == ROUTE0[L] + count_route(f)
                return
            link(dve.tensor_tensor(rt[4], rt[1], rt[3], ALU.mult))
            link(dve.tensor_reduce(small[1], v(rt[4]), AX.X, ALU.add))
            if f.softmax == "all":
                link(dve.tensor_scalar(small[1], small[1], 1e-20, None, ALU.add))
            link(dve.reciprocal(small[2], small[1]))
            link(dve.tensor_tensor(v(rt[4]), v(rt[4]), wide(small[2]), ALU.mult))
            dve.wait_ge(sem["prefix_ready"], L + 1)
            a = running_sum(dve, link)
            link(dve.tensor_tensor(a, a, LT[:, 0:NT * E], ALU.add))
            if L == 0:
                choices(dve, link, v, a, rt[5] if a is rt[6] else rt[6])
                assert n[0] == ROUTE0[L] + count_route(f)
                return
            link(dve.tensor_scalar(a, a, float(f.cap), None, ALU.is_lt))
            dve.tensor_tensor(comb_sb[:], rt[4], a, ALU.mult).then_inc(sem["comb_ready"], 1)

        def count_route(f):
            n = 1 + 4
            if f.softmax:
                n += 1 + (4 if f.softmax == "all" else 0)
            if f.topk == 2:
                n += 2 + 4
            if f.softmax:
                n += 4 + (1 if f.softmax == "all" else 0) + 2 + 10 + 2
            if f.topk == 1:
                n += 34
            if f.layer == 0:
                n += 3 + 2 * 13
            return n

        total = 0
        for f in FFNS:
            ROUTE0[f.layer] = total
            total += count_route(f)

        def groups(eng, body):
            body(0)
            with eng.Fori(1, NG) as g:
                body(g)

        WX = {0: WX3, 1: WX1, 3: WX3}
        wblks = {0: [view(slab0, WF0, "wa"), view(slab0, WF0, "wb"), view(slab0, WF0, "wc"), view(slab1, WY0, "wd")],
                 1: [view(slab1, WF1, "wa"), view(slab1, WF1, "wb"), view(slab0, WY1, "wc"), view(slab0, WY1, "wd")],
                 3: [view(slab1, WF3, "wa"), view(slab1, WF3, "wb"), view(slab0, WY3, "wc"), view(slab0, WY3, "wd")]}
        sums_of = {0: slab0, 1: slab1, 3: slab1}
        back_of = {0: slab1[:, 0:2 * NT * D], 1: slab0[:, 0:NT * D], 3: slab0[:, 0:NT * D]}
        NTH = {0: 0, 1: 1, 3: 2}
        NBS = {0: NB0, 1: NB, 3: NB}
        BEFORE = {0: 0, 1: NB0, 3: NB0 + NB}
        PLAIN = {0: 0, 3: 2 * NB0}
        MOVES = {0: 0, 1: 2, 3: 3}

        def block_steps(eng, L, step):
            for b in range(4):
                step(b, b, 0)
            with eng.Fori(0, NBS[L] // 4 - 2) as i:
                for k in range(4):
                    step(i * 4 + (4 + k), k, i + 1)
            for b in range(NBS[L] - 4, NBS[L] + 1):
                step(b, b % 4, b // 4)

        def block_on(L, b, back):
            return not isinstance(b, int) or 0 <= b - back < NBS[L]

        def blocks_pe(pe, L):
            n0, h0, wblk = BEFORE[L], PLAIN.get(L), wblks[L]
            r0 = n0 // 4
            pe.wait_ge(sem["slots_ready"], NTH[L] + 1)
            if L == 1:
                pe.wait_ge(sem["shared_added"], NG)

            def turn(b, k, r):
                pe.wait_ge(sem[f"rows_loaded_{k}"], (r + (r0 + 1)) * 16)
                if positive(b + (n0 - 1)):
                    pe.wait_ge(sem["block_t_ready"], b + (n0 - 1))
                for u in range(BT):
                    i = pe.transpose(bank(k % 2)[:, u * P:(u + 1) * P], xblk[k][:, u * P:(u + 1) * P], ident)
                i.then_inc(sem["block_turned"], 1)

            def hidden(b, k):
                if L != 1:
                    if positive(b * 2 + (h0 - 2)):
                        pe.wait_ge(sem["block_relu_ready"], b * 2 + (h0 - 2))
                    pe.sem_inc(sem["pe_passed"], 1)
                    for c in range(4):
                        i = pe.matmul(bank(2 + 2 * (k % 2) + c // 2)[:, c % 2 * BW:(c % 2 + 1) * BW],
                                      view(wblk[k], WX3, "w1")[:, c * P:(c + 1) * P], xbt[k % 2], start=True,
                                      stop=True)
                        if c % 2:
                            i.then_inc(sem["block_hidden_full"], 1)
                    return
                for c, (at, w) in enumerate(F1C):
                    if positive(b * 3 + (c - 3)):
                        pe.wait_ge(sem["block_gated_ready"], b * 3 + (c - 3))
                    hb = bank(2 + (3 * k + c) % 4)
                    pe.sem_inc(sem["pe_passed"], 1)
                    for h, name in enumerate(("w1", "w3")):
                        i = pe.matmul(hb[0:w, h * BW:(h + 1) * BW], view(wblk[k], WX1, name)[:, at:at + w],
                                      xbt[k % 2], start=True, stop=True)
                    i.then_inc(sem["block_chunk_full"], 1)

            def output(b, q):
                w2 = view(wblk[q], WX[L], "w2")
                if L != 1:
                    pe.wait_ge(sem["block_relu_ready"], b * 2 + (h0 + 2))
                    widths = [P] * 4
                else:
                    pe.wait_ge(sem["block_gated_ready"], b * 3 + 3)
                    widths = [w for _, w in F1C]
                if positive(b + (n0 - 1)):
                    pe.wait_ge(sem["block_copied"], b + (n0 - 1))
                pe.sem_inc(sem["pe_passed"], 1)
                for u in range(BT):
                    out_u = bank(6 + q % 2)[:, u * P:(u + 1) * P]
                    for c, w in enumerate(widths):
                        i = pe.matmul(out_u, hid3[q % 2][0:w, c * BW + u * P:c * BW + (u + 1) * P],
                                      w2[0:w, c * D:(c + 1) * D], start=c == 0, stop=L == 1 and c == 2)
                    if L != 1:
                        i = pe.matmul(out_u, const("ones"), view(wblk[q], WX3, "b2"), start=False, stop=True)
                i.then_inc(sem["block_summed"], 1)

            def step(b, k, r):
                if isinstance(b, int) and b == 0:
                    turn(0, 0, 0)
                if block_on(L, b, -1):
                    turn(b + 1, (k + 1) % 4, r + 1 if k == 3 else r)
                if block_on(L, b, 0):
                    pe.wait_ge(sem[f"weights_gathered_{k}"], (r + (r0 + 1)) * 16)
                    pe.wait_ge(sem["block_t_ready"], b + (n0 + 1))
                    pe.sem_inc(sem["pe_passed"], 1)
                    hidden(b, k)
                if block_on(L, b, 1):
                    output(b - 1, (k - 1) % 4)
            block_steps(pe, L, step)
            if L != 3:
                def turn_rows(g):
                    pe.wait_ge(sem["xt_group_ready"], g * GT + (L + 1) * NT)
                    ln_pe(pe, ln_number_ffn(L, g), LT, GT)
                groups(pe, turn_rows)

        def blocks_act(act, L):
            n0, h0, wblk = BEFORE[L], PLAIN.get(L), wblks[L]

            def step(b, k, r):
                if block_on(L, b, 0) and L != 1:
                    if positive(b + (n0 - 1)):
                        act.wait_ge(sem["block_summed"], b + (n0 - 1))
                    for c in range(4):
                        if c % 2 == 0:
                            act.wait_ge(sem["block_hidden_full"], b * 2 + (h0 + c // 2 + 1))
                            act.sem_inc(sem["act_passed"], 1)
                        i = act.activation(hid3[k % 2][:, c * BW:(c + 1) * BW],
                                           bank(2 + 2 * (k % 2) + c // 2)[:, c % 2 * BW:(c % 2 + 1) * BW], ACT.Relu,
                                           bias=view(wblk[k], WX3, "b1")[:, c:c + 1])
                        if c % 2:
                            i.then_inc(sem["block_relu_ready"], 1)
                if block_on(L, b, 0) and L == 1:
                    for c, (_, w) in enumerate(F1C):
                        if positive(b * 3 + (c - 1)):
                            act.wait_ge(sem["block_gated_ready"], b * 3 + (c - 1))
                        act.wait_ge(sem["block_chunk_full"], b * 3 + (c + 1))
                        act.sem_inc(sem["act_passed"], 1)
                        act.activation(gate3[(3 * k + c) % 2][0:w, :], bank(2 + (3 * k + c) % 4)[0:w, 0:BW],
                                       ACT.Silu).then_inc(sem["block_silu_ready"], 1)
            block_steps(act, L, step)
            if L != 3:
                groups(act, lambda g: ln_act(act, ln_number_ffn(L, g), LT, g * GT, GT))

        def blocks_dve(dve, L):
            n0 = BEFORE[L]

            def step(b, k, r):
                if block_on(L, b, 0):
                    dve.wait_ge(sem["block_turned"], b + (n0 + 1))
                    if L != 1:
                        if positive(b * 2 + (PLAIN[L] - 2)):
                            dve.wait_ge(sem["block_hidden_full"], b * 2 + (PLAIN[L] - 2))
                    else:
                        if positive(b * 3 - 3):
                            dve.wait_ge(sem["block_chunk_full"], b * 3 - 3)
                    dve.sem_inc(sem["dve_passed"], 1)
                    dve.tensor_copy(xbt[k % 2], bank(k % 2)[:, 0:BW]).then_inc(sem["block_t_ready"], 1)
                if block_on(L, b, 0) and L == 1:
                    dve.wait_ge(sem["block_summed"], b + (n0 - 1))
                    for c, (_, w) in enumerate(F1C):
                        dve.wait_ge(sem["block_silu_ready"], b * 3 + (c + 1))
                        dve.sem_inc(sem["dve_passed"], 1)
                        dve.tensor_tensor(hid3[k % 2][0:w, c * BW:(c + 1) * BW], gate3[(3 * k + c) % 2][0:w, :],
                                          bank(2 + (3 * k + c) % 4)[0:w, BW:], ALU.mult).then_inc(
                            sem["block_gated_ready"], 1)
                if block_on(L, b, 1):
                    dve.wait_ge(sem["block_summed"], b + n0)
                    dve.tensor_copy(sums_of[L][:, bass.ds((b - 1) * BW, BW)], bank(6 + (k - 1) % 2)[:, 0:BW]).then_inc(
                        sem["block_copied"], 1)
            block_steps(dve, L, step)
            back = back_of[L]
            for g in range(NG):
                if L == 0:
                    dve.wait_ge(sem[f"rows_back_{g}"], 2 * GT * 16)
                    for k, name in enumerate(("first_choice_added", "x_updated")):
                        if k == 1:
                            dve.wait_ge(sem["first_choice_added"], g + 1)
                        for t in range(g * GT, (g + 1) * GT):
                            i = dve.scalar_tensor_tensor(x_tiles(t, 1), back[:, (k * NT + t) * D:(k * NT + t + 1) * D],
                                                         weight0_sb[:, k * NT + t:k * NT + t + 1], x_tiles(t, 1),
                                                         ALU.mult, ALU.add)
                        i.then_inc(sem[name], 1)
                    ln_dve(dve, ln_number_ffn(L, g), g * GT, GT, own=g > 0)
                    ln_all_dve(dve, NG + g, ln_number_ffn(L, g), g * GT, GT)
                    continue
                dve.wait_ge(sem[f"rows_back_{g}"], (MOVES[L] + 1) * GT * 16)
                dve.scalar_tensor_tensor(x_tiles(g * GT, GT), back[:, g * GW:(g + 1) * GW], gain_sb[:, 4 + L:5 + L],
                                         x_tiles(g * GT, GT), ALU.mult, ALU.add).then_inc(sem["x_updated"], 1)
                if L == 1:
                    ln_dve(dve, ln_number_ffn(L, g), g * GT, GT, own=g > 0)
                    ln_all_dve(dve, 2 * NG + g, ln_number_ffn(L, g), g * GT, GT)

        def scale_rows(dve):
            dve.wait_ge(sem["gates_ready"], 1)
            dve.wait_ge(sem["rows_kept"], 2 * NT)
            for k in range(4):
                dve.tensor_tensor(slab1[:, k * 1024:(k + 1) * 1024].rearrange("p (w d) -> p w d", d=D),
                                  xn_sb[:, k * 1024:(k + 1) * 1024].rearrange("p (w d) -> p w d", d=D),
                                  m1_sb[:, k * 8:(k + 1) * 8].unsqueeze(2).broadcast_to([P, 8, D]),
                                  ALU.mult).then_inc(sem["rows_scaled"], 1)

        def at_rows(index):
            return bass.IndirectOffsetOnAxis(ap=index.bitcast(mybir.dt.uint32), axis=0)

        def blocks_pool(pool, L):
            n0, wblk, table = BEFORE[L], wblks[L], {0: experts0, 1: experts1, 3: experts3}[L]
            back = back_of[L]

            def gather_weights(b):
                if positive(n0 + b - 3):
                    pool.wait_ge(sem["block_summed"], n0 + b - 3)
                if L == 0:
                    e = b * BW // CAP0
                    pool.dma_start(wblk[b % 4], table[e * P:(e + 1) * P, :]).then_inc(
                        sem[f"weights_gathered_{b % 4}"], 16)
                else:
                    pool.indirect_dma_start(wblk[b % 4], None, table, at_rows(wrow_sb[:, b:b + 1])).then_inc(
                        sem[f"weights_gathered_{b % 4}"], 16)

            pool.wait_ge(sem["slots_ready"], NTH[L] + 1)
            for b in range(4):
                gather_weights(b)
            pool.wait_ge(sem["slots_zeroed"], 16)
            pool.wait_ge(sem["rows_kept"], (NTH[L] + 1) * NT)
            for t in range(NT):
                if L == 0:
                    for k in range(2):
                        pool.indirect_dma_start(slots_x, at_rows(slot0_sb[:, k * NT + t:k * NT + t + 1]),
                                                xn_sb[:, t * D:(t + 1) * D], None).then_inc(sem["rows_scattered"], 16)
                    continue
                if L == 1:
                    pool.wait_ge(sem["rows_scaled"], t // 8 + 1)
                pool.indirect_dma_start(slots_x, at_rows(slot_sb[:, t:t + 1]), slab1[:, t * D:(t + 1) * D],
                                        None).then_inc(sem["rows_scattered"], 16)
            for b in range(4, NBS[L]):
                gather_weights(b)
            pool.wait_ge(sem["sums_stored"], (n0 + NBS[L]) * 16)

            def rows_back(g):
                for t in range(g * GT, (g + 1) * GT):
                    if L == 0:
                        for k in range(2):
                            pool.indirect_dma_start(back[:, (k * NT + t) * D:(k * NT + t + 1) * D], None,
                                                    slots_y[0:NB0 * BW, :],
                                                    at_rows(from0_sb[:, k * NT + t:k * NT + t + 1])).then_inc(
                                sem[f"rows_back_{t // GT}"], 16)
                    else:
                        pool.indirect_dma_start(back[:, t * D:(t + 1) * D], None, slots_y,
                                                at_rows(slot_sb[:, t:t + 1])).then_inc(
                            sem[f"rows_back_{t // GT}"], 16)

            for g in range(NG):
                rows_back(g)
                if L != 3 and g > 1:
                    pass_on(pool, (NTH[L] + 1) * NG + g - 2)
            if L != 3:
                pass_on(pool, (NTH[L] + 1) * NG + NG - 2)
                pass_on(pool, (NTH[L] + 1) * NG + NG - 1)

        def pass_on(pool, m):
            pool.wait_ge(sem["rows_normalised"], m + 1)
            pool.sem_inc(sem["newton_steps"], 12)
            pool.sem_inc(sem["xn_centred"], 1)
            pool.sem_inc(sem["xn_ready"], 1)

        def blocks_sync(sp, L):
            n0 = BEFORE[L]

            def rows(table, b):
                return table[bass.ds(b * BW, BW), :].rearrange("(u p) d -> p u d", p=P)

            def step(b, k, r):
                if block_on(L, b, 0):
                    if positive(b + (n0 - 3)):
                        sp.wait_ge(sem["block_turned"], b + (n0 - 3))
                    sp.dma_start(xblk[k].rearrange("p (u d) -> p u d", d=D), rows(slots_x, b)).then_inc(
                        sem[f"rows_loaded_{k}"], 16)
                if block_on(L, b, 4):
                    store(b - 4)

            def store(b):
                sp.wait_ge(sem["block_copied"], b + (n0 + 1))
                sp.dma_start(rows(slots_y, b), sums_of[L][:, bass.ds(b * BW, BW)].rearrange(
                    "p (u d) -> p u d", d=D)).then_inc(sem["sums_stored"], 16)

            sp.wait_ge(sem["rows_scattered"], (MOVES[L] + (2 if L == 0 else 1)) * NT * 16)
            block_steps(sp, L, step)
            for b in range(NBS[L] - 3, NBS[L]):
                store(b)

        def ffn_pe(pe, f):
            L, nc_, J = f.layer, len(f.chunks), f.jobs
            hid_of = hid1 if L == 1 else hid
            k0 = 4 * NG if L == 0 else 0
            src_full = JOB0[L] + k0

            def turn(g):
                pe.wait_ge(sem["xt_group_ready"], g * GT + (L + 1) * NT)
                ln_pe(pe, ln_number_ffn(L, g), LT, GT)

            def body(g):
                G = g + L * NG
                y = [0]

                def y_slot():
                    n = g * f.ys + (Y0[L] + y[0])
                    if positive(n if y[0] == 0 else n - 1):
                        pe.wait_ge(sem["expert_added"], n if y[0] == 0 else n - 1)
                    k = y[0]
                    y[0] += 1
                    return k

                def first(e):
                    for c, (c0_, w) in enumerate(f.chunks):
                        j = e * nc_ + c
                        a, b = hidden_bank(f, j)
                        back = ring(f) if j >= ring(f) or J % ring(f) == 0 else 1
                        if positive(g * J + (own(f, k0 + j) - back + 1)):
                            pe.wait_ge(sem["hidden_gated_ready"], g * J + (own(f, k0 + j) - back + 1))
                        rhs = xt_sb[:, bass.ds(g * GW, GW)]
                        fw = F1 if L == 1 else (P if L == 2 else 512)
                        i = pe.matmul(a[0:w, :], w_of(f, "w1")[:, e * fw + c0_:e * fw + c0_ + w], rhs,
                                      start=True, stop=True)
                        if f.gated:
                            i = pe.matmul(b[0:w, :], w_of(f, "w3")[:, e * fw + c0_:e * fw + c0_ + w], rhs,
                                          start=True, stop=True)
                        i.then_inc(sem["hidden_full"], 1)

                def second(e):
                    k = y_slot()
                    yb = bank(4 + k % 2)
                    pe.wait_ge(sem["hidden_gated_ready"], g * J + own(f, k0 + (e + 1) * nc_))
                    for u in range(GT):
                        for c, (_, w) in enumerate(f.chunks):
                            i = pe.matmul(yb[:, u * P:(u + 1) * P],
                                          hid_of[(e % f.sets) * nc_ + c][0:w, u * P:(u + 1) * P],
                                          w_of(f, "w2")[0:w, (e * nc_ + c) * D:(e * nc_ + c + 1) * D],
                                          start=c == 0, stop=c == nc_ - 1)
                    i.then_inc(sem["expert_summed"], 1)

                order = list(range(f.experts))
                for m, e in enumerate(order):
                    first(e)
                    if m:
                        second(order[m - 1])
                    if m == 2 and L != 3 and not (isinstance(g, int) and g == 0):
                        turn(g - 1)
                second(order[-1])

            groups(pe, body)
            if L != 1:
                turn(NG - 1)

        def ffn_act(act, f):
            L, nc_, J = f.layer, len(f.chunks), f.jobs
            hid_of = hid1 if L == 1 else hid
            k0 = 4 * NG if L == 0 else 0
            full0 = JOB0[L] + k0

            def body(g):
                G = g + L * NG
                for e in range(f.experts):
                    for c, (_, w) in enumerate(f.chunks):
                        j = e * nc_ + c
                        a, b = hidden_bank(f, j)
                        act.wait_ge(sem["hidden_full"], g * J + (full0 + j + 1))
                        if positive(g * J + (own(f, k0 + j) - (0 if j == 0 else 1))):
                            act.wait_ge(sem["hidden_gated_ready"], g * J + (own(f, k0 + j) - (0 if j == 0 else 1)))
                        act.activation(gate[j % 2][0:w, :], a[0:w, :], ACT.Silu).then_inc(
                            sem["gate_silu_ready"], 1)
                    if e == 2 and not (isinstance(g, int) and g == 0) and L != 3:
                        ln_act(act, ln_number_ffn(L, g - 1), LT, (g - 1) * GT, GT)

            groups(act, body)
            if L != 1:
                ln_act(act, ln_number_ffn(L, NG - 1), LT, (NG - 1) * GT, GT)

        def ffn_dve(dve, f):
            L, nc_, J = f.layer, len(f.chunks), f.jobs
            hid_of = hid1 if L == 1 else hid
            k0 = 4 * NG if L == 0 else 0

            def body(g):
                G = g + L * NG
                y = [0]
                if L != 1:
                    dve.wait_ge(sem["comb_ready"], 1)
                    dve.tensor_copy(combs[:], comb_sb[:, bass.ds(g * (GT * E), GT * E)]).then_inc(
                        sem["comb_staged"], 1)
                    dve.wait_ge(sem["comb_staged"], g + 1)

                def mult(e):
                    for c, (_, w) in enumerate(f.chunks):
                        j = e * nc_ + c
                        _, b = hidden_bank(f, j)
                        dve.wait_ge(sem["gate_silu_ready"], g * J + (own(f, k0 + j) + 1))
                        if positive(hidden_set_free(f, g, e)):
                            dve.wait_ge(sem["expert_summed"], hidden_set_free(f, g, e))
                        dve.tensor_tensor(hid_of[(e % f.sets) * nc_ + c][0:w, :], gate[j % 2][0:w, :], b[0:w, :],
                                          ALU.mult).then_inc(sem["hidden_gated_ready"], 1)

                def add(e):
                    n = g * f.ys + (Y0[L] + y[0])
                    yb = bank(4 + y[0] % 2)
                    dve.wait_ge(sem["expert_summed"], n + 1)
                    if positive(n):
                        dve.wait_ge(sem["expert_added"], n)
                    for u in range(GT):
                        a, yy = acc[:, u * P:(u + 1) * P], yb[:, u * P:(u + 1) * P]
                        w = combs[:, u * E + e:u * E + e + 1] if e < E and L != 1 else 1.0
                        if y[0] == 0:
                            i = dve.tensor_scalar(a, yy, w, None, ALU.mult)
                        else:
                            i = dve.scalar_tensor_tensor(a, yy, w, a, ALU.mult, ALU.add)
                    i.then_inc(sem["expert_added"], 1)
                    y[0] += 1

                for e in range(f.experts):
                    if f.gated:
                        mult(e)
                    if e:
                        add(e - 1)
                add(f.experts - 1)
                dve.wait_ge(sem["expert_added"], (g + 1) * f.ys + Y0[L])
                xs = x_tiles(g * GT, GT)
                dve.scalar_tensor_tensor(xs, acc, gain_sb[:, 4 + L:5 + L], xs, ALU.mult, ALU.add).then_inc(
                    sem["shared_added" if L == 1 else "x_updated"], 1)
                if L != 1:
                    ln_dve(dve, ln_number_ffn(L, g), g * GT, GT)

            groups(dve, body)
            if L == 2:
                distances(dve)

        def ffn_pool(pool, f):
            L = f.layer

            def body(g):
                if L != 3:
                    ln_pool(pool, ln_number_ffn(L, g), g * GT, GT)

            if L != 3:
                groups(pool, body)

        def setup_act(act):
            act.wait_ge(sem["rows_loaded"], 16)
            act.activation(gain_sb[:], row("g"), ACT.Tanh).then_inc(sem["gains_ready"], 1)

        def setup_dve(dve):
            dve.memset(zeros_sb[:], 0.0).then_inc(sem["zeros_ready"], 1)
            dve.wait_ge(sem["gains_ready"], 1)
            for k, name in enumerate(("bu0", "bo1", "bo2")):
                i = dve.tensor_scalar(gbias_sb[:, k * D:(k + 1) * D], row(name), gain_sb[:, k:k + 1], None, ALU.mult)
            i.then_inc(sem["bias_ready"], 1)

        def setup_lens(dve):
            dve.wait_ge(sem["mask2_loaded"], 32)
            dve.tensor_reduce(lens_sb[:], xn_sb[:, 0:NT * S].bitcast(I32).rearrange("p (n t) -> p n t", t=S), AX.X,
                              ALU.add).then_inc(sem["setup_steps"], 1)
            dve.wait_ge(sem["setup_steps"], 1)
            dve.tensor_scalar(lens_sb[:], lens_sb[:], -1.0, float(S - 1), ALU.mult, ALU.add).then_inc(
                sem["setup_steps"], 1)
            dve.wait_ge(sem["setup_steps"], 2)
            dve.reciprocal(rlens_sb[:], lens_sb[:]).then_inc(sem["lens_ready"], 1)

        ATT_PE = {1: a13_pe(1), 2: a2_pe, 3: a13_pe(3)}
        ATT_ACT = {1: a13_act(1), 2: a2_act, 3: a13_act(3)}
        ATT_DVE = {1: a13_dve(1), 2: a2_dve, 3: a13_dve(3)}
        ATT_POOL = {1: a13_pool(1), 2: a2_pool, 3: a13_pool(3)}
        block = stack.enter_context(nc.Block())

        @block.sync
        def _(sp):
            for dst, src, name in ((x_sb[:, 0:GW], x_in[:, 0:GW], "x_start_loaded"),
                                   (const_sb, consts_in, "consts_loaded"),
                                   (x_sb[:, GW:], x_in[:, GW:], "x_loaded"),
                                   (slab1[:, 0:NWA0], wa0, "wa0_loaded"), (ctx_sb, ctx_t, "ctx_loaded"),
                                   (cols_sb, cols_in, "cols_loaded"), (slab0[:, WF0["rw1"][0]:WF0["rw2"][1]], ws0, "w0_loaded"),
                                   (wsa_sb, wsa, "wsa_loaded")):
                sp.dma_start(dst[:], src).then_inc(sem[name], 16)
            mask2b = mask2.rearrange("(n b) t -> b n t", b=2)
            for b, r in enumerate(halves()):
                sp.dma_start(xn_sb[r, 0:NT * S].bitcast(I32).rearrange("p (n t) -> p n t", t=S),
                             mask2b[b].unsqueeze(0).broadcast_to([64, NT, S])).then_inc(sem["mask2_loaded"], 16)
            sp.dma_start(qpos_sb[:], qpos).then_inc(sem["qpos_loaded"], 16)
            sp.wait_ge(sem["zeros_ready"], 1)
            sp.dma_start(slots_x[0:NB * BW, :].rearrange("(n p) d -> p n d", p=P),
                         zeros_sb[:].unsqueeze(1).broadcast_to([P, NB * BT, D])).then_inc(sem["slots_zeroed"], 16)
            if stop_after > 1:
                blocks_sync(sp, 0)
            if stop_after > 2:
                sp.wait_ge(sem["xt_group_ready"], 2 * NT)
                sp.dma_start(slab1[:, NWF1 - NWS1:NWF1], ws1).then_inc(sem["w1_loaded"], 16)
            if stop_after > 3:
                blocks_sync(sp, 1)
            if stop_after > 3:
                sp.wait_ge(sem["xt_group_ready"], 3 * NT)
                sp.dma_start(slab0[:, 0:NWF2], wf2).then_inc(sem["w2_loaded"], 16)
            if stop_after > 5:
                sp.wait_ge(sem["xt_tile_ready"], 3 * NT)
                kposb = kpos.rearrange("(n b) t -> b n t", b=2)
                for b, r in enumerate(halves()):
                    sp.dma_start(xn_sb[r, 0:NT * S].bitcast(I32).rearrange("p (n t) -> p n t", t=S),
                                 kposb[b].unsqueeze(0).broadcast_to([64, NT, S])).then_inc(sem["kpos_loaded"], 16)
                sp.dma_start(xn_sb[:, NT * S:].bitcast(I32), maskq).then_inc(sem["maskq_loaded"], 16)
                sp.dma_start(view(slab1, WF3, "router"), router3).then_inc(sem["w3_loaded"], 16)
            if stop_after == 8:
                blocks_sync(sp, 3)
            base = updates(ln_number_ffn(3, 0)) if stop_after == 8 else None
            if base:
                with sp.Fori(0, NG) as g:
                    sp.wait_ge(sem["x_updated"], g + base)
                    sp.dma_start(out[:, bass.ds(g * GW, GW)], x_sb[:, bass.ds(g * GW, GW)]).then_inc(
                        sem["stored"], 16)
                sp.wait_ge(sem["stored"], 16 * NG)
            else:
                n = updates(ln_number_attn(stop_after // 2, NT - 1) if stop_after % 2 else
                            ln_number_ffn(stop_after // 2 - 1, NG - 1)) if stop_after else 0
                sp.wait_ge(sem["x_updated"], n)
                sp.dma_start(out, x_sb[:]).then_inc(sem["stored"], 16)
                sp.wait_ge(sem["stored"], 16)

        @block.tensor
        def _(pe):
            pe.wait_ge(sem["consts_loaded"], 16)

            def first(g):
                if positive(g * GT):
                    pe.wait_ge(sem["xt_group_ready"], g * GT)
                ln_pe(pe, g, bank(7), GT)
            groups(pe, first)
            pe.wait_ge(sem["xt_group_ready"], NT)
            if stop_after > 0:
                a0_pe(pe)
            for f in FFNS:
                if f.layer:
                    if stop_after > 2 * f.layer:
                        ATT_PE[f.layer](pe)
                if stop_after > 2 * f.layer + 1:
                    route_pe(pe, f)
                    if f.layer in (1, 2):
                        ffn_pe(pe, f)
                    if f.layer in NTH:
                        blocks_pe(pe, f.layer)

        @block.scalar
        def _(act):
            act.dma_start(rows_sb[:], rows_in.broadcast_to([P, NROWS])).then_inc(sem["rows_loaded"], 16)
            setup_act(act)
            groups(act, lambda g: ln_act(act, g, bank(7), g * GT, GT))
            act.wait_ge(sem["cols_loaded"], 16)
            if stop_after > 0:
                a0_act(act)
            for f in FFNS:
                if f.layer:
                    if stop_after > 2 * f.layer:
                        ATT_ACT[f.layer](act)
                if stop_after > 2 * f.layer + 1:
                    route_act(act, f)
                    if f.layer in (1, 2):
                        ffn_act(act, f)
                    if f.layer in NTH:
                        blocks_act(act, f.layer)

        @block.vector
        def _(dve):
            setup_dve(dve)

            def first_rows(g):
                ln_dve(dve, g, g * GT, GT, True, own=True)
                ln_all_dve(dve, g, g, g * GT, GT)
            groups(dve, first_rows)
            dve.wait_ge(sem["cols_loaded"], 16)
            dve.wait_ge(sem["consts_loaded"], 16)
            if stop_after > 0:
                setup_lens(dve)
                a0_dve(dve)
            for f in FFNS:
                if f.layer:
                    if stop_after > 2 * f.layer:
                        ATT_DVE[f.layer](dve)
                if stop_after > 2 * f.layer + 1:
                    route_dve(dve, f)
                    if f.layer == 1:
                        scale_rows(dve)
                    if f.layer in (1, 2):
                        ffn_dve(dve, f)
                    if f.layer in NTH:
                        blocks_dve(dve, f.layer)

        @block.gpsimd
        def _(pool):
            groups(pool, lambda g: pass_on(pool, g))
            pool.wait_ge(sem["bias_ready"], 1)
            pool.wait_ge(sem["ctx_loaded"], 16)
            if stop_after > 0:
                a0_pool(pool)
            for f in FFNS:
                if f.layer:
                    if stop_after > 2 * f.layer:
                        ATT_POOL[f.layer](pool)
                if stop_after > 2 * f.layer + 1:
                    if f.layer in NTH:
                        blocks_pool(pool, f.layer)
                    else:
                        ffn_pool(pool, f)


def arrays_of(inputs):
    f = {k: np.asarray(v) for k, v in inputs.items()}

    def fill(table, width, **fields):
        a = np.zeros((P, width), np.float32)
        for name, v in fields.items():
            lo, hi = table[name]
            v = v.reshape(v.shape[0], -1)
            assert v.shape[1] == hi - lo, (name, v.shape, hi - lo)
            a[:v.shape[0], lo:hi] = v
        return a

    def tokens(a):
        return np.ascontiguousarray(a.reshape(NT, P, -1).transpose(1, 0, 2).reshape(P, -1))

    def chunks(a):
        return a.reshape(-1, P, a.shape[-1]).transpose(1, 0, 2)

    def experts(a):
        return a.transpose(1, 0, 2)

    def hidden(a):
        return a.reshape(a.shape[0], -1, P, a.shape[-1]).transpose(2, 0, 1, 3)

    def padded(a):
        z = np.zeros((a.shape[0], 3 * P, D), np.float32)
        z[:, :F1] = a
        return z

    i, j = np.arange(P)[:, None], np.arange(P)[None, :]
    consts = fill(CONST, NCONST, part=np.arange(P)[:, None], ident=(i == j), before=(i < j), ones=np.ones((P, P)),
                  iota8=np.tile(np.arange(E), (P, 1)), iota64=np.tile(np.arange(S), (P, 1)),
                  slopes=np.tile(np.float32(2.0 ** -0.5) ** np.arange(1, H + 1), (P, 1)),
                  headmask=(i % 32 // HD == np.arange(4)[None]),
                  refloc=np.tile((i % S + np.arange(-3, 2)[None]), (1, H)))
    rows = np.concatenate([f["L0_xattn_bv"], f["L0_xattn_bu"], f["L1_xattn_b_v"], f["L1_xattn_b_o"],
                           f["L2_xattn_bv"], f["L2_xattn_boff"], f["L2_xattn_bo"], f["g_xattn"], f["g_ffn"]])[None]
    cols = fill(COLS, NCOLS, bq0=f["L0_xattn_bq"].reshape(8, P).T, bk0=f["L0_xattn_bk"].reshape(8, P).T,
                bq1=f["L1_xattn_b_q"][:, None], bk1=f["L1_xattn_b_k"][:, None], bq2=f["L2_xattn_bq"][:, None],
                bk2=f["L2_xattn_bk"][:, None], rb1=f["L0_ffn_rb1"].reshape(4, P).T, rb2=f["L0_ffn_rb2"][:, None],
                gb3=f["L3_ffn_gate_b"][:, None])
    shared_g = f["L2_ffn_ws_gate"].reshape(2, P, D)
    shared_u = f["L2_ffn_ws_up"].reshape(2, P, D)
    shared_d = f["L2_ffn_ws_down"].reshape(D, 2, P).transpose(1, 0, 2)

    def swap(a):
        return a.transpose(0, 2, 1)

    def weight_rows(table, width, **fields):
        rows_of = np.zeros((E, P, width), np.float32)
        for name, a in fields.items():
            rows_of[:, :a.shape[1], table[name][0]:table[name][1]] = a.reshape(E, a.shape[1], -1)
        return rows_of.reshape(E * P, width)

    return {
        "x": tokens(f["x"].reshape(B * S, D)),
        "ctx_t": np.ascontiguousarray(f["ctx_1024"].reshape(B * S, D).T),
        "wa0": fill(WA0, NWA0, q=f["L0_xattn_Wq"], k=f["L0_xattn_Wk"], v=f["L0_xattn_Wv"], u=chunks(f["L0_xattn_Wu"])),
        "wsa": fill(WSA, NWSA, q1=f["L1_xattn_w_q"].T, k1=f["L1_xattn_w_k"].T, v1=f["L1_xattn_w_v"].T,
                    o1=f["L1_xattn_w_o"].T, q2=f["L2_xattn_Wq"].T, k2=f["L2_xattn_Wk"].T, v2=f["L2_xattn_Wv"].T,
                    off2=f["L2_xattn_Woff"].T, o2=f["L2_xattn_Wo"].T, q3=f["L3_xattn_W_q"].T,
                    k3=f["L3_xattn_W_k"].T, v3=f["L3_xattn_W_v"].T, o3=f["L3_xattn_W_o"].T),
        "ws0": fill(WS0, NWS0, rw1=f["L0_ffn_rw1"], rw2=chunks(f["L0_ffn_rw2"])),
        "ws1": fill(WS1, NWS1, router=f["L1_ffn_router_DE"], w1=f["L1_ffn_ws1_DF"], w3=f["L1_ffn_ws3_DF"],
                    w2=hidden(padded(f["L1_ffn_ws2_FD"][None]))),
        "wf2": fill(WF2, NWF2, router=f["L2_ffn_gate_w"].T,
                    w1=experts(swap(np.concatenate([f["L2_ffn_we_gate"], shared_g]))),
                    w3=experts(swap(np.concatenate([f["L2_ffn_we_up"], shared_u]))),
                    w2=experts(swap(np.concatenate([f["L2_ffn_we_down"], shared_d])))),
        "experts0": weight_rows(WX3, NWX3, w1=f["L0_ffn_ew1"], b1=f["L0_ffn_eb1"].reshape(E, 4, P).transpose(0, 2, 1),
                                w2=hidden(f["L0_ffn_ew2"]).transpose(1, 0, 2, 3), b2=f["L0_ffn_eb2"][:, None]),
        "experts1": weight_rows(WX1, NWX1, w1=f["L1_ffn_w1_eDF"], w3=f["L1_ffn_w3_eDF"],
                                w2=hidden(padded(f["L1_ffn_w2_eFD"])).transpose(1, 0, 2, 3)),
        "router3": np.ascontiguousarray(f["L3_ffn_gate_w"].T),
        "experts3": weight_rows(WX3, NWX3, w1=swap(f["L3_ffn_w1"]), b1=f["L3_ffn_b1"].reshape(E, 4, P).transpose(0, 2, 1),
                                w2=hidden(swap(f["L3_ffn_w2"])).transpose(1, 0, 2, 3), b2=f["L3_ffn_b2"][:, None]),
        "rows": rows, "cols": cols, "consts": consts,
        "mask2": f["mask_BxS2_if0"], "qpos": tokens(f["itok_BxS_8_8191"].reshape(B * S, 1)),
        "kpos": f["itok_BxS2_1_8191"], "maskq": tokens(f["mask_BxSxS2_if1"].reshape(B * S, S)),
    }


def kernel(**inputs):
    import concourse.bacc as bacc
    from concourse.bass_utils import run_bass_kernel_spmd

    nc = bacc.Bacc("TRN2", target_bir_lowering=False, num_devices=1)
    arrays = {f"in_{k}": np.ascontiguousarray(v) for k, v in arrays_of(inputs).items()}
    args = [nc.dram_tensor(k, v.shape, mybir.dt.from_np(v.dtype), kind="ExternalInput").ap() for k, v in arrays.items()]
    out = nc.dram_tensor("out", (P, NT * D), F32, kind="ExternalOutput").ap()
    flamingo(nc, *args, out)
    got = run_bass_kernel_spmd(nc, [arrays], core_ids=[0]).results[0]["out"]
    return np.ascontiguousarray(got.reshape(P, NT, D).transpose(1, 0, 2)).reshape(B, S, D)
```
